# Optimizing a Trainium2 kernel written in Bass

```python
import numpy as np
import jax
import jax.numpy as jnp

def _softmax(x, axis=-1):
    return jax.nn.softmax(x, axis=axis)

def _gelu(x):
    return jax.nn.gelu(x, approximate=True)

def _silu(x):
    return jax.nn.silu(x)

def _sigmoid(x):
    return jax.nn.sigmoid(x)

def _layernorm(x, axis=-1, eps=1e-05):
    m = jnp.mean(x, axis=axis, keepdims=True)
    v = jnp.var(x, axis=axis, keepdims=True)
    return (x - m) / jnp.sqrt(v + eps)

def _scatter_add(tgt, idx, src, axis=0):
    return tgt.at[idx].add(src)

def _segment_sum(src, seg, n):
    return jax.ops.segment_sum(src, seg, n)
kernel_name = 'mk_sandwich_d2_jaxref_r8_4b14be'

def setup_inputs(seed: int=0):
    np.random.seed(seed)
    _w = jnp.asarray

    def _L0_attn_setup():
        import jax, jax.numpy as jnp
        import numpy as np
        DIM = 128
        HEADS = 16
        DIM_HEAD = 64
        SEG = 64
        PM = 16
        THETA = 10000.0
        EPS = 1e-06

        def rmsnorm(x, w):
            var = jnp.mean(x * x, axis=-1, keepdims=True)
            return x * jax.lax.rsqrt(var + EPS) * w

        def rope(x):
            n, d = (x.shape[-2], x.shape[-1])
            inv_freq = 1.0 / THETA ** (jnp.arange(0, d, 2, dtype=jnp.float32) / d)
            freqs = jnp.arange(n, dtype=jnp.float32)[:, None] * inv_freq
            cos = jnp.repeat(jnp.cos(freqs), 2, axis=-1)
            sin = jnp.repeat(jnp.sin(freqs), 2, axis=-1)
            xp = x.reshape(*x.shape[:-1], d // 2, 2)
            x_rot = jnp.stack((-xp[..., 1], xp[..., 0]), axis=-1).reshape(x.shape)
            return x * cos + x_rot * sin
        key = jax.random.key(seed)
        ks = jax.random.split(key, 7)
        s = lambda fan_in: 1.0 / np.sqrt(fan_in)
        return {'seq': jax.random.normal(ks[0], (2, 1024, DIM), dtype=jnp.float32), 'norm_w': jnp.ones((DIM,), dtype=jnp.float32), 'w_qkv': jax.random.normal(ks[1], (DIM, 3 * HEADS * DIM_HEAD), dtype=jnp.float32) * s(DIM), 'pm_k': jax.random.normal(ks[2], (HEADS, PM, DIM_HEAD), dtype=jnp.float32) * 0.02, 'pm_v': jax.random.normal(ks[3], (HEADS, PM, DIM_HEAD), dtype=jnp.float32) * 0.02, 'w_out': jax.random.normal(ks[4], (HEADS * DIM_HEAD, DIM), dtype=jnp.float32) * s(HEADS * DIM_HEAD), 'b_out': jax.random.normal(ks[5], (DIM,), dtype=jnp.float32) * 0.01}
    _L0_attn_in = _L0_attn_setup()

    def _L0_ffn_setup():
        import jax, jax.numpy as jnp
        import numpy as np
        D_MODEL = 128
        NUM_HEADS = 4
        NUM_EXPERTS = 8
        TOP_K = 2
        D_FF = 128
        EPS = 1e-06

        def _rmsnorm(x, g):
            return x * jax.lax.rsqrt(jnp.mean(x * x, axis=-1, keepdims=True) + EPS) * g

        def _swiglu(x, w1, w2, w3):
            return jax.nn.silu(x @ w1.T) * (x @ w3.T) @ w2.T
        key = jax.random.key(seed)
        ks = jax.random.split(key, 16)
        d, e, f = (D_MODEL, NUM_EXPERTS, D_FF)
        dc = d // 4
        s = 0.02
        return {'X': jax.random.normal(ks[0], (2, 128, d), dtype=jnp.float32), 'g1': jnp.ones((d,), jnp.float32), 'g2': jnp.ones((d,), jnp.float32), 'Wq': jax.random.normal(ks[1], (d, d), jnp.float32) * s, 'Wkc': jax.random.normal(ks[2], (dc, d), jnp.float32) * s, 'Wvc': jax.random.normal(ks[3], (dc, d), jnp.float32) * s, 'Wo': jax.random.normal(ks[4], (d, d), jnp.float32) * s, 'Wr': jax.random.normal(ks[5], (e, d), jnp.float32) * s, 'expert_bias': jnp.zeros((e,), jnp.float32), 'sW1': jax.random.normal(ks[6], (f, d), jnp.float32) * s, 'sW2': jax.random.normal(ks[7], (d, f), jnp.float32) * s, 'sW3': jax.random.normal(ks[8], (f, d), jnp.float32) * s, 'eW1': jax.random.normal(ks[9], (e, f, d), jnp.float32) * s, 'eW2': jax.random.normal(ks[10], (e, d, f), jnp.float32) * s, 'eW3': jax.random.normal(ks[11], (e, f, d), jnp.float32) * s}
    _L0_ffn_in = _L0_ffn_setup()

    def _L1_attn_setup():
        import jax, jax.numpy as jnp
        import numpy as np
        D = 128
        HS = 128
        NKV = 2

        def apply_rope(x):
            d = x.shape[-1]
            T = x.shape[-2]
            positions = jnp.arange(0, d, 2, dtype=jnp.float32)
            theta = 10000.0 ** (-2.0 * positions / d)
            angles = jnp.arange(T, dtype=jnp.float32)[:, None] * theta[None, :]
            cos, sin = (jnp.cos(angles), jnp.sin(angles))
            xr = x.reshape(x.shape[:-1] + (d // 2, 2))
            out = jnp.stack([xr[..., 0] * cos - xr[..., 1] * sin, xr[..., 1] * cos + xr[..., 0] * sin], axis=-1)
            return out.reshape(x.shape)
        key = jax.random.key(seed)
        k1, k2, k3, k4, k5 = jax.random.split(key, 5)
        B, T = (4, 256)
        x = jax.random.normal(k1, (B, T, D), dtype=jnp.float32)
        s = 1.0 / np.sqrt(D)
        Wq = jax.random.normal(k2, (NKV, HS, D), dtype=jnp.float32) * s
        Wk = jax.random.normal(k3, (HS, D), dtype=jnp.float32) * s
        Wv = jax.random.normal(k4, (HS, D), dtype=jnp.float32) * s
        Wo = jax.random.normal(k5, (D, NKV * HS), dtype=jnp.float32) * (1.0 / np.sqrt(NKV * HS))
        return {'x': x, 'Wq': Wq, 'Wk': Wk, 'Wv': Wv, 'Wo': Wo}
    _L1_attn_in = _L1_attn_setup()

    def _L1_ffn_setup():
        import jax, jax.numpy as jnp
        import numpy as np
        B, S, H, E, K = (2, 256, 128, 8, 2)
        FF = 4 * H
        EPS = 1e-05
        key = jax.random.key(seed)
        ks = jax.random.split(key, 5)
        rn = lambda k, shape, scale: jax.random.normal(k, shape, dtype=jnp.float32) * scale
        return {'x': rn(ks[0], (B, S, H), 1.0), 'router_W': rn(ks[1], (H, E), H ** (-0.5)), 'router_b': jnp.zeros((E,), jnp.float32), 'ln_g': jnp.ones((E, H), jnp.float32), 'ln_b': jnp.zeros((E, H), jnp.float32), 'W1': rn(ks[2], (E, H, FF), H ** (-0.5)), 'b1': jnp.zeros((E, FF), jnp.float32), 'W2': rn(ks[3], (E, FF, H), FF ** (-0.5)), 'b2': jnp.zeros((E, H), jnp.float32)}
    _L1_ffn_in = _L1_ffn_setup()
    _d = {'L0_attn_seq': _L0_attn_in['seq'], 'L0_attn_norm_w': _L0_attn_in['norm_w'], 'L0_attn_w_qkv': _L0_attn_in['w_qkv'], 'L0_attn_pm_k': _L0_attn_in['pm_k'], 'L0_attn_pm_v': _L0_attn_in['pm_v'], 'L0_attn_w_out': _L0_attn_in['w_out'], 'L0_attn_b_out': _L0_attn_in['b_out'], 'L0_ffn_g1': _L0_ffn_in['g1'], 'L0_ffn_g2': _L0_ffn_in['g2'], 'L0_ffn_Wq': _L0_ffn_in['Wq'], 'L0_ffn_Wkc': _L0_ffn_in['Wkc'], 'L0_ffn_Wvc': _L0_ffn_in['Wvc'], 'L0_ffn_Wo': _L0_ffn_in['Wo'], 'L0_ffn_Wr': _L0_ffn_in['Wr'], 'L0_ffn_expert_bias': _L0_ffn_in['expert_bias'], 'L0_ffn_sW1': _L0_ffn_in['sW1'], 'L0_ffn_sW2': _L0_ffn_in['sW2'], 'L0_ffn_sW3': _L0_ffn_in['sW3'], 'L0_ffn_eW1': _L0_ffn_in['eW1'], 'L0_ffn_eW2': _L0_ffn_in['eW2'], 'L0_ffn_eW3': _L0_ffn_in['eW3'], 'L1_attn_Wq': _L1_attn_in['Wq'], 'L1_attn_Wk': _L1_attn_in['Wk'], 'L1_attn_Wv': _L1_attn_in['Wv'], 'L1_attn_Wo': _L1_attn_in['Wo'], 'L1_ffn_router_W': _L1_ffn_in['router_W'], 'L1_ffn_router_b': _L1_ffn_in['router_b'], 'L1_ffn_ln_g': _L1_ffn_in['ln_g'], 'L1_ffn_ln_b': _L1_ffn_in['ln_b'], 'L1_ffn_W1': _L1_ffn_in['W1'], 'L1_ffn_b1': _L1_ffn_in['b1'], 'L1_ffn_W2': _L1_ffn_in['W2'], 'L1_ffn_b2': _L1_ffn_in['b2']}
    _x0 = _d['L0_attn_seq']
    _d['L0_attn_seq'] = jax.random.normal(jax.random.fold_in(jax.random.key(seed), 1), (2, 2048, 128), dtype=_x0.dtype)
    del _x0
    return _d

def reference(L0_attn_seq, L0_attn_norm_w, L0_attn_w_qkv, L0_attn_pm_k, L0_attn_pm_v, L0_attn_w_out, L0_attn_b_out, L0_ffn_g1, L0_ffn_g2, L0_ffn_Wq, L0_ffn_Wkc, L0_ffn_Wvc, L0_ffn_Wo, L0_ffn_Wr, L0_ffn_expert_bias, L0_ffn_sW1, L0_ffn_sW2, L0_ffn_sW3, L0_ffn_eW1, L0_ffn_eW2, L0_ffn_eW3, L1_attn_Wq, L1_attn_Wk, L1_attn_Wv, L1_attn_Wo, L1_ffn_router_W, L1_ffn_router_b, L1_ffn_ln_g, L1_ffn_ln_b, L1_ffn_W1, L1_ffn_b1, L1_ffn_W2, L1_ffn_b2):

    def _L0_attn_ref(seq, norm_w, w_qkv, pm_k, pm_v, w_out, b_out):
        import jax, jax.numpy as jnp
        import numpy as np
        DIM = 128
        HEADS = 16
        DIM_HEAD = 64
        SEG = 64
        PM = 16
        THETA = 10000.0
        EPS = 1e-06

        def rmsnorm(x, w):
            var = jnp.mean(x * x, axis=-1, keepdims=True)
            return x * jax.lax.rsqrt(var + EPS) * w

        def rope(x):
            n, d = (x.shape[-2], x.shape[-1])
            inv_freq = 1.0 / THETA ** (jnp.arange(0, d, 2, dtype=jnp.float32) / d)
            freqs = jnp.arange(n, dtype=jnp.float32)[:, None] * inv_freq
            cos = jnp.repeat(jnp.cos(freqs), 2, axis=-1)
            sin = jnp.repeat(jnp.sin(freqs), 2, axis=-1)
            xp = x.reshape(*x.shape[:-1], d // 2, 2)
            x_rot = jnp.stack((-xp[..., 1], xp[..., 0]), axis=-1).reshape(x.shape)
            return x * cos + x_rot * sin
        b, n_orig, _ = seq.shape
        n_pad = -n_orig % SEG
        x = jnp.pad(seq, ((0, 0), (0, n_pad), (0, 0))) if n_pad else seq
        n = x.shape[1]
        xn = rmsnorm(x, norm_w)
        qkv = xn @ w_qkv
        q, k, v = jnp.split(qkv, 3, axis=-1)
        split = lambda t: t.reshape(b, n, HEADS, DIM_HEAD).transpose(0, 2, 1, 3)
        q, k, v = (split(q), split(k), split(v))
        q, k = (rope(q), rope(k))
        w = n // SEG
        seg = lambda t: t.reshape(b, HEADS, w, SEG, DIM_HEAD).transpose(0, 2, 1, 3, 4).reshape(b * w, HEADS, SEG, DIM_HEAD)
        q_s, k_s, v_s = (seg(q), seg(k), seg(v))
        pmk = jnp.broadcast_to(pm_k[None], (b * w, HEADS, PM, DIM_HEAD))
        pmv = jnp.broadcast_to(pm_v[None], (b * w, HEADS, PM, DIM_HEAD))
        k_s = jnp.concatenate((pmk, k_s), axis=-2)
        v_s = jnp.concatenate((pmv, v_s), axis=-2)
        scale = DIM_HEAD ** (-0.5)
        scores = jnp.einsum('bhid,bhjd->bhij', q_s, k_s) * scale
        rows = jnp.arange(SEG)[:, None]
        cols = jnp.arange(PM + SEG)[None, :]
        allowed = (cols < PM) | (cols - PM <= rows)
        scores = jnp.where(allowed, scores, jnp.finfo(scores.dtype).min)
        attn = jax.nn.softmax(scores, axis=-1)
        out = jnp.einsum('bhij,bhjd->bhid', attn, v_s)
        out = out.transpose(0, 2, 1, 3).reshape(b * w, SEG, HEADS * DIM_HEAD)
        out = out @ w_out + b_out
        out = out.reshape(b, n, DIM)[:, :n_orig]
        return out

    def _L0_ffn_ref(X, g1, g2, Wq, Wkc, Wvc, Wo, Wr, expert_bias, sW1, sW2, sW3, eW1, eW2, eW3):
        import jax, jax.numpy as jnp
        import numpy as np
        D_MODEL = 128
        NUM_HEADS = 4
        NUM_EXPERTS = 8
        TOP_K = 2
        D_FF = 128
        EPS = 1e-06

        def _rmsnorm(x, g):
            return x * jax.lax.rsqrt(jnp.mean(x * x, axis=-1, keepdims=True) + EPS) * g

        def _swiglu(x, w1, w2, w3):
            return jax.nn.silu(x @ w1.T) * (x @ w3.T) @ w2.T
        B, S, d = X.shape
        H = NUM_HEADS
        dk = d // H
        scale = 1.0 / jnp.sqrt(jnp.float32(dk))
        nx = _rmsnorm(X, g1)
        Q = (nx @ Wq.T).reshape(B, S, H, dk).transpose(0, 2, 1, 3)
        Kc = nx @ Wkc.T
        Vc = nx @ Wvc.T
        scores = jnp.einsum('bhsd,btd->bhst', Q, Kc) * scale
        attn = jax.nn.softmax(scores, axis=-1)
        out = jnp.einsum('bhst,btd->bhsd', attn, Vc)
        out = out.transpose(0, 2, 1, 3).reshape(B, S, d) @ Wo.T
        X = X + out
        nx = _rmsnorm(X, g2)
        xf = nx.reshape(-1, d)
        logits = xf @ Wr.T + expert_bias
        rw = jax.nn.softmax(logits, axis=-1)
        topw, topi = jax.lax.top_k(rw, TOP_K)
        topw = jax.nn.softmax(topw, axis=-1)
        combine = jnp.sum(jax.nn.one_hot(topi, NUM_EXPERTS, dtype=xf.dtype) * topw[..., None], axis=1)
        shared = _swiglu(xf, sW1, sW2, sW3)
        h = jax.nn.silu(jnp.einsum('td,efd->etf', xf, eW1)) * jnp.einsum('td,efd->etf', xf, eW3)
        eo = jnp.einsum('etf,edf->etd', h, eW2)
        specialist = jnp.einsum('te,etd->td', combine, eo)
        moe_out = (shared + specialist).reshape(B, S, d)
        return X + moe_out

    def _L1_attn_ref(x, Wq, Wk, Wv, Wo):
        import jax, jax.numpy as jnp
        import numpy as np
        D = 128
        HS = 128
        NKV = 2

        def apply_rope(x):
            d = x.shape[-1]
            T = x.shape[-2]
            positions = jnp.arange(0, d, 2, dtype=jnp.float32)
            theta = 10000.0 ** (-2.0 * positions / d)
            angles = jnp.arange(T, dtype=jnp.float32)[:, None] * theta[None, :]
            cos, sin = (jnp.cos(angles), jnp.sin(angles))
            xr = x.reshape(x.shape[:-1] + (d // 2, 2))
            out = jnp.stack([xr[..., 0] * cos - xr[..., 1] * sin, xr[..., 1] * cos + xr[..., 0] * sin], axis=-1)
            return out.reshape(x.shape)
        B, T, _ = x.shape
        k = apply_rope(x @ Wk.T)
        v = x @ Wv.T
        q = jnp.einsum('btd,hkd->bhtk', x, Wq)
        q = apply_rope(q)
        scale = HS ** (-0.5)
        scores = jnp.einsum('bhtk,bsk->bhts', q, k) * scale
        causal = jnp.tril(jnp.ones((T, T), dtype=bool))
        scores = jnp.where(causal, scores, -jnp.inf)
        w = jax.nn.softmax(scores, axis=-1)
        out = jnp.einsum('bhts,bsk->bhtk', w, v)
        out = out.transpose(0, 2, 1, 3).reshape(B, T, NKV * HS)
        return out @ Wo.T

    def _L1_ffn_ref(x, router_W, router_b, ln_g, ln_b, W1, b1, W2, b2):
        import jax, jax.numpy as jnp
        import numpy as np
        B, S, H, E, K = (2, 256, 128, 8, 2)
        FF = 4 * H
        EPS = 1e-05
        logits = x @ router_W + router_b
        w, idx = jax.lax.top_k(logits, K)
        w = jax.nn.softmax(w, axis=-1)
        gates = jnp.einsum('bske,bsk->bse', jax.nn.one_hot(idx, E, dtype=x.dtype), w)
        mu = jnp.mean(x, axis=-1, keepdims=True)
        var = jnp.mean(jnp.square(x - mu), axis=-1, keepdims=True)
        xhat = (x - mu) * jax.lax.rsqrt(var + EPS)
        h = xhat[:, :, None, :] * ln_g + ln_b
        a = jax.nn.gelu(jnp.einsum('bseh,ehf->bsef', h, W1) + b1, approximate=False)
        y = jnp.einsum('bsef,efh->bseh', a, W2) + b2
        y = y + x[:, :, None, :]
        out = jnp.einsum('bseh,bse->bsh', y, gates)
        return out
    x = L0_attn_seq
    x = x + _layernorm(_L0_attn_ref(_layernorm(x, axis=-1), L0_attn_norm_w, L0_attn_w_qkv, L0_attn_pm_k, L0_attn_pm_v, L0_attn_w_out, L0_attn_b_out), axis=-1)
    x = x + _layernorm(_L0_ffn_ref(_layernorm(x, axis=-1), L0_ffn_g1, L0_ffn_g2, L0_ffn_Wq, L0_ffn_Wkc, L0_ffn_Wvc, L0_ffn_Wo, L0_ffn_Wr, L0_ffn_expert_bias, L0_ffn_sW1, L0_ffn_sW2, L0_ffn_sW3, L0_ffn_eW1, L0_ffn_eW2, L0_ffn_eW3), axis=-1)
    x = x + _layernorm(_L1_attn_ref(_layernorm(x, axis=-1), L1_attn_Wq, L1_attn_Wk, L1_attn_Wv, L1_attn_Wo), axis=-1)
    x = x + _layernorm(_L1_ffn_ref(_layernorm(x, axis=-1), L1_ffn_router_W, L1_ffn_router_b, L1_ffn_ln_g, L1_ffn_ln_b, L1_ffn_W1, L1_ffn_b1, L1_ffn_W2, L1_ffn_b2), axis=-1)
    return x

_drawn_inputs = setup_inputs


def setup_inputs(seed=0):
    import zlib

    import numpy as np

    out = dict(_drawn_inputs(seed))
    spreads = {'L0_attn_norm_w': (1.0, 0.2),
     'L0_ffn_g1': (1.0, 0.6),
     'L0_ffn_g2': (1.0, 0.6),
     'L0_ffn_expert_bias': (0.0, 0.8),
     'L1_ffn_router_b': (0.0, 0.1),
     'L1_ffn_ln_g': (1.0, 0.6),
     'L1_ffn_ln_b': (0.0, 0.628),
     'L1_ffn_b1': (0.0, 0.611),
     'L1_ffn_b2': (0.0, 0.417)}
    factors = {'L0_attn_pm_k': 8.0,
     'L0_attn_pm_v': 2.848,
     'L0_ffn_Wq': 8.0,
     'L0_ffn_Wkc': 8.0,
     'L0_ffn_Wvc': 7.25,
     'L0_ffn_Wo': 6.862,
     'L0_ffn_Wr': 8.0,
     'L0_ffn_sW1': 8.0,
     'L0_ffn_sW2': 8.0,
     'L0_ffn_sW3': 8.0,
     'L0_ffn_eW1': 8.0,
     'L0_ffn_eW2': 8.0,
     'L0_ffn_eW3': 8.0}
    for name, (base, spread) in spreads.items():
        noise = np.random.default_rng([zlib.crc32(name.encode()), seed]).standard_normal(out[name].shape)
        drawn = base * np.exp(spread * noise) if base else spread * noise
        out[name] = jnp.asarray(drawn.astype(out[name].dtype))
    for name, factor in factors.items():
        out[name] = (out[name] * factor).astype(out[name].dtype)
    return out
```

```python
import numpy as np
import concourse.bass as bass
import concourse.mybir as mybir
from contextlib import ExitStack

F32 = mybir.dt.float32
F32R = mybir.dt.float32r
BF16 = mybir.dt.bfloat16
U32 = mybir.dt.uint32
ALU = mybir.AluOpType
ACT = mybir.ActivationFunctionType
AXX = mybir.AxisListType.X

P = 128
D = 128
BATCH = 2
SEQ = 2048
TILES = BATCH * SEQ // P
BT = SEQ // P
BLK = 512
BPT = BLK // P
NBLK = BATCH * SEQ // BLK
BB = SEQ // BLK


class Mem:

    def __init__(self, nc, prefix):
        self.nc, self.prefix, self.ctx, self.sems = nc, "m" + prefix, ExitStack(), []

    def __enter__(self):
        self.ctx.__enter__()
        return self

    def __exit__(self, *a):
        if self.sems:
            self.nc.clear_and_free_semaphores(self.sems)
            self.nc.all_engine_barrier()
        return self.ctx.__exit__(*a)

    def sb(self, name, shape, dt=F32):
        return self.ctx.enter_context(self.nc.sbuf_tensor(self.prefix + name, shape, dt))

    def ps(self, name, banks=1, dt=F32, cols=512):
        shape = [P, cols] if banks == 1 else [P, banks, cols]
        return self.ctx.enter_context(self.nc.psum_tensor(self.prefix + name, shape, dt))

    def sem(self, name):
        s = self.nc.alloc_semaphore(self.prefix + name)
        self.sems.append(s)
        return s


def wait_alone(eng, sem, value, passed):
    eng.wait_ge(sem, value)
    eng.sem_inc(passed, 1)


def matmul_split(nc, out, lhs_hi, lhs_lo, rhs_hi, rhs_lo, start=True, stop=True):
    nc.tensor.matmul(out, lhs_hi, rhs_hi, start=start, stop=False)
    nc.tensor.matmul(out, lhs_lo, rhs_hi, start=False, stop=False)
    return nc.tensor.matmul(out, lhs_hi, rhs_lo, start=False, stop=stop)


H0 = 16
DH0 = 64
SEG = 64
PM = 16
PAIRS = H0 // 2
KEYS0 = PM + SEG
SCALE0 = DH0 ** -0.5
SBANKS = 3
PAIRS_OF_BANK = [(0, 1, 2), (3, 4, 5), (6, 7)]


def local_attention(nc, dr, X, g):
    m = Mem(nc, "a_")
    with m:
        NQK = 4 * 1024
        wh = m.sb("wh", [P, 5 * 1024], F32R)
        wl = m.sb("wl", [P, 5 * 1024], F32R)
        cosT = m.sb("cosT", [P, SEQ])
        sinT = m.sb("sinT", [P, SEQ])
        kt = m.sb("kt", [P, PAIRS, BLK // SEG, 2 * KEYS0])
        wout = m.sb("wout", [P, PAIRS, D])
        pmvw = m.sb("pmvw", [P, 2, D])
        bout = m.sb("bout", [P, D])
        mask = m.sb("mask", [P, 3 * 2 * KEYS0], BF16)
        mean = m.sb("mean", [P, TILES, 2])
        xsc = m.sb("xsc", [P, TILES])
        eps = m.sb("eps", [P, TILES])

        with Mem(nc, "a0_") as t:
            raw = t.sb("raw", [P, 3 * 1024])
            rot = t.sb("rot", [P, 2 * 1024])
            nw = t.sb("nw", [P, 1])
            pmvT = t.sb("pmvT", [P, PAIRS, P])
            bst = t.sb("bst", [P, TILES, 6])
            va = t.sb("va", [P, TILES])
            r1 = t.sb("r1", [P, TILES])
            r2 = t.sb("r2", [P, TILES])
            pp = t.ps("pp", 2, cols=512)
            x_in = t.sem("x_in")
            w_in = t.sem("w_in")
            c_in = t.sem("c_in")
            scaled = t.sem("scaled")
            rotated = t.sem("rotated")
            hi_done = t.sem("hi_done")
            lo_done = t.sem("lo_done")
            stat = t.sem("stat")
            powed = t.sem("powed")
            pm_mm = t.sem("pm_mm")
            pm_cp = t.sem("pm_cp")
            with nc.Block() as block:
                @block.sync
                def _(sp):
                    sp.dma_start(raw[:, :], dr["w_qkv"]).then_inc(w_in, 16)
                    sp.dma_start(nw[:, :], dr["norm_w"]).then_inc(w_in, 16)
                    sp.dma_start(X[:, :, :], dr["x"].rearrange("(t p) d -> p t d", p=P)).then_inc(x_in, 16)
                    for dst, src in ((g["ident"][:, :], "ident"), (g["identb"][:, :], "identb"), (mask[:, :], "mask0"),
                                     (cosT[:, :], "cos0"), (sinT[:, :], "sin0"), (pmvT[:, :, :], "pmvT"),
                                     (bout[:, :], "b_out"), (wout[:, :, :], "w_out")):
                        sp.dma_start(dst, dr[src]).then_inc(c_in, 16)
                    for s in range(BLK // SEG):
                        sp.dma_start(kt[:, :, s, :], dr["pmkT"]).then_inc(c_in, 16)
                    sp.wait_ge(c_in, 16 * (8 + BLK // SEG))

                @block.vector
                def _(dve):
                    nc.vector.memset(eps[:, :], -0.5).then_inc(stat, 1)
                    dve.wait_ge(w_in, 32)
                    nc.vector.tensor_scalar(raw[:, :], raw[:, :], nw[:, 0:1], None, ALU.mult).then_inc(scaled, 1)
                    dve.wait_ge(scaled, 1)
                    pair = raw[:, 0:2048].rearrange("p (n two) -> p n two", two=2)
                    rpair = rot[:, :].rearrange("p (n two) -> p n two", two=2)
                    nc.vector.tensor_scalar(rpair[:, :, 0], pair[:, :, 1], -1.0, None, ALU.mult).then_inc(rotated, 1)
                    nc.vector.tensor_copy(rpair[:, :, 1], pair[:, :, 0]).then_inc(rotated, 1)
                    dve.wait_ge(x_in, 16)
                    for i in range(TILES):
                        nc.vector.bn_stats(bst[:, i, :], X[:, i, :]).then_inc(stat, 1)
                    dve.wait_ge(stat, 1 + TILES)
                    for i in range(TILES):
                        nc.vector.bn_aggr(mean[:, i, :], bst[:, i, :]).then_inc(stat, 1)
                    dve.wait_ge(stat, 1 + 2 * TILES)
                    nc.vector.tensor_scalar(va[:, :], mean[:, :, 1], 1e-5, None, ALU.add).then_inc(stat, 1)
                    srcs = [(raw, 0), (rot, 0), (raw, 1024), (rot, 1024), (raw, 2048)]
                    for k, (src, o) in enumerate(srcs):
                        dve.wait_ge(hi_done, k + 1)
                        nc.vector.tensor_tensor(wl[:, k * 1024:(k + 1) * 1024], src[:, o:o + 1024],
                                                wh[:, k * 1024:(k + 1) * 1024].bitcast(F32),
                                                ALU.subtract).then_inc(lo_done, 1)
                    dve.wait_ge(powed, 1)
                    nc.vector.tensor_tensor(r2[:, :], r1[:, :], r1[:, :], ALU.mult).then_inc(stat, 1)
                    dve.wait_ge(stat, 3 + 2 * TILES)
                    nc.vector.tensor_tensor(va[:, :], r2[:, :], mean[:, :, 1], ALU.mult).then_inc(stat, 1)
                    dve.wait_ge(stat, 4 + 2 * TILES)
                    nc.vector.tensor_scalar(r2[:, :], va[:, :], 1e-6, None, ALU.add).then_inc(stat, 1)
                    dve.wait_ge(powed, 2)
                    nc.vector.tensor_tensor(xsc[:, :], r1[:, :], va[:, :], ALU.mult).then_inc(stat, 1)
                    dve.wait_ge(pm_mm, 1)
                    nc.vector.tensor_copy(pmvw[:, :, :], pp[:, :, 0:D]).then_inc(pm_cp, 1)

                @block.gpsimd
                def _(pool):
                    pool.wait_ge(stat, 2 + 2 * TILES)
                    nc.gpsimd.tensor_tensor(r1[:, :], va[:, :], eps[:, :], ALU.pow).then_inc(powed, 1)
                    pool.wait_ge(stat, 5 + 2 * TILES)
                    nc.gpsimd.tensor_tensor(va[:, :], r2[:, :], eps[:, :], ALU.pow).then_inc(powed, 1)

                @block.scalar
                def _(act):
                    srcs = [(raw, 0, 0), (rot, 0, 2), (raw, 1024, 0), (rot, 1024, 0), (raw, 2048, 0)]
                    for k, (src, o, need) in enumerate(srcs):
                        if k == 0:
                            act.wait_ge(scaled, 1)
                        if need:
                            act.wait_ge(rotated, need)
                        nc.scalar.activation(wh[:, k * 1024:(k + 1) * 1024], src[:, o:o + 1024],
                                             ACT.Copy).then_inc(hi_done, 1)

                @block.tensor
                def _(pe):
                    pe.wait_ge(c_in, 16 * (8 + BLK // SEG))
                    for half in range(2):
                        for k in range(4):
                            last = nc.tensor.matmul(pp[:, half, 0:D], pmvT[:, 4 * half + k, :],
                                                    wout[:, 4 * half + k, :], start=(k == 0), stop=(k == 3))
                    last.then_inc(pm_mm, 1)

        xth = m.sb("xth", [P, BLK], F32R)
        xtl = m.sb("xtl", [P, BLK], F32R)
        t1 = m.sb("t1", [P, 2, BLK])
        xn = t1[:, 0, :].rearrange("p (s d) -> p s d", d=D)
        t2 = m.sb("t2", [P, 2, BLK])
        qt = m.sb("qt", [P, PAIRS, BLK])
        v = m.sb("v", [P, BPT, H0 * DH0])
        e = m.sb("e", [P, 2, H0, KEYS0])
        mx = m.sb("mx", [P, 2, H0])
        den = m.sb("den", [P, 2, H0])
        rden = m.sb("rden", [P, 2, H0])
        pb = m.sb("pb", [P, 2, H0, P])
        ppm = m.sb("ppm", [P, 2, H0 * PM])
        pt = m.sb("pt", [P, H0 + 2, P])
        ot = m.sb("ot", [P, PAIRS, P])
        y = m.sb("y", [P, 2, D])
        yst = m.sb("yst", [P, 2, 6])
        ymv = m.sb("ymv", [P, 2, 2])
        yve = m.sb("yve", [P, 2])
        yr = m.sb("yr", [P, 2])
        bank = m.ps("bank", 5)
        sbank = m.ps("sbank", SBANKS)

        zeroed = m.sem("zeroed")
        xn_ready = m.sem("xn_ready")
        xt_mm = m.sem("xt_mm")
        xth_ready = m.sem("xth_ready")
        xtl_ready = m.sem("xtl_ready")
        proj_mm = m.sem("proj_mm")
        rope_mul = m.sem("rope_mul")
        rope_add = m.sem("rope_add")
        k_high = m.sem("k_high")
        v_mm = m.sem("v_mm")
        v_copied = m.sem("v_copied")
        s_mm = m.sem("s_mm")
        s_max = m.sem("s_max")
        s_sub = m.sem("s_sub")
        exp_done = m.sem("exp_done")
        den_done = m.sem("den_done")
        rden_done = m.sem("rden_done")
        p_norm = m.sem("p_norm")
        p_norm_high = m.sem("p_norm_high")
        pt_mm = m.sem("pt_mm")
        pt_copied = m.sem("pt_copied")
        ot_mm = m.sem("ot_mm")
        ot_copied = m.sem("ot_copied")
        out_mm = m.sem("out_mm")
        y_read = m.sem("y_read")
        y_chain = m.sem("y_chain")
        y_pow = m.sem("y_pow")
        y_fin = m.sem("y_fin")

        NT = BPT

        with nc.Block() as block:
            @block.vector
            def _(dve):
                nc.vector.memset(pb[:, :, :, :], 0.0).then_inc(zeroed, 1)

                def body(j, par):
                    n = j * 2 + par
                    tile0 = par * BT + j * BPT
                    for s in range(NT):
                        nc.vector.tensor_scalar(xn[:, s, :], X[:, bass.ds(tile0 + s, 1), :],
                                                mean[:, bass.ds(tile0 + s, 1), 0], xsc[:, bass.ds(tile0 + s, 1)],
                                                ALU.subtract, ALU.mult).then_inc(xn_ready, 1)
                    dve.wait_ge(xth_ready, n + 1)
                    nc.vector.tensor_tensor(xtl[:, :], bank[:, 4, :], xth[:, :].bitcast(F32),
                                            ALU.subtract).then_inc(xtl_ready, 1)
                    for ct in range(2 * PAIRS):
                        k = ct % 2
                        dve.wait_ge(proj_mm, n * 16 + ct + 1)
                        if ct >= 2:
                            dve.wait_ge(rope_add, n * 16 + ct - 1)
                        nc.vector.tensor_tensor(t1[:, k, :], bank[:, 2 * k, :], cosT[:, bass.ds(j * BLK, BLK)],
                                                ALU.mult).then_inc(rope_mul, 1)
                        nc.vector.tensor_tensor(t2[:, k, :], bank[:, 2 * k + 1, :], sinT[:, bass.ds(j * BLK, BLK)],
                                                ALU.mult).then_inc(rope_mul, 1)
                        if ct >= PAIRS:
                            dve.wait_ge(rope_mul, n * 32 + 2 * ct + 2)
                            nc.vector.tensor_tensor(
                                kt[64:128, ct - PAIRS, :, KEYS0 + PM:2 * KEYS0],
                                t1[64:128, k, :].rearrange("p (a b) -> p a b", b=SEG),
                                t2[64:128, k, :].rearrange("p (a b) -> p a b", b=SEG), ALU.add).then_inc(k_high, 1)

                    def softmax_front(s):
                        w = s % 2
                        if s >= 2:
                            dve.wait_ge(p_norm, n * 8 + 2 * (s - 1))
                            dve.wait_ge(p_norm_high, n * 4 + s - 1)
                        for b3, prs in enumerate(PAIRS_OF_BANK):
                            h0, nh = 2 * prs[0], 2 * len(prs)
                            dve.wait_ge(s_mm, n * 12 + 3 * s + b3 + 1)
                            nc.vector.tensor_reduce(mx[:, w, h0:h0 + nh],
                                                    sbank[:, b3, 0:nh * KEYS0].rearrange("p (h k) -> p h k", k=KEYS0),
                                                    AXX, ALU.max).then_inc(s_max, 1)
                        for b3, prs in enumerate(PAIRS_OF_BANK):
                            h0, nh = 2 * prs[0], 2 * len(prs)
                            dve.wait_ge(s_max, n * 12 + 3 * s + b3 + 1)
                            nc.vector.tensor_tensor(e[:, w, h0:h0 + nh, :],
                                                    sbank[:, b3, 0:nh * KEYS0].rearrange("p (h k) -> p h k", k=KEYS0),
                                                    mx[:, w, h0:h0 + nh, None].to_broadcast([P, nh, KEYS0]),
                                                    ALU.subtract).then_inc(s_sub, 1)

                    def softmax_back(s):
                        w = s % 2
                        dve.wait_ge(exp_done, n * 4 + s + 1)
                        nc.vector.tensor_reduce(den[:, w, :], e[:, w, :, :], AXX, ALU.add).then_inc(den_done, 1)
                        dve.wait_ge(den_done, n * 4 + s + 1)
                        nc.vector.reciprocal(rden[:, w, :], den[:, w, :]).then_inc(rden_done, 1)
                        dve.wait_ge(rden_done, n * 4 + s + 1)
                        if s >= 2:
                            dve.wait_ge(pt_mm, n * 20 + 5 * (s - 1))
                        nc.vector.tensor_tensor(pb[64:128, w, :, SEG:2 * SEG], e[64:128, w, :, PM:KEYS0],
                                                rden[64:128, w, :, None].to_broadcast([64, H0, SEG]),
                                                ALU.mult).then_inc(p_norm_high, 1)

                    def out_read(s):
                        w = s % 2
                        dve.wait_ge(out_mm, n * 4 + s + 1)
                        nc.vector.tensor_tensor(y[:, w, :], bank[:, 4, 0:D], bout[:, :], ALU.add).then_inc(y_read, 1)
                        dve.wait_ge(y_read, n * 4 + s + 1)
                        nc.vector.bn_stats(yst[:, w, :], y[:, w, :]).then_inc(y_chain, 1)
                        wait_alone(dve, y_chain, n * 12 + 3 * s + 1, g["passed_dve"])
                        nc.vector.bn_aggr(ymv[:, w, :], yst[:, w, :]).then_inc(y_chain, 1)
                        dve.wait_ge(y_chain, n * 12 + 3 * s + 2)
                        nc.vector.tensor_scalar(yve[:, w:w + 1], ymv[:, w, 1:2], 1e-5, None, ALU.add).then_inc(y_chain, 1)

                    def finish(s):
                        w = s % 2
                        dve.wait_ge(y_pow, n * 4 + s + 1)
                        nc.vector.tensor_scalar(y[:, w, :], y[:, w, :], ymv[:, w, 0:1], yr[:, w:w + 1],
                                                ALU.subtract, ALU.mult).then_inc(y_fin, 1)
                        dve.wait_ge(y_fin, n * 8 + 2 * s + 1)
                        xs = X[:, bass.ds(tile0 + s, 1), :]
                        nc.vector.tensor_tensor(xs, xs, y[:, w, None, :], ALU.add).then_inc(y_fin, 1)

                    softmax_front(0)
                    softmax_back(0)
                    softmax_front(1)
                    softmax_back(1)
                    softmax_front(2)
                    softmax_back(2)
                    softmax_front(3)
                    out_read(0)
                    softmax_back(3)
                    out_read(1)
                    finish(0)
                    dve.wait_ge(y_fin, n * 8 + 2)
                    out_read(2)
                    finish(1)
                    dve.wait_ge(y_fin, n * 8 + 4)
                    out_read(3)
                    finish(2)
                    finish(3)
                    dve.wait_ge(y_fin, n * 8 + 8)

                with dve.Fori(0, BB) as j:
                    body(j, 0)
                    body(j, 1)

            @block.gpsimd
            def _(pool):
                pool.wait_ge(zeroed, 1)

                def body(j, par):
                    n = j * 2 + par
                    for ct in range(2 * PAIRS):
                        k = ct % 2
                        pool.wait_ge(rope_mul, n * 32 + 2 * ct + 2)
                        if ct < PAIRS:
                            nc.gpsimd.tensor_tensor(qt[:, ct, :], t1[:, k, :], t2[:, k, :], ALU.add).then_inc(rope_add, 1)
                        else:
                            nc.gpsimd.tensor_tensor(
                                kt[0:64, ct - PAIRS, :, PM:KEYS0],
                                t1[0:64, k, :].rearrange("p (a b) -> p a b", b=SEG),
                                t2[0:64, k, :].rearrange("p (a b) -> p a b", b=SEG), ALU.add).then_inc(rope_add, 1)

                    def normalise(s):
                        w = s % 2
                        pool.wait_ge(rden_done, n * 4 + s + 1)
                        if s >= 2:
                            pool.wait_ge(pt_mm, n * 20 + 5 * (s - 1))
                        nc.gpsimd.tensor_tensor(pb[0:64, w, :, 0:SEG], e[0:64, w, :, PM:KEYS0],
                                                rden[0:64, w, :, None].to_broadcast([64, H0, SEG]),
                                                ALU.mult).then_inc(p_norm, 1)
                        nc.gpsimd.tensor_tensor(ppm[:, w, :].rearrange("p (h k) -> p h k", k=PM), e[:, w, :, 0:PM],
                                                rden[:, w, :, None].to_broadcast([P, H0, PM]),
                                                ALU.mult).then_inc(p_norm, 1)

                    def power(s):
                        w = s % 2
                        pool.wait_ge(y_chain, n * 12 + 3 * s + 3)
                        nc.gpsimd.tensor_tensor(yr[:, w:w + 1], yve[:, w:w + 1], eps[:, 0:1], ALU.pow).then_inc(y_pow, 1)

                    normalise(0)
                    normalise(1)
                    normalise(2)
                    power(0)
                    normalise(3)
                    power(1)
                    power(2)
                    power(3)

                with pool.Fori(0, BB) as j:
                    body(j, 0)
                    body(j, 1)

            @block.scalar
            def _(act):
                def body(j, par):
                    n = j * 2 + par
                    act.wait_ge(xt_mm, n + 1)
                    nc.scalar.activation(xth[:, :], bank[:, 4, :], ACT.Copy).then_inc(xth_ready, 1)
                    for c in range(2 * NT):
                        act.wait_ge(v_mm, n * 8 + c + 1)
                        nc.scalar.activation(v[:, c // 2, (c % 2) * 512:(c % 2) * 512 + 512], bank[:, c % 4, :],
                                             ACT.Copy).then_inc(v_copied, 1)

                    def exps(s):
                        act.wait_ge(s_sub, n * 12 + 3 * s + 3)
                        nc.scalar.activation(e[:, s % 2, :, :], e[:, s % 2, :, :], ACT.Exp,
                                             scale=SCALE0).then_inc(exp_done, 1)

                    def pt_copy(s):
                        for q in range(5):
                            i = 5 * s + q
                            nh = 4 if q < 4 else 2
                            act.wait_ge(pt_mm, n * 20 + i + 1)
                            nc.scalar.activation(pt[:, 4 * q:4 * q + nh, :],
                                                 bank[:, i % 2, 0:nh * P].rearrange("p (a b) -> p a b", b=P),
                                                 ACT.Copy).then_inc(pt_copied, 1)

                    def ot_copy(s):
                        for q in range(2):
                            act.wait_ge(ot_mm, n * 8 + 2 * s + q + 1)
                            nc.scalar.activation(ot[:, 4 * q:4 * q + 4, :],
                                                 bank[:, 2 + q, :].rearrange("p (a b) -> p a b", b=P),
                                                 ACT.Copy).then_inc(ot_copied, 1)

                    exps(0)
                    exps(1)
                    exps(2)
                    pt_copy(0)
                    ot_copy(0)
                    exps(3)
                    for s in range(1, NT):
                        pt_copy(s)
                        ot_copy(s)

                with act.Fori(0, BB) as j:
                    body(j, 0)
                    body(j, 1)

            @block.tensor
            def _(pe):
                ident, identb = g["ident"], g["identb"]

                def body(j, par):
                    n = j * 2 + par
                    for s in range(NT):
                        pe.wait_ge(xn_ready, n * 4 + s + 1)
                        last = nc.tensor.transpose(bank[:, 4, s * P:(s + 1) * P], xn[:, s, :], ident[:, :])
                    last.then_inc(xt_mm, 1)
                    pe.wait_ge(xth_ready, n + 1)
                    pe.wait_ge(xtl_ready, n + 1)
                    for ct in range(2 * PAIRS):
                        k = ct % 2
                        if ct >= 2:
                            pe.wait_ge(rope_mul, n * 32 + 2 * ct - 2)
                        for r in range(2):
                            c = (ct // PAIRS) * 2048 + r * 1024 + (ct % PAIRS) * P
                            last = matmul_split(nc, bank[:, 2 * k + r, :], wh[:, c:c + P], wl[:, c:c + P],
                                                xth[:, :], xtl[:, :])
                        last.then_inc(proj_mm, 1)
                    for c in range(2 * NT):
                        if c == 0:
                            pe.wait_ge(rope_mul, n * 32 + 30)
                        if c == 2:
                            pe.wait_ge(rope_mul, n * 32 + 32)
                        if c >= 4:
                            pe.wait_ge(v_copied, n * 8 + c - 3)
                        ts = slice((c // 2) * P, (c // 2 + 1) * P)
                        vc = slice(4096 + (c % 2) * 512, 4096 + (c % 2) * 512 + 512)
                        matmul_split(nc, bank[:, c % 4, :], xth[:, ts], xtl[:, ts], wh[:, vc],
                                     wl[:, vc]).then_inc(v_mm, 1)

                    def scores(s):
                        if s == 0:
                            pe.wait_ge(rope_add, n * 16 + 16)
                            pe.wait_ge(k_high, n * 8 + 8)
                        for b3, prs in enumerate(PAIRS_OF_BANK):
                            if s > 0:
                                pe.wait_ge(s_sub, n * 12 + 3 * (s - 1) + b3 + 1)
                            wd = 2 * KEYS0 * len(prs)
                            for hf in range(2):
                                nc.tensor.matmul(sbank[64 * hf:64 * hf + 64, b3, 0:wd], identb[:, 64 * hf:64 * hf + 64],
                                                 mask[:, 0:wd], start=True, stop=False, skip_group_check=True)
                            for i, pr in enumerate(prs):
                                for hf in range(2):
                                    q0 = s * P + 64 * hf
                                    last = nc.tensor.matmul(
                                        sbank[64 * hf:64 * hf + 64, b3, i * 160:(i + 1) * 160],
                                        qt[:, pr, q0:q0 + 64], kt[:, pr, 2 * s + hf, :],
                                        start=False, stop=True, skip_group_check=True)
                            last.then_inc(s_mm, 1)

                    def transposes(s):
                        w = s % 2
                        pe.wait_ge(p_norm, n * 8 + 2 * s + 2)
                        pe.wait_ge(p_norm_high, n * 4 + s + 1)
                        for q in range(5):
                            i = 5 * s + q
                            if i < 2:
                                pe.wait_ge(v_copied, n * 8 + 8)
                            else:
                                pe.wait_ge(pt_copied, n * 20 + i - 1)
                            for a in range(4 if q < 4 else 2):
                                src = pb[:, w, 4 * q + a, :] if q < 4 else ppm[:, w, a * P:(a + 1) * P]
                                last = nc.tensor.transpose(bank[:, i % 2, a * P:(a + 1) * P], src, ident[:, :])
                            last.then_inc(pt_mm, 1)

                    def values(s):
                        for q in range(2):
                            pe.wait_ge(pt_copied, n * 20 + 5 * s + 2 * q + 2)
                            if s > 0:
                                pe.wait_ge(ot_copied, n * 8 + 2 * (s - 1) + q + 1)
                            for pr in range(4 * q, 4 * q + 4):
                                for hh in range(2):
                                    h = 2 * pr + hh
                                    last = nc.tensor.matmul(
                                        bank[64 * hh:64 * hh + 64, 2 + q, (pr % 4) * P:(pr % 4 + 1) * P],
                                        v[:, s, h * DH0:(h + 1) * DH0], pt[:, h, :], start=True, stop=True)
                            last.then_inc(ot_mm, 1)

                    def out_project(s):
                        if s > 0:
                            pe.wait_ge(y_read, n * 4 + s)
                        pe.wait_ge(pt_copied, n * 20 + 5 * s + 5)
                        for i in range(2):
                            nc.tensor.matmul(bank[:, 4, 0:D], pt[:, H0 + i, :], pmvw[:, i, :], start=(i == 0), stop=False)
                        for pr in range(PAIRS):
                            if pr % 4 == 0:
                                pe.wait_ge(ot_copied, n * 8 + 2 * s + pr // 4 + 1)
                            last = nc.tensor.matmul(bank[:, 4, 0:D], ot[:, pr, :], wout[:, pr, :], start=False,
                                                    stop=(pr == PAIRS - 1))
                        last.then_inc(out_mm, 1)

                    scores(0)
                    scores(1)
                    for s in range(NT):
                        if s + 2 < NT:
                            scores(s + 2)
                        transposes(s)
                        values(s)
                        out_project(s)

                with pe.Fori(0, BB) as j:
                    body(j, 0)
                    body(j, 1)


class Stats:

    def __init__(self, m, t, g):
        self.passed = g["passed_dve"]
        self.mean = m.sb("mean", [P, TILES, 2])
        self.r = m.sb("r", [P, TILES])
        self.r2 = m.sb("r2", [P, TILES])
        self.rr = m.sb("rr", [P, TILES])
        self.half = m.sb("half", [P, TILES])
        self.bst = t.sb("bst", [P, TILES, 6])
        self.va = t.sb("va", [P, TILES])
        self.vb = t.sb("vb", [P, TILES])
        self.vc = t.sb("vc", [P, TILES])
        self.step = t.sem("stat_step")
        self.powed = t.sem("stat_pow")


def stats_vector(nc, dve, X, S, eps2, mid=None):
    T = TILES
    nc.vector.memset(S.half[:, :], -0.5).then_inc(S.step, 1)
    for i in range(T):
        nc.vector.bn_stats(S.bst[:, i, :], X[:, i, :]).then_inc(S.step, 1)
    dve.wait_ge(S.step, 1 + T)
    for i in range(T):
        nc.vector.bn_aggr(S.mean[:, i, :], S.bst[:, i, :]).then_inc(S.step, 1)
    dve.wait_ge(S.step, 1 + 2 * T)
    nc.vector.tensor_scalar(S.va[:, :], S.mean[:, :, 1], 1e-5, None, ALU.add).then_inc(S.step, 1)
    if mid:
        mid()
    dve.wait_ge(S.powed, 1)
    nc.vector.tensor_tensor(S.vb[:, :], S.r[:, :], S.r[:, :], ALU.mult).then_inc(S.step, 1)
    dve.wait_ge(S.step, 3 + 2 * T)
    nc.vector.tensor_tensor(S.vc[:, :], S.vb[:, :], S.mean[:, :, 1], ALU.mult).then_inc(S.step, 1)
    dve.wait_ge(S.step, 4 + 2 * T)
    nc.vector.tensor_scalar(S.vb[:, :], S.vc[:, :], eps2, None, ALU.add).then_inc(S.step, 1)
    dve.wait_ge(S.powed, 2)
    nc.vector.tensor_tensor(S.rr[:, :], S.r[:, :], S.r2[:, :], ALU.mult).then_inc(S.step, 1)


def stats_pool(nc, pool, S):
    pool.wait_ge(S.step, 2 + 2 * TILES)
    nc.gpsimd.tensor_tensor(S.r[:, :], S.va[:, :], S.half[:, :], ALU.pow).then_inc(S.powed, 1)
    pool.wait_ge(S.step, 5 + 2 * TILES)
    nc.gpsimd.tensor_tensor(S.r2[:, :], S.vb[:, :], S.half[:, :], ALU.pow).then_inc(S.powed, 1)


HB = 4
DK = D // HB
QROWS = 3 * DK
SCALE_B = 1.0 / np.sqrt(np.float32(DK))
KT = SEQ // P
NCH = SEQ // BLK
NE = 8
UNITS = 2 * BB
P1 = 2 * BPT * NCH
RING = 3


def mqa_attention(nc, dr, X, g, S, wq, wkv, ao):
    m = Mem(nc, "b1_")
    with m:
        xn = m.sb("xn", [P, BPT, D])
        xh = m.sb("xh", [P, SEQ], F32R)
        xl = m.sb("xl", [P, SEQ], F32R)
        ks = m.sb("ks", [QROWS + 2, SEQ], F32R)
        qs = [m.sb(f"qs{w}", [QROWS + 2, 2, BLK], F32R) for w in range(2)]
        vt = m.sb("vt", [P, BLK])
        v1 = m.sb("v1", [P, KT, DK + 1])
        pt = m.sb("pt", [P, RING, 2, BLK])
        mxp = m.sb("mxp", [P, 2 * BPT, NCH])
        negm = m.sb("negm", [P, 2, BPT])
        mt = m.sb("mt", [P, BPT, 2 * DK])
        ots = m.sb("ots", [P, BLK])
        rd = m.sb("rd", [P, BPT, 2])
        p1b = m.ps("p1b", 2)
        stb = m.ps("stb", 4)
        pvb = m.ps("pvb")
        misc = m.ps("misc")

        zeroed = m.sem("zeroed")
        xn_ready = m.sem("xn_ready")
        xt_mm = m.sem("xt_mm")
        xh_ready = m.sem("xh_ready")
        xl_ready = m.sem("xl_ready")
        kv_mm = m.sem("kv_mm")
        k_hi = m.sem("k_hi")
        k_lo = m.sem("k_lo")
        vt_ready = m.sem("vt_ready")
        vt_mm = m.sem("vt_mm")
        v_ready = m.sem("v_ready")
        q_mm = m.sem("q_mm")
        q_hi = m.sem("q_hi")
        q_lo = m.sem("q_lo")
        p1_mm = m.sem("p1_mm")
        p1_max = m.sem("p1_max")
        m_neg = m.sem("m_neg")
        m_split = m.sem("m_split")
        mt_mm = m.sem("mt_mm")
        m_rows = m.sem("m_rows")
        st_mm = m.sem("st_mm")
        exp_done = m.sem("exp_done")
        pv_mm = m.sem("pv_mm")
        pv_evac = m.sem("pv_evac")
        post_mm = m.sem("post_mm")
        rd_done = m.sem("rd_done")
        post_done = m.sem("post_done")

        def schedule(unit, epilogue):
            def run(eng, b):
                unit(b, 0, 0, True, False)
                unit(b, 0, 1, False, False)
                with eng.Fori(1, BB - 1) as n:
                    unit(b, n, 0, False, False)
                    unit(b, n, 1, False, False)
                unit(b, BB - 1, 0, False, False)
                unit(b, BB - 1, 1, False, True)
                epilogue(b)
            return run

        with nc.Block() as block:
            @block.vector
            def _(dve):
                nc.vector.memset(ks[QROWS:QROWS + 2, :].bitcast(F32), 1.0).then_inc(zeroed, 1)
                nc.vector.memset(v1[:, :, DK:DK + 1], 1.0).then_inc(zeroed, 1)
                nc.vector.memset(mt[:, :, :], 0.0).then_inc(zeroed, 1)
                nc.vector.memset(ots[:, :], 0.0).then_inc(zeroed, 1)
                dve.wait_ge(zeroed, 4)

                def load(b, i):
                    n = b * BB + i
                    for s in range(BPT):
                        tile = bass.ds(n * BPT + s, 1)
                        nc.vector.tensor_scalar(xn[:, s, :], X[:, tile, :], S.mean[:, tile, 0], S.rr[:, tile],
                                                ALU.subtract, ALU.mult).then_inc(xn_ready, 1)
                    cols = bass.ds(i * BLK, BLK)
                    dve.wait_ge(xh_ready, n + 1)
                    nc.vector.tensor_tensor(xl[:, cols], p1b[:, 0, :], xh[:, cols].bitcast(F32),
                                            ALU.subtract).then_inc(xl_ready, 1)
                    dve.wait_ge(kv_mm, n + 1)
                    nc.vector.tensor_copy(vt[QROWS:P, :], p1b[QROWS:P, 1, :]).then_inc(vt_ready, 1)
                    dve.wait_ge(k_hi, n + 1)
                    nc.vector.tensor_tensor(ks[DK:2 * DK, cols], p1b[DK:2 * DK, 1, :], ks[DK:2 * DK, cols].bitcast(F32),
                                            ALU.subtract).then_inc(k_lo, 1)
                    dve.wait_ge(vt_mm, n + 1)
                    nc.vector.tensor_copy(v1[:, bass.ds(i * BPT, BPT), 0:DK],
                                          misc[:, 0:BPT * DK].rearrange("p (a b) -> p a b", b=DK)).then_inc(v_ready, 1)

                def q_low(V, w):
                    for hh in range(2):
                        src = misc[2 * DK:3 * DK, :] if hh == 0 else p1b[2 * DK:3 * DK, 0, :]
                        dst = qs[w][2 * DK:3 * DK, hh, :]
                        dve.wait_ge(q_hi, V * 2 + hh + 1)
                        nc.vector.tensor_tensor(dst, src, dst.bitcast(F32), ALU.subtract).then_inc(q_lo, 1)

                def maxima(V, w):
                    for r in range(P1):
                        dve.wait_ge(p1_mm, V * P1 + r + 1)
                        nc.vector.tensor_reduce(mxp[:, r // NCH, r % NCH:r % NCH + 1], p1b[:, r % 2, :], AXX,
                                                ALU.max).then_inc(p1_max, 1)
                    dve.wait_ge(p1_max, V * P1 + P1)
                    nc.vector.tensor_reduce(negm[:, :, :].rearrange("p h t -> p (h t)"), mxp[:, :, :], AXX, ALU.max,
                                            negate=True).then_inc(m_neg, 1)
                    dve.wait_ge(m_neg, V + 1)
                    nt = negm[:, :, :].rearrange("p h t -> p t h")
                    hi, lo = mt[:, :, 0:2 * DK:DK], mt[:, :, 1:2 * DK:DK]
                    nc.vector.tensor_copy(hi.bitcast(F32R), nt).then_inc(m_split, 1)
                    dve.wait_ge(m_split, V * 2 + 1)
                    nc.vector.tensor_tensor(lo.bitcast(F32R), nt, hi, ALU.subtract).then_inc(m_split, 1)
                    dve.wait_ge(mt_mm, V + 1)
                    for hh in range(2):
                        nc.vector.tensor_copy(qs[w][QROWS:QROWS + 2, hh, :], misc[DK * hh:DK * hh + 2, :]).then_inc(m_rows, 1)

                def evacuate(U):
                    dve.wait_ge(pv_mm, (U + 1) * KT)
                    for hh in range(2):
                        nc.vector.tensor_copy(ots[64 * hh:64 * hh + DK + 1, :], pvb[64 * hh:64 * hh + DK + 1, :])\
                            .then_inc(pv_evac, 1)

                def post(U, b, n, w):
                    dve.wait_ge(post_mm, U + 1)
                    o = misc[:, :].rearrange("p (t h c) -> p t h c", t=BPT, h=2)
                    nc.vector.reciprocal(rd[:, :, :], o[:, :, :, DK]).then_inc(rd_done, 1)
                    dve.wait_ge(rd_done, U + 1)
                    for t in range(BPT):
                        dst = ao[:, bass.ds(b * BT + n * BPT + t, 1), w * 64:w * 64 + 64]
                        nc.vector.tensor_tensor(dst.rearrange("p a (h c) -> p (a h) c", h=2), o[:, t, :, 0:DK],
                                                rd[:, t, :, None].to_broadcast([P, 2, DK]),
                                                ALU.mult).then_inc(post_done, 1)

                def unit(b, n, w, first, last):
                    U = b * UNITS + n * 2 + w
                    if not first:
                        post(U - 1, b, n - 1 + w, 1 - w)
                    if not last:
                        q_low(U + 1, 1 - w)
                        maxima(U + 1, 1 - w)
                    evacuate(U)

                def epilogue(b):
                    post(b * UNITS + UNITS - 1, b, BB - 1, 1)

                run = schedule(unit, epilogue)
                with dve.Fori(0, BATCH) as b:
                    with dve.Fori(0, BB) as i:
                        load(b, i)
                    q_low(b * UNITS, 0)
                    maxima(b * UNITS, 0)
                    run(dve, b)

            @block.scalar
            def _(act):
                def load(b, i):
                    n = b * BB + i
                    cols = bass.ds(i * BLK, BLK)
                    act.wait_ge(xt_mm, n + 1)
                    nc.scalar.activation(xh[:, cols], p1b[:, 0, :], ACT.Copy).then_inc(xh_ready, 1)
                    act.wait_ge(kv_mm, n + 1)
                    act.wait_ge(vt_ready, n + 1)
                    nc.scalar.activation(ks[0:QROWS, cols], p1b[0:QROWS, 1, :], ACT.Copy).then_inc(k_hi, 1)

                def q_high(V, w):
                    for hh in range(2):
                        src = misc[0:QROWS, :] if hh == 0 else p1b[0:QROWS, 0, :]
                        act.wait_ge(q_mm, V * 2 + hh + 1)
                        nc.scalar.activation(qs[w][0:QROWS, hh, :], src, ACT.Copy).then_inc(q_hi, 1)

                def unit(b, n, w, first, last):
                    U = b * UNITS + n * 2 + w
                    for i in range(KT):
                        act.wait_ge(st_mm, U * KT + i + 1)
                        if i >= RING:
                            act.wait_ge(pv_mm, U * KT + i - RING + 1)
                        nc.scalar.activation(pt[:, i % RING, :, :], stb[:, 2 * (i % 2):2 * (i % 2) + 2, :], ACT.Exp,
                                             scale=float(SCALE_B)).then_inc(exp_done, 1)
                        if i == 1 and not last:
                            q_high(U + 1, 1 - w)

                run = schedule(unit, lambda b: None)
                with act.Fori(0, BATCH) as b:
                    with act.Fori(0, BB) as i:
                        load(b, i)
                    q_high(b * UNITS, 0)
                    run(act, b)

            @block.tensor
            def _(pe):
                ident = g["ident"]
                pe.wait_ge(zeroed, 4)

                def load(b, i):
                    n = b * BB + i
                    for s in range(BPT):
                        pe.wait_ge(xn_ready, n * BPT + s + 1)
                        last = nc.tensor.transpose(p1b[:, 0, s * P:(s + 1) * P], xn[:, s, :], ident[:, :])
                    last.then_inc(xt_mm, 1)
                    cols = bass.ds(i * BLK, BLK)
                    pe.wait_ge(xh_ready, n + 1)
                    pe.wait_ge(xl_ready, n + 1)
                    matmul_split(nc, p1b[:, 1, :], wkv[0][:, :], wkv[1][:, :], xh[:, cols], xl[:, cols]).then_inc(kv_mm, 1)
                    pe.wait_ge(k_lo, n + 1)
                    wait_alone(pe, vt_ready, n + 1, g["passed_pe"])
                    for s in range(BPT):
                        last = nc.tensor.transpose(misc[:, s * DK:(s + 1) * DK], vt[QROWS:P, s * P:(s + 1) * P],
                                                   ident[QROWS:P, QROWS:P])
                    last.then_inc(vt_mm, 1)
                    pe.wait_ge(v_ready, n + 1)

                def project(V, n, w):
                    cols = bass.ds(n * BLK, BLK)
                    for hh in range(2):
                        h = 2 * w + hh
                        out = misc[0:QROWS, :] if hh == 0 else p1b[0:QROWS, 0, :]
                        matmul_split(nc, out, wq[0][:, h, :], wq[1][:, h, :], xh[:, cols], xl[:, cols]).then_inc(q_mm, 1)

                def first_pass(V, w, r):
                    if r == 0:
                        pe.wait_ge(q_lo, V * 2 + 2)
                    if r >= 2:
                        pe.wait_ge(p1_max, V * P1 + r - 1)
                    hh, t, c = r // (BPT * NCH), (r // NCH) % BPT, r % NCH
                    nc.tensor.matmul(p1b[:, r % 2, :], qs[w][0:QROWS, hh, t * P:(t + 1) * P],
                                     ks[0:QROWS, c * BLK:(c + 1) * BLK], start=True, stop=True).then_inc(p1_mm, 1)

                def max_rows(V):
                    wait_alone(pe, m_split, V * 2 + 2, g["passed_pe"])
                    for t in range(BPT):
                        last = nc.tensor.transpose(misc[0:2 * DK, t * P:(t + 1) * P], mt[:, t, :], ident[:, :])
                    last.then_inc(mt_mm, 1)

                def scores(U, w, i):
                    if i == 0:
                        pe.wait_ge(m_rows, U * 2 + 2)
                    if i >= 2:
                        pe.wait_ge(exp_done, U * KT + i - 1)
                    for hh in range(2):
                        last = nc.tensor.matmul(stb[:, 2 * (i % 2) + hh, :], ks[:, i * P:(i + 1) * P], qs[w][:, hh, :],
                                                start=True, stop=True)
                    last.then_inc(st_mm, 1)

                def values(U, i):
                    pe.wait_ge(exp_done, U * KT + i + 1)
                    for hh in range(2):
                        last = nc.tensor.matmul(pvb[64 * hh:64 * hh + DK + 1, :], v1[:, i, :], pt[:, i % RING, hh, :],
                                                start=(i == 0), stop=(i == KT - 1), skip_group_check=True)
                    last.then_inc(pv_mm, 1)

                def post(U):
                    pe.wait_ge(pv_evac, U * 2 + 2)
                    for t in range(BPT):
                        last = nc.tensor.transpose(misc[:, t * P:t * P + P], ots[:, t * P:(t + 1) * P], ident[:, :])
                    last.then_inc(post_mm, 1)

                def unit(b, n, w, first, last):
                    U = b * UNITS + n * 2 + w
                    scores(U, w, 0)
                    r = 0
                    for i in range(KT):
                        if i + 1 < KT:
                            scores(U, w, i + 1)
                        if i == 0 and not first:
                            post(U - 1)
                        if i == 1 and not last:
                            if not first:
                                pe.wait_ge(post_done, U * BPT)
                            project(U + 1, n + w, 1 - w)
                        if i >= 2 and not last:
                            for _ in range(3):
                                if r < P1:
                                    first_pass(U + 1, 1 - w, r)
                                    r += 1
                        if i == KT - 1 and not last:
                            max_rows(U + 1)
                        values(U, i)

                def epilogue(b):
                    post(b * UNITS + UNITS - 1)
                    pe.wait_ge(post_done, (b + 1) * UNITS * BPT)

                run = schedule(unit, epilogue)
                with pe.Fori(0, BATCH) as b:
                    with pe.Fori(0, BB) as i:
                        load(b, i)
                    project(b * UNITS, 0, 0)
                    for r in range(P1):
                        first_pass(b * UNITS, 0, r)
                    max_rows(b * UNITS)
                    run(pe, b)


def ffn_mixture(nc, dr, X, g, S, w, ao):
    m = Mem(nc, "b2_")
    with m:
        w1, w2, wr, wo, ebias = w["w13"], w["w2"], w["wr"], w["wo"], w["ebias"]
        x2 = m.sb("x2", [P, TILES, D])
        nh = m.sb("nh", [P, TILES * P], F32R)
        nl = m.sb("nl", [P, TILES * P], F32R)
        lg = m.sb("lg", [P, TILES, NE])
        gate = m.sb("gate", [P, TILES, NE])
        with Mem(nc, "b2a_") as t:
            aos = t.sb("aos", [P, BPT, D])
            aot = t.sb("aot", [P, BLK])
            h = t.sb("h", [P, BPT, D])
            sq = t.sb("sq", [P, BPT, D])
            ss = t.sb("ss", [P, BPT])
            sv = t.sb("sv", [P, BPT])
            r2 = t.sb("r2", [P, BPT])
            xn = t.sb("xn", [P, BPT, D])
            lt = t.sb("lt", [32, BLK])
            bk = t.ps("bk", 5)
            copied = t.sem("copied")
            at_mm = t.sem("at_mm")
            at_ready = t.sem("at_ready")
            o_mm = t.sem("o_mm")
            ln = t.sem("ln")
            x2_done = t.sem("x2_done")
            sq_done = t.sem("sq_done")
            powed = t.sem("powed")
            xn_done = t.sem("xn_done")
            xt_mm = t.sem("xt_mm")
            xh_done = t.sem("xh_done")
            xl_done = t.sem("xl_done")
            l_mm = t.sem("l_mm")
            l_copied = t.sem("l_copied")
            lt_mm = t.sem("lt_mm")
            l_done = t.sem("l_done")
            with nc.Block() as block:
                @block.scalar
                def _(act):
                    with act.Fori(0, NBLK) as n:
                        nc.scalar.activation(aos[:, :, :], ao[:, bass.ds(n * BPT, BPT), :], ACT.Copy).then_inc(copied, 1)
                        act.wait_ge(at_mm, n + 1)
                        nc.scalar.activation(aot[:, :], bk[:, 0, :], ACT.Copy).then_inc(at_ready, 1)
                        act.wait_ge(xt_mm, n + 1)
                        nc.scalar.activation(nh[:, bass.ds(n * BLK, BLK)], bk[:, 2, :], ACT.Copy).then_inc(xh_done, 1)
                        act.wait_ge(l_mm, n + 1)
                        nc.scalar.activation(lt[:, :], bk[0:32, 3, :], ACT.Copy).then_inc(l_copied, 1)

                @block.gpsimd
                def _(pool):
                    with pool.Fori(0, NBLK) as n:
                        pool.wait_ge(sq_done, n * 3 + 3)
                        nc.gpsimd.tensor_tensor(r2[:, :], sv[:, :], S.half[:, 0:BPT], ALU.pow).then_inc(powed, 1)

                @block.vector
                def _(dve):
                    with dve.Fori(0, NBLK) as n:
                        for s in range(BPT):
                            tile = bass.ds(n * BPT + s, 1)
                            nc.vector.tensor_scalar(h[:, s, :], X[:, tile, :], S.mean[:, tile, 0], S.r[:, tile],
                                                    ALU.subtract, ALU.mult).then_inc(ln, 1)
                        blk = bass.ds(n * BPT, BPT)
                        dve.wait_ge(o_mm, n + 1)
                        dve.wait_ge(ln, n * 4 + 4)
                        nc.vector.tensor_tensor(x2[:, blk, :], bk[:, 1, :].rearrange("p (a b) -> p a b", b=D),
                                                h[:, :, :], ALU.add).then_inc(x2_done, 1)
                        dve.wait_ge(x2_done, n + 1)
                        nc.vector.tensor_tensor(sq[:, :, :], x2[:, blk, :], x2[:, blk, :], ALU.mult).then_inc(sq_done, 1)
                        dve.wait_ge(sq_done, n * 3 + 1)
                        nc.vector.tensor_reduce(ss[:, :], sq[:, :, :], AXX, ALU.add).then_inc(sq_done, 1)
                        dve.wait_ge(sq_done, n * 3 + 2)
                        nc.vector.tensor_scalar(sv[:, :], ss[:, :], 1.0 / D, 1e-6, ALU.mult, ALU.add).then_inc(sq_done, 1)
                        dve.wait_ge(powed, n + 1)
                        nc.vector.tensor_tensor(xn[:, :, :], x2[:, blk, :], r2[:, :, None].to_broadcast([P, BPT, D]),
                                                ALU.mult).then_inc(xn_done, 1)
                        cols = bass.ds(n * BLK, BLK)
                        dve.wait_ge(xh_done, n + 1)
                        nc.vector.tensor_tensor(nl[:, cols], bk[:, 2, :], nh[:, cols].bitcast(F32),
                                                ALU.subtract).then_inc(xl_done, 1)
                        dve.wait_ge(lt_mm, n + 1)
                        nc.vector.tensor_tensor(lg[:, blk, :],
                                                bk[:, 4, 0:BPT * 32].rearrange("p (a b) -> p a b", b=32)[:, :, 0:NE],
                                                ebias[:, None, :].to_broadcast([P, BPT, NE]), ALU.add).then_inc(l_done, 1)

                @block.tensor
                def _(pe):
                    ident = g["ident"]
                    with pe.Fori(0, NBLK) as n:
                        pe.wait_ge(copied, n + 1)
                        for s in range(BPT):
                            last = nc.tensor.transpose(bk[:, 0, s * P:(s + 1) * P], aos[:, s, :], ident[:, :])
                        last.then_inc(at_mm, 1)
                        pe.wait_ge(at_ready, n + 1)
                        for s in range(BPT):
                            last = nc.tensor.matmul(bk[:, 1, s * P:(s + 1) * P], aot[:, s * P:(s + 1) * P], wo[:, :],
                                                    start=True, stop=True)
                        last.then_inc(o_mm, 1)
                        pe.wait_ge(xn_done, n + 1)
                        for s in range(BPT):
                            last = nc.tensor.transpose(bk[:, 2, s * P:(s + 1) * P], xn[:, s, :], ident[:, :])
                        last.then_inc(xt_mm, 1)
                        pe.wait_ge(xh_done, n + 1)
                        pe.wait_ge(xl_done, n + 1)
                        cols = bass.ds(n * BLK, BLK)
                        matmul_split(nc, bk[:, 3, :], wr[0][:, :], wr[1][:, :], nh[:, cols], nl[:, cols]).then_inc(l_mm, 1)
                        wait_alone(pe, l_copied, n + 1, g["passed_pe"])
                        for s in range(BPT):
                            last = nc.tensor.transpose(bk[:, 4, s * 32:(s + 1) * 32], lt[:, s * P:(s + 1) * P],
                                                       ident[0:32, 0:32])
                        last.then_inc(lt_mm, 1)
                        pe.wait_ge(l_done, n + 1)

        router(nc, g, lg, gate, softmax_first=True, prefix="b2b_")

        s1 = m.sb("s1", [P, 2, BLK])
        hh = m.sb("hh", [P, 2, BLK])
        acc = m.sb("acc", [P, BPT, D])
        F = FinishNorm(m)
        ub = m.ps("ub", 4)
        db = m.ps("db", 2)
        up_mm = m.sem("up_mm")
        silu = m.sem("silu")
        h_done = m.sem("h_done")
        down_mm = m.sem("down_mm")
        acc_done = m.sem("acc_done")
        NX = NE + 1
        order = [NE] + list(range(NE))
        with nc.Block() as block:
            @block.scalar
            def _(act):
                with act.Fori(0, NBLK) as n:
                    for i in range(NX):
                        act.wait_ge(up_mm, (n * NX + i) * 2 + 1)
                        if i >= 2:
                            act.wait_ge(h_done, n * NX + i - 1)
                        nc.scalar.activation(s1[:, i % 2, :], ub[:, 2 * (i % 2), :], ACT.Silu).then_inc(silu, 1)

            @block.gpsimd
            def _(pool):
                with pool.Fori(0, NBLK) as n:
                    F.pool(nc, pool, n, S)

            @block.vector
            def _(dve):
                with dve.Fori(0, NBLK) as n:
                    def accumulate(i):
                        e = order[i]
                        dve.wait_ge(down_mm, n * NX + i + 1)
                        for s in range(BPT):
                            tile = bass.ds(n * BPT + s, 1)
                            src = db[:, i % 2, s * P:(s + 1) * P]
                            if i == 0:
                                nc.vector.tensor_tensor(acc[:, s, None, :], db[:, 0, None, s * P:(s + 1) * P],
                                                        x2[:, tile, :], ALU.add).then_inc(acc_done, 1)
                            else:
                                dve.wait_ge(acc_done, (n * NX + i) * BPT)
                                nc.vector.scalar_tensor_tensor(acc[:, s, :], src, gate[:, tile, e], acc[:, s, :],
                                                               ALU.mult, ALU.add).then_inc(acc_done, 1)

                    for i in range(NX):
                        dve.wait_ge(up_mm, (n * NX + i) * 2 + 2)
                        dve.wait_ge(silu, n * NX + i + 1)
                        if i >= 2:
                            dve.wait_ge(down_mm, n * NX + i - 1)
                        nc.vector.tensor_tensor(hh[:, i % 2, :], s1[:, i % 2, :], ub[:, 2 * (i % 2) + 1, :],
                                                ALU.mult).then_inc(h_done, 1)
                        if i >= 1:
                            accumulate(i - 1)
                    accumulate(NX - 1)
                    dve.wait_ge(acc_done, (n * NX + NX) * BPT)
                    F.vector(nc, dve, n, acc, X, S)

            @block.tensor
            def _(pe):
                with pe.Fori(0, NBLK) as n:
                    cols = bass.ds(n * BLK, BLK)

                    def up(i):
                        e = order[i]
                        if i >= 2:
                            pe.wait_ge(h_done, n * NX + i - 1)
                        for k in range(2):
                            matmul_split(nc, ub[:, 2 * (i % 2) + k, :], w1[0][:, k, e, :], w1[1][:, k, e, :],
                                         nh[:, cols], nl[:, cols]).then_inc(up_mm, 1)

                    def down(i):
                        pe.wait_ge(h_done, n * NX + i + 1)
                        if i >= 2:
                            pe.wait_ge(acc_done, (n * NX + i - 1) * BPT)
                        for s in range(BPT):
                            last = nc.tensor.matmul(db[:, i % 2, s * P:(s + 1) * P], hh[:, i % 2, s * P:(s + 1) * P],
                                                    w2[:, order[i], :], start=True, stop=True)
                        last.then_inc(down_mm, 1)

                    up(0)
                    for i in range(NX):
                        if i + 1 < NX:
                            up(i + 1)
                        down(i)
                    pe.wait_ge(acc_done, (n * NX + NX) * BPT)


class FinishNorm:

    def __init__(self, m):
        self.st = m.sb("fst", [P, BPT, 6])
        self.mv = m.sb("fmv", [P, BPT, 2])
        self.ve = m.sb("fve", [P, BPT])
        self.rs = m.sb("frs", [P, BPT])
        self.step = m.sem("fstep")
        self.powed = m.sem("fpowed")
        self.N = 2 * BPT + 1 + 2 * BPT

    def vector(self, nc, dve, n, acc, X, S):
        o = n * self.N
        for s in range(BPT):
            nc.vector.bn_stats(self.st[:, s, :], acc[:, s, :]).then_inc(self.step, 1)
        for s in range(BPT):
            wait_alone(dve, self.step, o + s + 1, S.passed)
            nc.vector.bn_aggr(self.mv[:, s, :], self.st[:, s, :]).then_inc(self.step, 1)
        dve.wait_ge(self.step, o + 2 * BPT)
        nc.vector.tensor_scalar(self.ve[:, :], self.mv[:, :, 1], 1e-5, None, ALU.add).then_inc(self.step, 1)
        dve.wait_ge(self.powed, n + 1)
        for s in range(BPT):
            nc.vector.tensor_scalar(acc[:, s, :], acc[:, s, :], self.mv[:, s, 0:1], self.rs[:, s:s + 1],
                                    ALU.subtract, ALU.mult).then_inc(self.step, 1)
        for s in range(BPT):
            dve.wait_ge(self.step, o + 2 * BPT + 2 + s)
            xs = X[:, bass.ds(n * BPT + s, 1), :]
            nc.vector.tensor_tensor(xs, xs, acc[:, s, None, :], ALU.add).then_inc(self.step, 1)
        dve.wait_ge(self.step, o + self.N)

    def pool(self, nc, pool, n, S):
        pool.wait_ge(self.step, n * self.N + 2 * BPT + 1)
        nc.gpsimd.tensor_tensor(self.rs[:, :], self.ve[:, :], S.half[:, 0:BPT], ALU.pow).then_inc(self.powed, 1)


def router(nc, g, lg, gate, softmax_first, prefix):
    T = TILES
    with Mem(nc, prefix) as t:
        pr = t.sb("pr", [P, T, NE])
        mx = t.sb("mx", [P, T])
        top = t.sb("top", [P, T, 8])
        idx = t.sb("idx", [P, T, 8], U32)
        idf = t.sb("idf", [P, T, 2])
        df = t.sb("df", [P, T])
        ex = t.sb("ex", [P, T])
        wt = t.sb("wt", [P, 2, T])
        oh = t.sb("oh", [P, T, NE])
        step = t.sem("step")
        exps = t.sem("exps")
        iota = g["iota"]
        with nc.Block() as block:
            @block.scalar
            def _(act):
                k = 0
                if softmax_first:
                    act.wait_ge(step, 2)
                    nc.scalar.activation(pr[:, :, :], pr[:, :, :], ACT.Exp).then_inc(exps, 1)
                    k = 3
                act.wait_ge(step, 2 + k + 2 * T - (0 if softmax_first else 1))
                nc.scalar.activation(ex[:, :], df[:, :], ACT.Exp).then_inc(exps, 1)

            @block.vector
            def _(dve):
                c = 0

                def bc(x):
                    return x.to_broadcast([P, T, NE])

                if softmax_first:
                    nc.vector.tensor_reduce(mx[:, :], lg[:, :, :], AXX, ALU.max).then_inc(step, 1)
                    dve.wait_ge(step, 1)
                    nc.vector.tensor_tensor(pr[:, :, :], lg[:, :, :], bc(mx[:, :, None]), ALU.subtract).then_inc(step, 1)
                    dve.wait_ge(exps, 1)
                    nc.vector.tensor_reduce(mx[:, :], pr[:, :, :], AXX, ALU.add).then_inc(step, 1)
                    dve.wait_ge(step, 3)
                    nc.vector.reciprocal(df[:, :], mx[:, :]).then_inc(step, 1)
                    dve.wait_ge(step, 4)
                    nc.vector.tensor_tensor(lg[:, :, :], pr[:, :, :], bc(df[:, :, None]), ALU.mult).then_inc(step, 1)
                    c = 5
                    dve.wait_ge(step, c)
                for i in range(T):
                    nc.vector.max(top[:, i, :], lg[:, i, :]).then_inc(step, 1)
                dve.wait_ge(step, c + T)
                nc.vector.tensor_tensor(df[:, :], top[:, :, 1], top[:, :, 0], ALU.subtract).then_inc(step, 1)
                for i in range(T):
                    nc.vector.max_index(idx[:, i, :], top[:, i, :], lg[:, i, :]).then_inc(step, 1)
                dve.wait_ge(step, c + 2 * T + 1)
                nc.vector.tensor_copy(idf[:, :, :], idx[:, :, 0:2]).then_inc(step, 1)
                dve.wait_ge(exps, 2 if softmax_first else 1)
                nc.vector.tensor_scalar(mx[:, :], ex[:, :], 1.0, None, ALU.add).then_inc(step, 1)
                dve.wait_ge(step, c + 2 * T + 3)
                nc.vector.reciprocal(wt[:, 0, :], mx[:, :]).then_inc(step, 1)
                dve.wait_ge(step, c + 2 * T + 4)
                nc.vector.tensor_tensor(wt[:, 1, :], ex[:, :], wt[:, 0, :], ALU.mult).then_inc(step, 1)
                for k, dst in ((0, gate), (1, oh)):
                    nc.vector.tensor_tensor(dst[:, :, :], iota[:, None, :].to_broadcast([P, T, NE]),
                                            bc(idf[:, :, k:k + 1]), ALU.is_equal).then_inc(step, 1)
                    dve.wait_ge(step, c + 2 * T + 6 + 2 * k)
                    nc.vector.tensor_tensor(dst[:, :, :], dst[:, :, :], bc(wt[:, k, :, None]), ALU.mult).then_inc(step, 1)
                dve.wait_ge(step, c + 2 * T + 9)
                nc.vector.tensor_tensor(gate[:, :, :], gate[:, :, :], oh[:, :, :], ALU.add).then_inc(step, 1)


def ffn_layer0(nc, dr, X, g):
    with Mem(nc, "b_") as m:
        ao = m.sb("ao", [P, TILES, D])
        wq = [m.sb(f"wq{k}", [P, HB, QROWS], F32R) for k in range(2)]
        wkv = [m.sb(f"wkv{k}", [P, P], F32R) for k in range(2)]
        w = {"w13": [m.sb(f"w13{k}", [P, 2, NE + 1, D], F32R) for k in range(2)],
             "wr": [m.sb(f"wr{k}", [P, P], F32R) for k in range(2)],
             "w2": m.sb("w2", [P, NE + 1, D]), "wo": m.sb("wo", [P, D]), "ebias": m.sb("ebias", [P, NE])}
        with Mem(nc, "b0_") as t:
            S = Stats(m, t, g)
            rq = t.sb("rq", [P, HB * QROWS])
            rkv = t.sb("rkv", [P, P])
            rr = t.sb("rr", [P, P])
            r13 = t.sb("r13", [P, 2 * (NE + 1) * D])
            g12 = t.sb("g12", [P, 2])
            w_in = t.sem("w_in")
            scaled = t.sem("scaled")
            hi = t.sem("hi")
            lo = t.sem("lo")
            sets = [(rq, wq, "p h q -> p (h q)", 0), (rkv, wkv, None, 0), (rr, w["wr"], None, 1),
                    (r13, w["w13"], "p k e f -> p (k e f)", 1)]

            def flat(x, pat):
                a = x[:, :] if pat is None else x[tuple([slice(None)] * len(x.shape))].rearrange(pat)
                return a

            with nc.Block() as block:
                @block.sync
                def _(sp):
                    for dst, src in ((rq[:, :], "b_wq"), (rkv[:, :], "b_wkv"), (rr[:, :], "b_wr"), (r13[:, :], "b_w13"),
                                     (g12[:, :], "b_g12"), (w["w2"][:, :, :], "b_w2"), (w["wo"][:, :], "b_wo"),
                                     (w["ebias"][:, :], "b_ebias"), (g["iota"][:, :], "iota")):
                        sp.dma_start(dst, dr[src]).then_inc(w_in, 16)
                    sp.wait_ge(w_in, 16 * 9)

                @block.vector
                def _(dve):
                    def weights():
                        dve.wait_ge(w_in, 16 * 9)
                        for raw, _, _, gi in sets:
                            nc.vector.tensor_scalar(raw[:, :], raw[:, :], g12[:, gi:gi + 1], None,
                                                    ALU.mult).then_inc(scaled, 1)
                        for k, (raw, dst, pat, _) in enumerate(sets):
                            dve.wait_ge(hi, k + 1)
                            nc.vector.tensor_tensor(flat(dst[1], pat), raw[:, :], flat(dst[0], pat).bitcast(F32),
                                                    ALU.subtract).then_inc(lo, 1)
                    stats_vector(nc, dve, X, S, 1e-6, weights)

                @block.gpsimd
                def _(pool):
                    stats_pool(nc, pool, S)

                @block.scalar
                def _(act):
                    for k, (raw, dst, pat, _) in enumerate(sets):
                        act.wait_ge(scaled, k + 1)
                        nc.scalar.activation(flat(dst[0], pat), raw[:, :], ACT.Copy).then_inc(hi, 1)
        mqa_attention(nc, dr, X, g, S, wq, wkv, ao)
        ffn_mixture(nc, dr, X, g, S, w, ao)


HC = 2
SCALE_C = float(D) ** -0.5


def causal_attention(nc, dr, X, g):
    with Mem(nc, "c_") as m:
        NW = 2 * (1 + HC)
        wh = m.sb("wh", [P, NW, D], F32R)
        wl = m.sb("wl", [P, NW, D], F32R)
        wv = m.sb("wv", [P, D])
        wo = m.sb("wo", [P, HC, D])
        mask = m.sb("mask", [P, P], BF16)
        cosT = m.sb("cosT", [P, SEQ])
        sinT = m.sb("sinT", [P, SEQ])
        with Mem(nc, "c0_") as t:
            S = Stats(m, t, g)
            raw = t.sb("raw", [P, NW, D])
            w_in = t.sem("w_in")
            c_in = t.sem("c_in")
            rot = t.sem("rot")
            hi = t.sem("hi")
            lo = t.sem("lo")
            with nc.Block() as block:
                @block.sync
                def _(sp):
                    sp.dma_start(raw[:, 0::2, :], dr["c_wkq"]).then_inc(w_in, 16)
                    for dst, src in ((wv[:, :], "c_wv"), (wo[:, :, :], "c_wo"), (mask[:, :], "mask1"),
                                     (cosT[:, :], "cos1"), (sinT[:, :], "sin1")):
                        sp.dma_start(dst, dr[src]).then_inc(c_in, 16)
                    sp.wait_ge(c_in, 16 * 5)

                @block.vector
                def _(dve):
                    def weights():
                        dve.wait_ge(w_in, 16)
                        for k in range(0, NW, 2):
                            src = raw[:, k, :].rearrange("p (n two) -> p n two", two=2)
                            dst = raw[:, k + 1, :].rearrange("p (n two) -> p n two", two=2)
                            nc.vector.tensor_scalar(dst[:, :, 0], src[:, :, 1], -1.0, None, ALU.mult).then_inc(rot, 1)
                            nc.vector.tensor_copy(dst[:, :, 1], src[:, :, 0]).then_inc(rot, 1)
                        dve.wait_ge(hi, 1)
                        nc.vector.tensor_tensor(wl[:, :, :], raw[:, :, :], wh[:, :, :].bitcast(F32),
                                                ALU.subtract).then_inc(lo, 1)
                    stats_vector(nc, dve, X, S, 1e-5, weights)

                @block.gpsimd
                def _(pool):
                    stats_pool(nc, pool, S)

                @block.scalar
                def _(act):
                    act.wait_ge(rot, NW)
                    nc.scalar.activation(wh[:, :, :], raw[:, :, :], ACT.Copy).then_inc(hi, 1)

        xn = m.sb("xn", [P, BPT, D])
        x32 = m.sb("x32", [P, BLK])
        xh = m.sb("xh", [P, BLK], F32R)
        xl = m.sb("xl", [P, BLK], F32R)
        t1 = m.sb("t1", [P, 2, BLK])
        t2 = m.sb("t2", [P, 2, BLK])
        rp = m.sb("rp", [P, 2, BLK])
        kqh = m.sb("kqh", [P, 1 + HC, SEQ], F32R)
        kql = m.sb("kql", [P, 1 + HC, SEQ], F32R)
        v = m.sb("v", [P, KT, D])
        p = m.sb("p", [P, 2, SEQ])
        pt = m.sb("pt", [P, 2, BLK])
        mp = m.sb("mp", [P, 2, NCH])
        mm = m.sb("mm", [P, 2])
        nb = m.sb("nb", [P, 2])
        ps = m.sb("ps", [P, 2, NCH])
        den = m.sb("den", [P, 2])
        rden = m.sb("rden", [P, 2])
        o = m.sb("o", [P, HC, D])
        ot = m.sb("ot", [P, HC * P])
        acc = m.sb("acc", [P, BPT, D])
        F = FinishNorm(m)
        sb4 = m.ps("sb4", 4)
        tb = m.ps("tb", 2)
        pv = m.ps("pv")
        misc = m.ps("misc")

        xn_ready = m.sem("xn_ready")
        xt_mm = m.sem("xt_mm")
        x_copied = m.sem("x_copied")
        xl_ready = m.sem("xl_ready")
        v_mm = m.sem("v_mm")
        v_copied = m.sem("v_copied")
        proj_mm = m.sem("proj_mm")
        rope_mul = m.sem("rope_mul")
        rope_add = m.sem("rope_add")
        rope_hi = m.sem("rope_hi")
        rope_lo = m.sem("rope_lo")
        s_mm = m.sem("s_mm")
        s_max = m.sem("s_max")
        bias_step = m.sem("bias_step")
        exp_done = m.sem("exp_done")
        pt_mm = m.sem("pt_mm")
        pt_copied = m.sem("pt_copied")
        pv_mm = m.sem("pv_mm")
        den_step = m.sem("den_step")
        o_ready = m.sem("o_ready")
        ot_mm = m.sem("ot_mm")
        ot_copied = m.sem("ot_copied")
        out_mm = m.sem("out_mm")
        y_copied = m.sem("y_copied")

        units = [(qt, h) for qt in range(KT) for h in range(HC)]
        NU = len(units)
        chunks = [(qt + BPT) // BPT for qt, _ in units]
        first = [sum(chunks[:u]) for u in range(NU + 1)]
        NC = first[NU]
        R = 1 + HC

        def tiles_of(u, c):
            return min(BPT, units[u][0] + 1 - c * BPT)

        with nc.Block() as block:
            @block.vector
            def _(dve):
                def load(b, i):
                    n = b * BB + i
                    for s in range(BPT):
                        tile = bass.ds(n * BPT + s, 1)
                        nc.vector.tensor_scalar(xn[:, s, :], X[:, tile, :], S.mean[:, tile, 0], S.r[:, tile],
                                                ALU.subtract, ALU.mult).then_inc(xn_ready, 1)
                    dve.wait_ge(x_copied, n * 2 + 2)
                    nc.vector.tensor_tensor(xl[:, :], misc[:, :], xh[:, :].bitcast(F32), ALU.subtract).then_inc(xl_ready, 1)
                    cols = bass.ds(i * BLK, BLK)
                    for k in range(R):
                        dve.wait_ge(proj_mm, n * R + k + 1)
                        if k == 2:
                            dve.wait_ge(rope_add, n * R + 1)
                        nc.vector.tensor_tensor(t1[:, k % 2, :], sb4[:, 2 * (k % 2), :], cosT[:, cols],
                                                ALU.mult).then_inc(rope_mul, 1)
                        nc.vector.tensor_tensor(t2[:, k % 2, :], sb4[:, 2 * (k % 2) + 1, :], sinT[:, cols],
                                                ALU.mult).then_inc(rope_mul, 1)
                    for k in range(R):
                        dve.wait_ge(rope_hi, n * R + k + 1)
                        nc.vector.tensor_tensor(kql[:, k, cols], rp[:, k % 2, :], kqh[:, k, cols].bitcast(F32),
                                                ALU.subtract).then_inc(rope_lo, 1)

                def chunk_max(b, u, c):
                    G = b * NC + first[u] + c
                    dve.wait_ge(s_mm, G + 1)
                    nc.vector.tensor_reduce(mp[:, u % 2, c:c + 1], sb4[:, (first[u] + c) % 4, 0:tiles_of(u, c) * P],
                                            AXX, ALU.max).then_inc(s_max, 1)

                def bias(b, u):
                    U = b * NU + u
                    dve.wait_ge(s_max, b * NC + first[u + 1])
                    nc.vector.tensor_reduce(mm[:, u % 2:u % 2 + 1], mp[:, u % 2, 0:chunks[u]], AXX,
                                            ALU.max).then_inc(bias_step, 1)
                    dve.wait_ge(bias_step, U * 2 + 1)
                    nc.vector.tensor_scalar(nb[:, u % 2:u % 2 + 1], mm[:, u % 2:u % 2 + 1], -SCALE_C, None,
                                            ALU.mult).then_inc(bias_step, 1)

                def output(b, u):
                    U = b * NU + u
                    w = u % 2
                    dve.wait_ge(exp_done, b * NC + first[u + 1])
                    nc.vector.tensor_reduce(den[:, w:w + 1], ps[:, w, 0:chunks[u]], AXX, ALU.add).then_inc(den_step, 1)
                    dve.wait_ge(den_step, U * 2 + 1)
                    nc.vector.reciprocal(rden[:, w:w + 1], den[:, w:w + 1]).then_inc(den_step, 1)
                    dve.wait_ge(den_step, U * 2 + 2)
                    dve.wait_ge(pv_mm, b * NC + first[u + 1])
                    nc.vector.tensor_scalar(o[:, w, :], pv[:, 0:D], rden[:, w:w + 1], None, ALU.mult).then_inc(o_ready, 1)

                def row_done(b, qt):
                    dve.wait_ge(out_mm, b * KT + qt + 1)
                    nc.vector.tensor_copy(acc[:, qt % BPT, :], misc[:, 2 * P:3 * P]).then_inc(y_copied, 1)
                    if qt % BPT == BPT - 1:
                        dve.wait_ge(y_copied, b * KT + qt + 1)
                        F.vector(nc, dve, b * BB + qt // BPT, acc, X, S)

                with dve.Fori(0, BATCH) as b:
                    with dve.Fori(0, BB) as i:
                        load(b, i)
                    for c in range(chunks[0]):
                        chunk_max(b, 0, c)
                    bias(b, 0)
                    for u in range(NU):
                        nxt = chunks[u + 1] if u + 1 < NU else 0
                        for c in range(max(nxt, chunks[u])):
                            if c < nxt:
                                chunk_max(b, u + 1, c)
                            if c < chunks[u]:
                                G = b * NC + first[u] + c
                                dve.wait_ge(pt_mm, G + 1)
                                if first[u] + c >= 2:
                                    dve.wait_ge(pv_mm, G - 1)
                                wd = tiles_of(u, c) * P
                                gi = (first[u] + c) % 2
                                nc.vector.tensor_copy(pt[:, gi, 0:wd], tb[:, gi, 0:wd]).then_inc(pt_copied, 1)
                        if nxt:
                            bias(b, u + 1)
                        output(b, u)
                        if u % 2 == 0 and u > 0:
                            row_done(b, units[u][0] - 1)
                    row_done(b, KT - 1)

            @block.gpsimd
            def _(pool):
                def load(b, i):
                    n = b * BB + i
                    for k in range(R):
                        pool.wait_ge(rope_mul, n * 2 * R + 2 * k + 2)
                        if k == 2:
                            pool.wait_ge(rope_lo, n * R + 1)
                        nc.gpsimd.tensor_tensor(rp[:, k % 2, :], t1[:, k % 2, :], t2[:, k % 2, :], ALU.add)\
                            .then_inc(rope_add, 1)

                with pool.Fori(0, BATCH) as b:
                    with pool.Fori(0, BB) as i:
                        load(b, i)
                    with pool.Fori(0, BB) as i:
                        F.pool(nc, pool, b * BB + i, S)

            @block.scalar
            def _(act):
                def load(b, i):
                    n = b * BB + i
                    act.wait_ge(xt_mm, n + 1)
                    nc.scalar.activation(x32[:, :], misc[:, :], ACT.Copy).then_inc(x_copied, 1)
                    nc.scalar.activation(xh[:, :], misc[:, :], ACT.Copy).then_inc(x_copied, 1)
                    act.wait_ge(v_mm, n + 1)
                    nc.scalar.activation(v[:, bass.ds(i * BPT, BPT), :], pv[:, :].rearrange("p (a b) -> p a b", b=D),
                                         ACT.Copy).then_inc(v_copied, 1)
                    for k in range(R):
                        act.wait_ge(rope_add, n * R + k + 1)
                        nc.scalar.activation(kqh[:, k, bass.ds(i * BLK, BLK)], rp[:, k % 2, :], ACT.Copy).then_inc(rope_hi, 1)

                with act.Fori(0, BATCH) as b:
                    with act.Fori(0, BB) as i:
                        load(b, i)
                    for u in range(NU):
                        w = u % 2
                        act.wait_ge(bias_step, (b * NU + u) * 2 + 2)
                        if u >= 2:
                            act.wait_ge(den_step, (b * NU + u - 1) * 2)
                        for c in range(chunks[u]):
                            wd = tiles_of(u, c) * P
                            nc.scalar.activation(p[:, w, c * BLK:c * BLK + wd], sb4[:, (first[u] + c) % 4, 0:wd], ACT.Exp,
                                                 bias=nb[:, w:w + 1], scale=SCALE_C,
                                                 accum_out=ps[:, w, c:c + 1]).then_inc(exp_done, 1)
                        if w == 0 and u > 0:
                            act.wait_ge(ot_mm, b * KT + units[u][0])
                            nc.scalar.activation(ot[:, :], misc[:, 0:HC * P], ACT.Copy).then_inc(ot_copied, 1)
                    act.wait_ge(ot_mm, b * KT + KT)
                    nc.scalar.activation(ot[:, :], misc[:, 0:HC * P], ACT.Copy).then_inc(ot_copied, 1)

            @block.tensor
            def _(pe):
                ident, identb = g["ident"], g["identb"]

                def load(b, i):
                    n = b * BB + i
                    for s in range(BPT):
                        pe.wait_ge(xn_ready, n * BPT + s + 1)
                        last = nc.tensor.transpose(misc[:, s * P:(s + 1) * P], xn[:, s, :], ident[:, :])
                    last.then_inc(xt_mm, 1)
                    pe.wait_ge(x_copied, n * 2 + 2)
                    for s in range(BPT):
                        last = nc.tensor.matmul(pv[:, s * P:(s + 1) * P], x32[:, s * P:(s + 1) * P], wv[:, :],
                                                start=True, stop=True)
                    last.then_inc(v_mm, 1)
                    pe.wait_ge(xl_ready, n + 1)
                    for k in range(R):
                        if k == 2:
                            pe.wait_ge(rope_mul, n * 2 * R + 2)
                        for r in range(2):
                            last = matmul_split(nc, sb4[:, 2 * (k % 2) + r, :], wh[:, 2 * k + r, :], wl[:, 2 * k + r, :],
                                                xh[:, :], xl[:, :])
                        last.then_inc(proj_mm, 1)
                    pe.wait_ge(rope_mul, n * 2 * R + 2 * R)
                    pe.wait_ge(v_copied, n + 1)

                def scores(b, u, c):
                    qt, h = units[u]
                    k = first[u] + c
                    if k >= 4:
                        pe.wait_ge(exp_done, b * NC + k - 3)
                    qs = slice(qt * P, (qt + 1) * P)
                    wd = max(2, tiles_of(u, c)) * P
                    ks = slice(c * BLK, c * BLK + wd)
                    diag = c == chunks[u] - 1
                    last = matmul_split(nc, sb4[:, k % 4, 0:wd], kqh[:, 1 + h, qs], kql[:, 1 + h, qs],
                                        kqh[:, 0, ks], kql[:, 0, ks])
                    if diag:
                        d0 = (tiles_of(u, c) - 1) * P
                        last = nc.tensor.matmul(sb4[:, k % 4, d0:d0 + P], identb[:, :], mask[:, :], start=False, stop=True,
                                                skip_group_check=True)
                    last.then_inc(s_mm, 1)

                def transposes(b, u, c):
                    k = first[u] + c
                    pe.wait_ge(exp_done, b * NC + k + 1)
                    if k >= 2:
                        pe.wait_ge(pt_copied, b * NC + k - 1)
                    for a in range(tiles_of(u, c)):
                        last = nc.tensor.transpose(tb[:, k % 2, a * P:(a + 1) * P],
                                                   p[:, u % 2, c * BLK + a * P:c * BLK + (a + 1) * P], ident[:, :])
                    last.then_inc(pt_mm, 1)

                def values(b, u, c):
                    k = first[u] + c
                    pe.wait_ge(pt_copied, b * NC + k + 1)
                    if c == 0 and u > 0:
                        pe.wait_ge(o_ready, b * NU + u)
                    nt = tiles_of(u, c)
                    for a in range(nt):
                        last = nc.tensor.matmul(pv[:, 0:D], pt[:, k % 2, a * P:(a + 1) * P], v[:, c * BPT + a, :],
                                                start=(c == 0 and a == 0), stop=(c == chunks[u] - 1 and a == nt - 1))
                    last.then_inc(pv_mm, 1)

                def turn(b, qt):
                    pe.wait_ge(o_ready, b * NU + 2 * qt + 2)
                    if qt > 0:
                        pe.wait_ge(y_copied, b * KT + qt)
                    for h in range(HC):
                        last = nc.tensor.transpose(misc[:, h * P:(h + 1) * P], o[:, h, :], ident[:, :])
                    last.then_inc(ot_mm, 1)

                def out_project(b, qt):
                    pe.wait_ge(ot_copied, b * KT + qt + 1)
                    for h in range(HC):
                        last = nc.tensor.matmul(misc[:, 2 * P:3 * P], ot[:, h * P:(h + 1) * P], wo[:, h, :],
                                                start=(h == 0), stop=(h == HC - 1))
                    last.then_inc(out_mm, 1)

                with pe.Fori(0, BATCH) as b:
                    with pe.Fori(0, BB) as i:
                        load(b, i)
                    pe.wait_ge(rope_lo, (b + 1) * BB * R)
                    for c in range(chunks[0]):
                        scores(b, 0, c)
                    for u in range(NU):
                        nxt = chunks[u + 1] if u + 1 < NU else 0
                        for c in range(max(nxt, chunks[u] + 1)):
                            if c < nxt:
                                scores(b, u + 1, c)
                            if c < chunks[u]:
                                transposes(b, u, c)
                            if c == 0 and u % 2 == 0 and u > 0:
                                turn(b, units[u][0] - 1)
                            if 1 <= c <= chunks[u]:
                                values(b, u, c - 1)
                        if u % 2 == 0 and u > 0:
                            out_project(b, units[u][0] - 1)
                    turn(b, KT - 1)
                    out_project(b, KT - 1)
                    pe.wait_ge(y_copied, (b + 1) * KT)


FF = 4 * D
FC = FF // P


def ffn_layer1(nc, dr, X, g, out):
    with Mem(nc, "d_") as m:
        wh = m.sb("wh", [P, NE, FF], F32R)
        wl = m.sb("wl", [P, NE, FF], F32R)
        w2 = m.sb("w2", [P, NE, FC, D])
        b1 = m.sb("b1", [P, NE, FC])
        b2 = m.sb("b2", [P, NE, D])
        wr = [m.sb(f"wr{k}", [P, P], F32R) for k in range(2)]
        rbias = m.sb("rbias", [P, NE])
        inv = m.sb("inv", [P, TILES])
        with Mem(nc, "d0_") as t:
            S = Stats(m, t, g)
            raw = t.sb("raw", [P, NE, FF])
            b1raw = t.sb("b1raw", [P, NE, FC])
            rr = t.sb("rr", [P, P])
            lng = t.sb("lng", [P, NE])
            lnb = t.sb("lnb", [P, NE])
            bp = t.ps("bp")
            w_in = t.sem("w_in")
            c_in = t.sem("c_in")
            hi = t.sem("hi")
            lo = t.sem("lo")
            b_mm = t.sem("b_mm")
            b_done = t.sem("b_done")
            with nc.Block() as block:
                @block.sync
                def _(sp):
                    for dst, src in ((raw[:, :, :], "d_w1"), (lng[:, :], "d_lng"), (lnb[:, :], "d_lnb"),
                                     (rr[:, :], "d_wr"), (b1raw[:, :, :], "d_b1")):
                        sp.dma_start(dst, dr[src]).then_inc(w_in, 16)
                    for dst, src in ((w2[:, :, :, :], "d_w2"), (b2[:, :, :], "d_b2"), (rbias[:, :], "d_rbias")):
                        sp.dma_start(dst, dr[src]).then_inc(c_in, 16)
                    sp.wait_ge(c_in, 16 * 3)

                @block.scalar
                def _(act):
                    act.wait_ge(w_in, 16 * 5)
                    for e in range(NE):
                        nc.scalar.activation(wh[:, e, :], raw[:, e, :], ACT.Copy, scale=lng[:, e:e + 1]).then_inc(hi, 1)
                    nc.scalar.activation(wr[0][:, :], rr[:, :], ACT.Copy).then_inc(hi, 1)

                @block.vector
                def _(dve):
                    def weights():
                        for e in range(NE):
                            dve.wait_ge(hi, e + 1)
                            nc.vector.scalar_tensor_tensor(wl[:, e, :], raw[:, e, :], lng[:, e:e + 1],
                                                           wh[:, e, :].bitcast(F32), ALU.mult,
                                                           ALU.subtract).then_inc(lo, 1)
                        dve.wait_ge(hi, NE + 1)
                        nc.vector.tensor_tensor(wr[1][:, :], rr[:, :], wr[0][:, :].bitcast(F32),
                                                ALU.subtract).then_inc(lo, 1)
                    stats_vector(nc, dve, X, S, 1e-5, weights)
                    nc.vector.reciprocal(inv[:, :], S.r2[:, :]).then_inc(b_done, 1)
                    dve.wait_ge(b_mm, 1)
                    nc.vector.tensor_tensor(b1[:, :, :], bp[:, 0:NE * FC].rearrange("p (e c) -> p e c", c=FC),
                                            b1raw[:, :, :], ALU.add).then_inc(b_done, 1)

                @block.gpsimd
                def _(pool):
                    stats_pool(nc, pool, S)

                @block.tensor
                def _(pe):
                    pe.wait_ge(w_in, 16 * 5)
                    for e in range(NE):
                        for c in range(FC):
                            last = nc.tensor.matmul(bp[:, e * FC + c:e * FC + c + 1], raw[:, e, c * P:(c + 1) * P],
                                                    lnb[:, e:e + 1], start=True, stop=True)
                    last.then_inc(b_mm, 1)

        nh = m.sb("nh", [P, TILES * P], F32R)
        nl = m.sb("nl", [P, TILES * P], F32R)
        lg = m.sb("lg", [P, TILES, NE])
        gate = m.sb("gate", [P, TILES, NE])
        gsum = m.sb("gsum", [P, TILES])
        with Mem(nc, "d1_") as t:
            xn = t.sb("xn", [P, BPT, D])
            lt = t.sb("lt", [32, BLK])
            bk = t.ps("bk", 3)
            xn_done = t.sem("xn_done")
            xt_mm = t.sem("xt_mm")
            xh_done = t.sem("xh_done")
            xl_done = t.sem("xl_done")
            l_mm = t.sem("l_mm")
            l_copied = t.sem("l_copied")
            lt_mm = t.sem("lt_mm")
            l_done = t.sem("l_done")
            with nc.Block() as block:
                @block.scalar
                def _(act):
                    with act.Fori(0, NBLK) as n:
                        act.wait_ge(xt_mm, n + 1)
                        nc.scalar.activation(nh[:, bass.ds(n * BLK, BLK)], bk[:, 0, :], ACT.Copy).then_inc(xh_done, 1)
                        act.wait_ge(l_mm, n + 1)
                        nc.scalar.activation(lt[:, :], bk[0:32, 1, :], ACT.Copy).then_inc(l_copied, 1)

                @block.vector
                def _(dve):
                    with dve.Fori(0, NBLK) as n:
                        for s in range(BPT):
                            tile = bass.ds(n * BPT + s, 1)
                            nc.vector.tensor_scalar(xn[:, s, :], X[:, tile, :], S.mean[:, tile, 0], S.rr[:, tile],
                                                    ALU.subtract, ALU.mult).then_inc(xn_done, 1)
                        cols = bass.ds(n * BLK, BLK)
                        blk = bass.ds(n * BPT, BPT)
                        dve.wait_ge(xh_done, n + 1)
                        nc.vector.tensor_tensor(nl[:, cols], bk[:, 0, :], nh[:, cols].bitcast(F32),
                                                ALU.subtract).then_inc(xl_done, 1)
                        dve.wait_ge(lt_mm, n + 1)
                        nc.vector.tensor_tensor(lg[:, blk, :],
                                                bk[:, 2, 0:BPT * 32].rearrange("p (a b) -> p a b", b=32)[:, :, 0:NE],
                                                inv[:, blk, None].to_broadcast([P, BPT, NE]), ALU.mult).then_inc(l_done, 1)
                        dve.wait_ge(l_done, n * 2 + 1)
                        nc.vector.tensor_tensor(lg[:, blk, :], lg[:, blk, :], rbias[:, None, :].to_broadcast([P, BPT, NE]),
                                                ALU.add).then_inc(l_done, 1)

                @block.tensor
                def _(pe):
                    ident = g["ident"]
                    with pe.Fori(0, NBLK) as n:
                        for s in range(BPT):
                            pe.wait_ge(xn_done, n * BPT + s + 1)
                            last = nc.tensor.transpose(bk[:, 0, s * P:(s + 1) * P], xn[:, s, :], ident[:, :])
                        last.then_inc(xt_mm, 1)
                        pe.wait_ge(xh_done, n + 1)
                        pe.wait_ge(xl_done, n + 1)
                        cols = bass.ds(n * BLK, BLK)
                        matmul_split(nc, bk[:, 1, :], wr[0][:, :], wr[1][:, :], nh[:, cols], nl[:, cols]).then_inc(l_mm, 1)
                        wait_alone(pe, l_copied, n + 1, g["passed_pe"])
                        for s in range(BPT):
                            last = nc.tensor.transpose(bk[:, 2, s * 32:(s + 1) * 32], lt[:, s * P:(s + 1) * P],
                                                       ident[0:32, 0:32])
                        last.then_inc(lt_mm, 1)
                        pe.wait_ge(l_done, n * 2 + 2)

        router(nc, g, lg, gate, softmax_first=False, prefix="d2_")

        a = m.sb("a", [P, 2, FC, BLK])
        xi = m.sb("xi", [P, BPT, D])
        acc = m.sb("acc", [P, BPT, D])
        F = FinishNorm(m)
        ub = m.ps("ub", FC)
        db = m.ps("db", 2)
        summed = m.sem("summed")
        ln = m.sem("ln")
        up_mm = m.sem("up_mm")
        gelu = m.sem("gelu")
        down_mm = m.sem("down_mm")
        acc_done = m.sem("acc_done")
        stored = m.sem("stored")
        NA = BPT * (1 + 2 * NE)
        with nc.Block() as block:
            @block.sync
            def _(sp):
                with sp.Fori(0, NBLK) as n:
                    sp.wait_ge(F.step, n * F.N + F.N)
                    sp.dma_start(out.rearrange("(t p) d -> p t d", p=P)[:, bass.ds(n * BPT, BPT), :],
                                 X[:, bass.ds(n * BPT, BPT), :]).then_inc(stored, 16)
                sp.wait_ge(stored, 16 * NBLK)

            @block.scalar
            def _(act):
                with act.Fori(0, NBLK) as n:
                    for e in range(NE):
                        for c in range(FC):
                            act.wait_ge(up_mm, (n * NE + e) * FC + c + 1)
                            if e >= 2 and c == 0:
                                act.wait_ge(down_mm, n * NE + e - 1)
                            nc.scalar.activation(a[:, e % 2, c, :], ub[:, c, :], ACT.Gelu,
                                                 bias=b1[:, e, c:c + 1]).then_inc(gelu, 1)

            @block.gpsimd
            def _(pool):
                with pool.Fori(0, NBLK) as n:
                    F.pool(nc, pool, n, S)

            @block.vector
            def _(dve):
                nc.vector.tensor_reduce(gsum[:, :], gate[:, :, :], AXX, ALU.add).then_inc(summed, 1)
                dve.wait_ge(summed, 1)
                with dve.Fori(0, NBLK) as n:
                    tiles = [bass.ds(n * BPT + s, 1) for s in range(BPT)]
                    for s in range(BPT):
                        nc.vector.tensor_scalar(xi[:, s, :], X[:, tiles[s], :], S.mean[:, tiles[s], 0], S.r[:, tiles[s]],
                                                ALU.subtract, ALU.mult).then_inc(ln, 1)
                    for s in range(BPT):
                        dve.wait_ge(ln, n * BPT + s + 1)
                        nc.vector.tensor_scalar(acc[:, s, :], xi[:, s, :], gsum[:, tiles[s]], None,
                                                ALU.mult).then_inc(acc_done, 1)
                    for e in range(NE):
                        for s in range(BPT):
                            dve.wait_ge(acc_done, n * NA + e * BPT + s + 1)
                            nc.vector.scalar_tensor_tensor(acc[:, s, :], b2[:, e, :], gate[:, tiles[s], e], acc[:, s, :],
                                                           ALU.mult, ALU.add).then_inc(acc_done, 1)
                    for e in range(NE):
                        dve.wait_ge(down_mm, n * NE + e + 1)
                        for s in range(BPT):
                            dve.wait_ge(acc_done, n * NA + (NE + e) * BPT + s + 1)
                            nc.vector.scalar_tensor_tensor(acc[:, s, :], db[:, e % 2, s * P:(s + 1) * P],
                                                           gate[:, tiles[s], e], acc[:, s, :], ALU.mult,
                                                           ALU.add).then_inc(acc_done, 1)
                    dve.wait_ge(acc_done, n * NA + NA)
                    F.vector(nc, dve, n, acc, X, S)

            @block.tensor
            def _(pe):
                with pe.Fori(0, NBLK) as n:
                    cols = bass.ds(n * BLK, BLK)

                    def up(e, c):
                        if e > 0:
                            pe.wait_ge(gelu, (n * NE + e - 1) * FC + c + 1)
                        cs = slice(c * P, (c + 1) * P)
                        matmul_split(nc, ub[:, c, :], wh[:, e, cs], wl[:, e, cs], nh[:, cols], nl[:, cols]).then_inc(up_mm, 1)

                    def down(e, s):
                        if s == 0:
                            pe.wait_ge(gelu, (n * NE + e + 1) * FC)
                            if e >= 2:
                                pe.wait_ge(acc_done, n * NA + (NE + e) * BPT)
                        for c in range(FC):
                            last = nc.tensor.matmul(db[:, e % 2, s * P:(s + 1) * P], a[:, e % 2, c, s * P:(s + 1) * P],
                                                    w2[:, e, c, :], start=(c == 0), stop=(c == FC - 1))
                        if s == BPT - 1:
                            last.then_inc(down_mm, 1)

                    for c in range(FC):
                        up(0, c)
                    for e in range(NE):
                        for s in range(BPT):
                            if e + 1 < NE:
                                up(e + 1, s)
                            down(e, s)
                    pe.wait_ge(gelu, (n + 1) * NE * FC)
                    pe.wait_ge(acc_done, n * NA + NA)


def rope_tables(n, d, scale):
    pos = np.arange(0, d, 2, dtype=np.float32)
    if scale == 1:
        freq = (np.float32(1.0) / np.float32(10000.0) ** (pos / np.float32(d))).astype(np.float32)
    else:
        freq = (np.float32(10000.0) ** (np.float32(-2.0) * pos / np.float32(d))).astype(np.float32)
    ang = np.arange(n, dtype=np.float32)[None, :] * freq[:, None]
    return (np.repeat(np.cos(ang), 2, axis=0).astype(np.float32),
            np.repeat(np.sin(ang), 2, axis=0).astype(np.float32))


def host_layout(a):
    f = np.float32
    z = {}
    z["ident"] = np.eye(P, dtype=f)
    z["identb"] = np.eye(P, dtype=f).astype(mybir.dt.np(BF16))
    cos, sin = rope_tables(SEQ, DH0, 1)
    z["cos0"], z["sin0"] = np.tile(cos, (2, 1)), np.tile(sin, (2, 1))
    row = np.arange(P)[:, None] % SEG
    col = np.arange(KEYS0)[None, :]
    masked = np.where((col < PM) | (col - PM <= row), 0.0, -1e30)
    z["mask0"] = np.tile(masked, (1, 6)).astype(mybir.dt.np(BF16))
    z["x"] = a["L0_attn_seq"].reshape(-1, D)
    z["norm_w"] = a["L0_attn_norm_w"].reshape(D, 1)
    z["w_qkv"] = a["L0_attn_w_qkv"]
    z["w_out"] = a["L0_attn_w_out"].reshape(PAIRS, P, D).transpose(1, 0, 2)
    z["b_out"] = np.broadcast_to(a["L0_attn_b_out"], (P, D))
    pk, pv = a["L0_attn_pm_k"], a["L0_attn_pm_v"]
    pmk = np.zeros((P, PAIRS, 2 * KEYS0), f)
    pmv = np.zeros((P, PAIRS, P), f)
    for h in range(H0):
        rows = slice((h % 2) * DH0, (h % 2 + 1) * DH0)
        pmk[rows, h // 2, (h % 2) * KEYS0:(h % 2) * KEYS0 + PM] = pk[h].T
        pmv[rows, h // 2, (h % 8) * PM:(h % 8 + 1) * PM] = pv[h].T
    z["pmkT"], z["pmvT"] = pmk, pmv
    wq, wkc, wvc = a["L0_ffn_Wq"].T, a["L0_ffn_Wkc"].T, a["L0_ffn_Wvc"].T
    z["b_wq"] = np.concatenate([wq[:, h * DK:(h + 1) * DK] for h in range(HB) for _ in range(3)], axis=1)
    z["b_wkv"] = np.concatenate([wkc, wkc, wkc, wvc], axis=1)
    z["b_wr"] = np.pad(a["L0_ffn_Wr"].T, ((0, 0), (0, P - NE)))
    z["b_w13"] = np.concatenate([
        np.concatenate([a["L0_ffn_eW" + k].transpose(2, 0, 1), a["L0_ffn_sW" + k].T[:, None, :]], axis=1)
        .reshape(D, -1) for k in "13"], axis=1)
    z["b_g12"] = np.stack([a["L0_ffn_g1"], a["L0_ffn_g2"]], axis=1)
    z["b_w2"] = np.concatenate([a["L0_ffn_eW2"].transpose(2, 0, 1), a["L0_ffn_sW2"].T[:, None, :]], axis=1)
    z["b_wo"] = a["L0_ffn_Wo"].T
    z["b_ebias"] = np.broadcast_to(a["L0_ffn_expert_bias"], (P, NE))
    z["iota"] = np.broadcast_to(np.arange(NE, dtype=f), (P, NE))
    cos, sin = rope_tables(SEQ, D, 2)
    z["cos1"], z["sin1"] = cos, sin
    z["mask1"] = np.where(np.arange(P)[None, :] <= np.arange(P)[:, None], 0.0, -1e30).astype(mybir.dt.np(BF16))
    z["c_wkq"] = np.stack([a["L1_attn_Wk"].T] + [a["L1_attn_Wq"][h].T for h in range(HC)], axis=1)
    z["c_wv"] = a["L1_attn_Wv"].T
    z["c_wo"] = a["L1_attn_Wo"].T.reshape(HC, D, D).transpose(1, 0, 2)
    z["d_w1"] = a["L1_ffn_W1"].transpose(1, 0, 2)
    z["d_lng"], z["d_lnb"] = a["L1_ffn_ln_g"].T, a["L1_ffn_ln_b"].T
    z["d_wr"] = np.pad(a["L1_ffn_router_W"], ((0, 0), (0, P - NE)))
    z["d_b1"] = a["L1_ffn_b1"].reshape(NE, FC, P).transpose(2, 0, 1)
    z["d_w2"] = a["L1_ffn_W2"].reshape(NE, FC, P, D).transpose(2, 0, 1, 3)
    z["d_b2"] = np.broadcast_to(a["L1_ffn_b2"], (P, NE, D))
    z["d_rbias"] = np.broadcast_to(a["L1_ffn_router_b"], (P, NE))
    return {k: np.ascontiguousarray(v) for k, v in z.items()}


def build_program(nc, dr, out):
    with Mem(nc, "g_") as gm:
        X = gm.sb("X", [P, TILES, D])
        g = {"ident": gm.sb("ident", [P, P]), "identb": gm.sb("identb", [P, P], BF16), "iota": gm.sb("iota", [P, NE]),
             "passed_dve": gm.sem("passed_dve"), "passed_pe": gm.sem("passed_pe")}
        local_attention(nc, dr, X, g)
        ffn_layer0(nc, dr, X, g)
        causal_attention(nc, dr, X, g)
        ffn_layer1(nc, dr, X, g, out)


def kernel(**inputs):
    import concourse.bacc as bacc
    from concourse.bass_utils import run_bass_kernel_spmd

    arrays = host_layout({k: np.asarray(v) for k, v in inputs.items()})
    nc = bacc.Bacc("TRN2", target_bir_lowering=False, num_devices=1)
    dr = {k: nc.dram_tensor(k, v.shape, mybir.dt.from_np(v.dtype), kind="ExternalInput").ap()
          for k, v in arrays.items()}
    out = nc.dram_tensor("out", (BATCH * SEQ, D), F32, kind="ExternalOutput").ap()
    build_program(nc, dr, out)
    r = run_bass_kernel_spmd(nc, [arrays], core_ids=[0])
    return r.results[0]["out"].reshape(BATCH, SEQ, D)
```

```python
import numpy as np
import concourse.bass as bass
import concourse.mybir as mybir
from contextlib import ExitStack

F32 = mybir.dt.float32
F32R = mybir.dt.float32r
BF16 = mybir.dt.bfloat16
U32 = mybir.dt.uint32
ALU = mybir.AluOpType
ACT = mybir.ActivationFunctionType
AXX = mybir.AxisListType.X

P = 128
D = 128
BATCH = 2
SEQ = 2048
TILES = BATCH * SEQ // P
BT = SEQ // P
BLK = 512
BPT = BLK // P
NBLK = BATCH * SEQ // BLK
BB = SEQ // BLK


class Mem:

    def __init__(self, nc, prefix):
        self.nc, self.prefix, self.ctx, self.sems = nc, "m" + prefix, ExitStack(), []

    def __enter__(self):
        self.ctx.__enter__()
        return self

    def __exit__(self, *a):
        if self.sems:
            self.nc.clear_and_free_semaphores(self.sems)
            self.nc.all_engine_barrier()
        return self.ctx.__exit__(*a)

    def sb(self, name, shape, dt=F32):
        return self.ctx.enter_context(self.nc.sbuf_tensor(self.prefix + name, shape, dt))

    def ps(self, name, banks=1, dt=F32, cols=512):
        shape = [P, cols] if banks == 1 else [P, banks, cols]
        return self.ctx.enter_context(self.nc.psum_tensor(self.prefix + name, shape, dt))

    def sem(self, name):
        s = self.nc.alloc_semaphore(self.prefix + name)
        self.sems.append(s)
        return s


def wait_alone(eng, sem, value, passed):
    eng.wait_ge(sem, value)
    eng.sem_inc(passed, 1)


def matmul_split(nc, out, lhs_hi, lhs_lo, rhs_hi, rhs_lo, start=True, stop=True):
    nc.tensor.matmul(out, lhs_hi, rhs_hi, start=start, stop=False)
    nc.tensor.matmul(out, lhs_lo, rhs_hi, start=False, stop=False)
    return nc.tensor.matmul(out, lhs_hi, rhs_lo, start=False, stop=stop)


H0 = 16
DH0 = 64
SEG = 64
PM = 16
PAIRS = H0 // 2
KEYS0 = PM + SEG
SCALE0 = DH0 ** -0.5
SBANKS = 3
PAIRS_OF_BANK = [(0, 1, 2), (3, 4, 5), (6, 7)]
SUB = 256
ST = SUB // P
SSEG = SUB // SEG
NSUB = BATCH * SEQ // SUB
FILL = [("pt", 0), ("pt", 1), ("ot", 0), ("pt", 2), ("pt", 3), ("ot", 1), ("pt", 4)]
FILLS = len(FILL)


def local_attention(nc, dr, X, g):
    m = Mem(nc, "a_")
    with m:
        NQK = 4 * 1024
        wh = m.sb("wh", [P, 5 * 1024], F32R)
        wl = m.sb("wl", [P, 5 * 1024], F32R)
        cs = m.sb("cs", [P, SEQ // SUB, 2, SUB])
        kt = m.sb("kt", [P, 2, PAIRS, SSEG, 2 * KEYS0])
        wout = m.sb("wout", [P, PAIRS, D])
        pmvw = m.sb("pmvw", [P, 2, D])
        bout = m.sb("bout", [P, D])
        mask = m.sb("mask", [P, 3 * 2 * KEYS0], BF16)
        mean = m.sb("mean", [P, TILES, 2])
        xsc = m.sb("xsc", [P, TILES])
        eps = m.sb("eps", [P, TILES])

        with Mem(nc, "a0_") as t:
            raw = t.sb("raw", [P, 3 * 1024])
            rot = t.sb("rot", [P, 2 * 1024])
            nw = t.sb("nw", [P, 1])
            pmvT = t.sb("pmvT", [P, PAIRS, P])
            bst = t.sb("bst", [P, TILES, 6])
            va = t.sb("va", [P, TILES])
            r1 = t.sb("r1", [P, TILES])
            r2 = t.sb("r2", [P, TILES])
            pp = t.ps("pp", 2, cols=512)
            x_in = t.sem("x_in")
            w_in = t.sem("w_in")
            c_in = t.sem("c_in")
            scaled = t.sem("scaled")
            rotated = t.sem("rotated")
            hi_done = t.sem("hi_done")
            lo_done = t.sem("lo_done")
            stat = t.sem("stat")
            powed = t.sem("powed")
            pm_mm = t.sem("pm_mm")
            pm_cp = t.sem("pm_cp")
            with nc.Block() as block:
                @block.sync
                def _(sp):
                    sp.dma_start(raw[:, :], dr["w_qkv"]).then_inc(w_in, 16)
                    sp.dma_start(nw[:, :], dr["norm_w"]).then_inc(w_in, 16)
                    sp.dma_start(X[:, :, :], dr["x"].rearrange("(t p) d -> p t d", p=P)).then_inc(x_in, 16)
                    for dst, src in ((g["ident"][:, :], "ident"), (g["identb"][:, :], "identb"), (mask[:, :], "mask0"),
                                     (cs[:, :, :, :], "cs0"), (pmvT[:, :, :], "pmvT"),
                                     (bout[:, :], "b_out"), (wout[:, :, :], "w_out")):
                        sp.dma_start(dst, dr[src]).then_inc(c_in, 16)
                    for s in range(2 * SSEG):
                        sp.dma_start(kt[:, s // SSEG, :, s % SSEG, :], dr["pmkT"]).then_inc(c_in, 16)
                    sp.wait_ge(c_in, 16 * (7 + 2 * SSEG))

                @block.vector
                def _(dve):
                    nc.vector.memset(eps[:, :], -0.5).then_inc(stat, 1)
                    dve.wait_ge(w_in, 32)
                    nc.vector.tensor_scalar(raw[:, :], raw[:, :], nw[:, 0:1], None, ALU.mult).then_inc(scaled, 1)
                    dve.wait_ge(scaled, 1)
                    pair = raw[:, 0:2048].rearrange("p (n two) -> p n two", two=2)
                    rpair = rot[:, :].rearrange("p (n two) -> p n two", two=2)
                    nc.vector.tensor_scalar(rpair[:, :, 0], pair[:, :, 1], -1.0, None, ALU.mult).then_inc(rotated, 1)
                    nc.vector.tensor_copy(rpair[:, :, 1], pair[:, :, 0]).then_inc(rotated, 1)
                    dve.wait_ge(x_in, 16)
                    for i in range(TILES):
                        nc.vector.bn_stats(bst[:, i, :], X[:, i, :]).then_inc(stat, 1)
                    dve.wait_ge(stat, 1 + TILES)
                    for i in range(TILES):
                        nc.vector.bn_aggr(mean[:, i, :], bst[:, i, :]).then_inc(stat, 1)
                    dve.wait_ge(stat, 1 + 2 * TILES)
                    nc.vector.tensor_scalar(va[:, :], mean[:, :, 1], 1e-5, None, ALU.add).then_inc(stat, 1)
                    srcs = [(raw, 0), (rot, 0), (raw, 1024), (rot, 1024), (raw, 2048)]
                    for k, (src, o) in enumerate(srcs):
                        dve.wait_ge(hi_done, k + 1)
                        nc.vector.tensor_tensor(wl[:, k * 1024:(k + 1) * 1024], src[:, o:o + 1024],
                                                wh[:, k * 1024:(k + 1) * 1024].bitcast(F32),
                                                ALU.subtract).then_inc(lo_done, 1)
                    dve.wait_ge(powed, 1)
                    nc.vector.tensor_tensor(r2[:, :], r1[:, :], r1[:, :], ALU.mult).then_inc(stat, 1)
                    dve.wait_ge(stat, 3 + 2 * TILES)
                    nc.vector.tensor_tensor(va[:, :], r2[:, :], mean[:, :, 1], ALU.mult).then_inc(stat, 1)
                    dve.wait_ge(stat, 4 + 2 * TILES)
                    nc.vector.tensor_scalar(r2[:, :], va[:, :], 1e-6, None, ALU.add).then_inc(stat, 1)
                    dve.wait_ge(powed, 2)
                    nc.vector.tensor_tensor(xsc[:, :], r1[:, :], va[:, :], ALU.mult).then_inc(stat, 1)
                    dve.wait_ge(pm_mm, 1)
                    nc.vector.tensor_copy(pmvw[:, :, :], pp[:, :, 0:D]).then_inc(pm_cp, 1)

                @block.gpsimd
                def _(pool):
                    pool.wait_ge(stat, 2 + 2 * TILES)
                    nc.gpsimd.tensor_tensor(r1[:, :], va[:, :], eps[:, :], ALU.pow).then_inc(powed, 1)
                    pool.wait_ge(stat, 5 + 2 * TILES)
                    nc.gpsimd.tensor_tensor(va[:, :], r2[:, :], eps[:, :], ALU.pow).then_inc(powed, 1)

                @block.scalar
                def _(act):
                    srcs = [(raw, 0, 0), (rot, 0, 2), (raw, 1024, 0), (rot, 1024, 0), (raw, 2048, 0)]
                    for k, (src, o, need) in enumerate(srcs):
                        if k == 0:
                            act.wait_ge(scaled, 1)
                        if need:
                            act.wait_ge(rotated, need)
                        nc.scalar.activation(wh[:, k * 1024:(k + 1) * 1024], src[:, o:o + 1024],
                                             ACT.Copy).then_inc(hi_done, 1)

                @block.tensor
                def _(pe):
                    pe.wait_ge(c_in, 16 * (7 + 2 * SSEG))
                    for half in range(2):
                        for k in range(4):
                            last = nc.tensor.matmul(pp[:, half, 0:D], pmvT[:, 4 * half + k, :],
                                                    wout[:, 4 * half + k, :], start=(k == 0), stop=(k == 3))
                    last.then_inc(pm_mm, 1)

        xn = m.sb("xn", [P, ST, D])
        xth = m.sb("xth", [P, SUB], F32R)
        xtl = m.sb("xtl", [P, SUB], F32R)
        tr = m.sb("tr", [P, 4, 2, SUB])
        qt = m.sb("qt", [P, 2, PAIRS, SUB])
        v = m.sb("v", [P, 2, ST, H0 * DH0])
        e = m.sb("e", [P, ST, H0, KEYS0])
        mx = m.sb("mx", [P, ST, H0])
        den = m.sb("den", [P, ST, H0])
        rden = m.sb("rden", [P, ST, H0])
        pb = m.sb("pb", [P, ST, H0, P])
        ppm = m.sb("ppm", [P, ST, H0 * PM])
        pt = m.sb("pt", [P, H0 + 2, P])
        ot = m.sb("ot", [P, PAIRS, P])
        y = m.sb("y", [P, ST, D])
        yst = m.sb("yst", [P, ST, 6])
        ymv = m.sb("ymv", [P, ST, 2])
        yve = m.sb("yve", [P, ST])
        yr = m.sb("yr", [P, ST])
        pbank = m.ps("pbank", 2)
        sbank = m.ps("sbank", SBANKS)
        fbank = m.ps("fbank", 2)
        misc = m.ps("misc")

        zeroed = m.sem("zeroed")
        xn_ready = m.sem("xn_ready")
        xt_mm = m.sem("xt_mm")
        xth_ready = m.sem("xth_ready")
        xtl_ready = m.sem("xtl_ready")
        proj_mm = m.sem("proj_mm")
        rope_mul = m.sem("rope_mul")
        rope_add = m.sem("rope_add")
        k_high = m.sem("k_high")
        v_mm = m.sem("v_mm")
        v_copied = m.sem("v_copied")
        s_mm = m.sem("s_mm")
        s_max = m.sem("s_max")
        s_sub = m.sem("s_sub")
        exp_done = m.sem("exp_done")
        den_done = m.sem("den_done")
        rden_done = m.sem("rden_done")
        p_norm = m.sem("p_norm")
        p_norm_high = m.sem("p_norm_high")
        fill_mm = m.sem("fill_mm")
        fill_copied = m.sem("fill_copied")
        out_mm = m.sem("out_mm")
        y_read = m.sem("y_read")
        y_chain = m.sem("y_chain")
        y_pow = m.sem("y_pow")
        y_fin = m.sem("y_fin")
        NCT = 2 * PAIRS

        class Sub:

            def __init__(self, j, par):
                self.n, self.par, self.j = j * 2 + par, par, j
                self.tile0 = par * BT + j * ST

        def steps(eng, step):
            step(Sub(0, 0), None, Sub(0, 1))
            step(Sub(0, 1), Sub(0, 0), Sub(1, 0))
            with eng.Fori(1, NSUB // 2 - 1) as j:
                step(Sub(j, 0), Sub(j - 1, 1), Sub(j, 1))
                step(Sub(j, 1), Sub(j, 0), Sub(j + 1, 0))
            last = NSUB // 2 - 1
            step(Sub(last, 0), Sub(last - 1, 1), Sub(last, 1))
            step(Sub(last, 1), Sub(last, 0), None)
            step(None, Sub(last, 1), None)

        with nc.Block() as block:
            @block.vector
            def _(dve):
                nc.vector.memset(pb[:, :, :, :], 0.0).then_inc(zeroed, 1)

                def norm(b):
                    if not (isinstance(b.n, int) and b.n == 0):
                        dve.wait_ge(xt_mm, b.n)
                    for s in range(ST):
                        tile = bass.ds(b.tile0 + s, 1)
                        nc.vector.tensor_scalar(xn[:, s, :], X[:, tile, :], mean[:, tile, 0], xsc[:, tile],
                                                ALU.subtract, ALU.mult).then_inc(xn_ready, 1)

                def low(b):
                    dve.wait_ge(xth_ready, b.n + 1)
                    nc.vector.tensor_tensor(xtl[:, :], misc[:, 0:SUB], xth[:, :].bitcast(F32),
                                            ALU.subtract).then_inc(xtl_ready, 1)

                def high_half(b, ct):
                    if ct < PAIRS:
                        return
                    dve.wait_ge(rope_mul, b.n * NCT + ct + 1)
                    nc.vector.tensor_tensor(
                        kt[64:128, b.par, ct - PAIRS, :, KEYS0 + PM:2 * KEYS0],
                        tr[64:128, ct % 4, 0, :].rearrange("p (a b) -> p a b", b=SEG),
                        tr[64:128, ct % 4, 1, :].rearrange("p (a b) -> p a b", b=SEG), ALU.add).then_inc(k_high, 1)

                def rope(b, ct):
                    dve.wait_ge(proj_mm, b.n * NCT + ct + 1)
                    if ct >= 4 or not isinstance(b.n, int) or b.n > 0:
                        dve.wait_ge(rope_add, b.n * NCT + ct - 3)
                    nc.vector.tensor_tensor(tr[:, ct % 4, :, :], pbank[:, ct % 2, :].rearrange("p (r c) -> p r c", r=2),
                                            cs[:, bass.ds(b.j, 1), :, :].rearrange("p o r c -> p (o r) c"),
                                            ALU.mult).then_inc(rope_mul, 1)
                    high_half(b, ct)

                def tile_max(a, s, b3):
                    h0, nh = 2 * PAIRS_OF_BANK[b3][0], 2 * len(PAIRS_OF_BANK[b3])
                    c = (a.n * ST + s) * 3 + b3 + 1
                    dve.wait_ge(s_mm, c)
                    nc.vector.tensor_reduce(mx[:, s, h0:h0 + nh],
                                            sbank[:, b3, 0:nh * KEYS0].rearrange("p (h k) -> p h k", k=KEYS0),
                                            AXX, ALU.max).then_inc(s_max, 1)

                def tile_sub(a, s, b3):
                    h0, nh = 2 * PAIRS_OF_BANK[b3][0], 2 * len(PAIRS_OF_BANK[b3])
                    dve.wait_ge(s_max, (a.n * ST + s) * 3 + b3 + 1)
                    nc.vector.tensor_tensor(e[:, s, h0:h0 + nh, :],
                                            sbank[:, b3, 0:nh * KEYS0].rearrange("p (h k) -> p h k", k=KEYS0),
                                            mx[:, s, h0:h0 + nh, None].to_broadcast([P, nh, KEYS0]),
                                            ALU.subtract).then_inc(s_sub, 1)

                def softmax_back(a, s):
                    T = a.n * ST + s
                    dve.wait_ge(exp_done, T + 1)
                    nc.vector.tensor_reduce(den[:, s, :], e[:, s, :, :], AXX, ALU.add).then_inc(den_done, 1)
                    dve.wait_ge(den_done, T + 1)
                    nc.vector.reciprocal(rden[:, s, :], den[:, s, :]).then_inc(rden_done, 1)
                    dve.wait_ge(rden_done, T + 1)
                    nc.vector.tensor_tensor(pb[64:128, s, :, SEG:2 * SEG], e[64:128, s, :, PM:KEYS0],
                                            rden[64:128, s, :, None].to_broadcast([64, H0, SEG]),
                                            ALU.mult).then_inc(p_norm_high, 1)

                def out_read(a, s):
                    T = a.n * ST + s
                    dve.wait_ge(out_mm, T + 1)
                    nc.vector.tensor_tensor(y[:, s, :], misc[:, SUB:SUB + D], bout[:, :], ALU.add).then_inc(y_read, 1)
                    dve.wait_ge(y_read, T + 1)
                    nc.vector.bn_stats(yst[:, s, :], y[:, s, :]).then_inc(y_chain, 1)
                    wait_alone(dve, y_chain, T * 3 + 1, g["passed_dve"])
                    nc.vector.bn_aggr(ymv[:, s, :], yst[:, s, :]).then_inc(y_chain, 1)
                    dve.wait_ge(y_chain, T * 3 + 2)
                    nc.vector.tensor_scalar(yve[:, s:s + 1], ymv[:, s, 1:2], 1e-5, None, ALU.add).then_inc(y_chain, 1)

                def finish(a, s):
                    T = a.n * ST + s
                    dve.wait_ge(y_pow, T + 1)
                    nc.vector.tensor_scalar(y[:, s, :], y[:, s, :], ymv[:, s, 0:1], yr[:, s:s + 1],
                                            ALU.subtract, ALU.mult).then_inc(y_fin, 1)
                    dve.wait_ge(y_fin, T * 2 + 1)
                    xs = X[:, bass.ds(a.tile0 + s, 1), :]
                    nc.vector.tensor_tensor(xs, xs, y[:, s, None, :], ALU.add).then_inc(y_fin, 1)

                def step(b, a, nxt):
                    def ropes(*cts):
                        if b:
                            for ct in cts:
                                rope(b, ct)

                    def attend(f, *args):
                        if a:
                            f(a, *args)

                    if b:
                        low(b)
                    for k in range(3):
                        attend(tile_max, 0, k)
                    for k in range(3):
                        attend(tile_sub, 0, k)
                    ropes(0)
                    attend(softmax_back, 0)
                    ropes(1, 2, 3)
                    for k in range(3):
                        attend(tile_max, 1, k)
                    for k in range(3):
                        attend(tile_sub, 1, k)
                    ropes(4, 5, 6)
                    attend(softmax_back, 1)
                    ropes(7, 8, 9, 10)
                    attend(out_read, 0)
                    ropes(11, 12)
                    if nxt:
                        norm(nxt)
                    ropes(13)
                    attend(finish, 0)
                    ropes(14, 15)
                    attend(out_read, 1)
                    attend(finish, 1)

                norm(Sub(0, 0))
                steps(dve, step)

            @block.gpsimd
            def _(pool):
                pool.wait_ge(zeroed, 1)

                def step(b, a, nxt):
                    def adds(*cts):
                        for ct in cts if b else ():
                            pool.wait_ge(rope_mul, b.n * NCT + ct + 1)
                            if ct < PAIRS:
                                nc.gpsimd.tensor_tensor(qt[:, b.par, ct, :], tr[:, ct % 4, 0, :], tr[:, ct % 4, 1, :],
                                                        ALU.add).then_inc(rope_add, 1)
                            else:
                                nc.gpsimd.tensor_tensor(
                                    kt[0:64, b.par, ct - PAIRS, :, PM:KEYS0],
                                    tr[0:64, ct % 4, 0, :].rearrange("p (a b) -> p a b", b=SEG),
                                    tr[0:64, ct % 4, 1, :].rearrange("p (a b) -> p a b", b=SEG),
                                    ALU.add).then_inc(rope_add, 1)

                    def normalise(s):
                        if a:
                            pool.wait_ge(rden_done, a.n * ST + s + 1)
                            nc.gpsimd.tensor_tensor(pb[0:64, s, :, 0:SEG], e[0:64, s, :, PM:KEYS0],
                                                    rden[0:64, s, :, None].to_broadcast([64, H0, SEG]),
                                                    ALU.mult).then_inc(p_norm, 1)
                            nc.gpsimd.tensor_tensor(ppm[:, s, :].rearrange("p (h k) -> p h k", k=PM), e[:, s, :, 0:PM],
                                                    rden[:, s, :, None].to_broadcast([P, H0, PM]),
                                                    ALU.mult).then_inc(p_norm, 1)

                    def power(s):
                        if a:
                            pool.wait_ge(y_chain, (a.n * ST + s + 1) * 3)
                            nc.gpsimd.tensor_tensor(yr[:, s:s + 1], yve[:, s:s + 1], eps[:, 0:1], ALU.pow).then_inc(y_pow, 1)

                    adds(0)
                    normalise(0)
                    adds(*range(1, 7))
                    normalise(1)
                    adds(7, 8, 9, 10)
                    power(0)
                    adds(*range(11, 16))
                    power(1)

                steps(pool, step)

            @block.scalar
            def _(act):
                def high(b):
                    act.wait_ge(xt_mm, b.n + 1)
                    nc.scalar.activation(xth[:, :], misc[:, 0:SUB], ACT.Copy).then_inc(xth_ready, 1)

                def step(b, a, nxt):
                    def exps(s):
                        if a:
                            act.wait_ge(s_sub, (a.n * ST + s + 1) * 3)
                            nc.scalar.activation(e[:, s, :, :], e[:, s, :, :], ACT.Exp, scale=SCALE0).then_inc(exp_done, 1)

                    def evacuate(s, *fills):
                        for i in fills if a else ():
                            F = (a.n * ST + s) * FILLS + i
                            kind, q = FILL[i]
                            act.wait_ge(fill_mm, F + 1)
                            nh = 2 if (kind, q) == ("pt", 4) else 4
                            dst = pt if kind == "pt" else ot
                            nc.scalar.activation(dst[:, 4 * q:4 * q + nh, :],
                                                 fbank[:, (s * FILLS + i) % 2, 0:nh * P].rearrange("p (a b) -> p a b", b=P),
                                                 ACT.Copy).then_inc(fill_copied, 1)

                    def values(*cs):
                        for c in cs if b else ():
                            act.wait_ge(v_mm, b.n * 2 * ST + c + 1)
                            nc.scalar.activation(v[:, b.par, c // 2, (c % 2) * 512:(c % 2) * 512 + 512], pbank[:, c % 2, :],
                                                 ACT.Copy).then_inc(v_copied, 1)

                    values(0, 1, 2, 3)
                    exps(0)
                    evacuate(0, 0, 1)
                    exps(1)
                    evacuate(0, 2, 3, 4, 5, 6)
                    evacuate(1, *range(FILLS))
                    if nxt:
                        high(nxt)

                high(Sub(0, 0))
                steps(act, step)

            @block.tensor
            def _(pe):
                ident, identb = g["ident"], g["identb"]

                def turn(b):
                    for s in range(ST):
                        pe.wait_ge(xn_ready, b.n * ST + s + 1)
                        last = nc.tensor.transpose(misc[:, s * P:(s + 1) * P], xn[:, s, :], ident[:, :])
                    last.then_inc(xt_mm, 1)

                def scores(b, s, b3):
                    T = b.n * ST + s
                    if s > 0 or not isinstance(b.n, int) or b.n > 0:
                        pe.wait_ge(s_sub, (T - 1) * 3 + b3 + 1)
                    if (s, b3) == (0, 0):
                        pe.wait_ge(rope_add, (b.n + 1) * NCT)
                        pe.wait_ge(k_high, (b.n + 1) * PAIRS)
                    prs = PAIRS_OF_BANK[b3]
                    wd = 2 * KEYS0 * len(prs)
                    for hf in range(2):
                        nc.tensor.matmul(sbank[64 * hf:64 * hf + 64, b3, 0:wd], identb[:, 64 * hf:64 * hf + 64],
                                         mask[:, 0:wd], start=True, stop=False, skip_group_check=True)
                    for i, pr in enumerate(prs):
                        for hf in range(2):
                            q0 = s * P + 64 * hf
                            last = nc.tensor.matmul(
                                sbank[64 * hf:64 * hf + 64, b3, i * 160:(i + 1) * 160],
                                qt[:, b.par, pr, q0:q0 + 64], kt[:, b.par, pr, 2 * s + hf, :],
                                start=False, stop=True, skip_group_check=True)
                    last.then_inc(s_mm, 1)

                def step(b, a, nxt):
                    def project(*cts):
                        for ct in cts if b else ():
                            if ct >= 2:
                                pe.wait_ge(rope_mul, b.n * NCT + ct - 1)
                            else:
                                pe.wait_ge(v_copied, b.n * 2 * ST + 3 + ct)
                            for r in range(2):
                                c = (ct // PAIRS) * 2048 + r * 1024 + (ct % PAIRS) * P
                                last = matmul_split(nc, pbank[:, ct % 2, r * SUB:(r + 1) * SUB], wh[:, c:c + P],
                                                    wl[:, c:c + P], xth[:, :], xtl[:, :])
                            last.then_inc(proj_mm, 1)

                    def values_of(*cs):
                        for c in cs if b else ():
                            if c == 0:
                                pe.wait_ge(xth_ready, b.n + 1)
                                pe.wait_ge(xtl_ready, b.n + 1)
                            if c < 2 and a:
                                pe.wait_ge(rope_mul, b.n * NCT - 1 + c)
                            if c >= 2:
                                pe.wait_ge(v_copied, b.n * 2 * ST + c - 1)
                            ts = slice((c // 2) * P, (c // 2 + 1) * P)
                            vc = slice(4096 + (c % 2) * 512, 4096 + (c % 2) * 512 + 512)
                            matmul_split(nc, pbank[:, c % 2, :], xth[:, ts], xtl[:, ts], wh[:, vc],
                                         wl[:, vc]).then_inc(v_mm, 1)

                    def fill(s, i):
                        if not a:
                            return
                        T = a.n * ST + s
                        F = T * FILLS + i
                        kind, q = FILL[i]
                        bank = fbank[:, (s * FILLS + i) % 2, :]
                        if i == 0:
                            pe.wait_ge(p_norm, T * 2 + 2)
                            pe.wait_ge(p_norm_high, T + 1)
                        if s > 0 or i >= 2 or not isinstance(a.n, int) or a.n > 0:
                            pe.wait_ge(fill_copied, F - 1)
                        if kind == "pt":
                            for k in range(4 if q < 4 else 2):
                                src = pb[:, s, 4 * q + k, :] if q < 4 else ppm[:, s, k * P:(k + 1) * P]
                                last = nc.tensor.transpose(bank[:, k * P:(k + 1) * P], src, ident[:, :])
                        else:
                            pe.wait_ge(fill_copied, T * FILLS + FILL.index(("pt", 2 * q + 1)) + 1)
                            if (s, q) == (0, 0):
                                pe.wait_ge(v_copied, (a.n + 1) * 2 * ST)
                            for pr in range(4 * q, 4 * q + 4):
                                for hh in range(2):
                                    h = 2 * pr + hh
                                    last = nc.tensor.matmul(
                                        bank[64 * hh:64 * hh + 64, (pr % 4) * P:(pr % 4 + 1) * P],
                                        v[:, a.par, s, h * DH0:(h + 1) * DH0], pt[:, h, :], start=True, stop=True)
                        last.then_inc(fill_mm, 1)

                    def out_project(s):
                        if not a:
                            return
                        T = a.n * ST + s
                        if s > 0 or not isinstance(a.n, int) or a.n > 0:
                            pe.wait_ge(y_read, T)
                        pe.wait_ge(fill_copied, (T + 1) * FILLS - 1)
                        for pr in range(PAIRS):
                            nc.tensor.matmul(misc[:, SUB:SUB + D], ot[:, pr, :], wout[:, pr, :], start=(pr == 0), stop=False)
                        pe.wait_ge(fill_copied, (T + 1) * FILLS)
                        for i in range(2):
                            last = nc.tensor.matmul(misc[:, SUB:SUB + D], pt[:, H0 + i, :], pmvw[:, i, :], start=False,
                                                    stop=(i == 1))
                        last.then_inc(out_mm, 1)

                    values_of(0, 1, 2, 3)
                    for b3 in range(SBANKS):
                        project(b3)
                        if a:
                            scores(a, 1, b3)
                    project(3, 4, 5)
                    fill(0, 0)
                    fill(0, 1)
                    fill(0, 2)
                    project(6)
                    fill(0, 3)
                    project(7)
                    fill(0, 4)
                    fill(0, 5)
                    project(8)
                    fill(0, 6)
                    out_project(0)
                    project(9, 10, 11)
                    fill(1, 0)
                    fill(1, 1)
                    project(12)
                    fill(1, 2)
                    fill(1, 3)
                    project(13)
                    fill(1, 4)
                    project(14)
                    fill(1, 5)
                    project(15)
                    fill(1, 6)
                    out_project(1)
                    if b:
                        scores(b, 0, 0)
                    if nxt:
                        if a:
                            pe.wait_ge(y_read, (a.n + 1) * ST)
                        turn(nxt)
                    if b:
                        scores(b, 0, 1)
                        scores(b, 0, 2)

                turn(Sub(0, 0))
                steps(pe, step)


class Stats:

    def __init__(self, m, t, g):
        self.passed = g["passed_dve"]
        self.mean = m.sb("mean", [P, TILES, 2])
        self.r = m.sb("r", [P, TILES])
        self.r2 = m.sb("r2", [P, TILES])
        self.rr = m.sb("rr", [P, TILES])
        self.half = m.sb("half", [P, TILES])
        self.bst = t.sb("bst", [P, TILES, 6])
        self.va = t.sb("va", [P, TILES])
        self.vb = t.sb("vb", [P, TILES])
        self.vc = t.sb("vc", [P, TILES])
        self.step = t.sem("stat_step")
        self.powed = t.sem("stat_pow")


def stats_vector(nc, dve, X, S, eps2, mid=None):
    T = TILES
    nc.vector.memset(S.half[:, :], -0.5).then_inc(S.step, 1)
    for i in range(T):
        nc.vector.bn_stats(S.bst[:, i, :], X[:, i, :]).then_inc(S.step, 1)
    dve.wait_ge(S.step, 1 + T)
    for i in range(T):
        nc.vector.bn_aggr(S.mean[:, i, :], S.bst[:, i, :]).then_inc(S.step, 1)
    dve.wait_ge(S.step, 1 + 2 * T)
    nc.vector.tensor_scalar(S.va[:, :], S.mean[:, :, 1], 1e-5, None, ALU.add).then_inc(S.step, 1)
    if mid:
        mid()
    dve.wait_ge(S.powed, 1)
    nc.vector.tensor_tensor(S.vb[:, :], S.r[:, :], S.r[:, :], ALU.mult).then_inc(S.step, 1)
    dve.wait_ge(S.step, 3 + 2 * T)
    nc.vector.tensor_tensor(S.vc[:, :], S.vb[:, :], S.mean[:, :, 1], ALU.mult).then_inc(S.step, 1)
    dve.wait_ge(S.step, 4 + 2 * T)
    nc.vector.tensor_scalar(S.vb[:, :], S.vc[:, :], eps2, None, ALU.add).then_inc(S.step, 1)
    dve.wait_ge(S.powed, 2)
    nc.vector.tensor_tensor(S.rr[:, :], S.r[:, :], S.r2[:, :], ALU.mult).then_inc(S.step, 1)


def stats_pool(nc, pool, S):
    pool.wait_ge(S.step, 2 + 2 * TILES)
    nc.gpsimd.tensor_tensor(S.r[:, :], S.va[:, :], S.half[:, :], ALU.pow).then_inc(S.powed, 1)
    pool.wait_ge(S.step, 5 + 2 * TILES)
    nc.gpsimd.tensor_tensor(S.r2[:, :], S.vb[:, :], S.half[:, :], ALU.pow).then_inc(S.powed, 1)


HB = 4
DK = D // HB
QROWS = 3 * DK
SCALE_B = 1.0 / np.sqrt(np.float32(DK))
KT = SEQ // P
NCH = SEQ // BLK
NE = 8
UNITS = 2 * BB
P1 = 2 * BPT * NCH
RING = 3
GRP = 4


def mqa_attention(nc, dr, X, g, S, wq, wkv, ao):
    m = Mem(nc, "b1_")
    with m:
        xn = m.sb("xn", [P, BPT, D])
        xh = m.sb("xh", [P, SEQ], F32R)
        xl = m.sb("xl", [P, SEQ], F32R)
        ks = m.sb("ks", [QROWS + 2, SEQ], F32R)
        qs = [m.sb(f"qs{w}", [QROWS + 2, 2, BLK], F32R) for w in range(2)]
        vt = m.sb("vt", [P, BLK])
        v1 = m.sb("v1", [P, KT, DK + 1])
        pt = m.sb("pt", [P, RING, 2, BLK])
        mxp = m.sb("mxp", [P, 2 * BPT, NCH])
        negm = m.sb("negm", [P, 2, BPT])
        mt = m.sb("mt", [P, BPT, 2 * DK])
        ots = m.sb("ots", [P, BLK])
        rd = m.sb("rd", [P, BPT, 2])
        p1b = m.ps("p1b", 2)
        stb = m.ps("stb", 4)
        pvb = m.ps("pvb")
        misc = m.ps("misc")

        zeroed = m.sem("zeroed")
        xn_ready = m.sem("xn_ready")
        xt_mm = m.sem("xt_mm")
        xh_ready = m.sem("xh_ready")
        xl_ready = m.sem("xl_ready")
        kv_mm = m.sem("kv_mm")
        k_hi = m.sem("k_hi")
        k_lo = m.sem("k_lo")
        vt_ready = m.sem("vt_ready")
        vt_mm = m.sem("vt_mm")
        v_ready = m.sem("v_ready")
        q_mm = m.sem("q_mm")
        q_hi = m.sem("q_hi")
        q_lo = m.sem("q_lo")
        p1_mm = m.sem("p1_mm")
        p1_max = m.sem("p1_max")
        m_neg = m.sem("m_neg")
        m_split = m.sem("m_split")
        mt_mm = m.sem("mt_mm")
        m_rows = m.sem("m_rows")
        st_mm = m.sem("st_mm")
        exp_done = m.sem("exp_done")
        pv_mm = m.sem("pv_mm")
        pv_evac = m.sem("pv_evac")
        post_mm = m.sem("post_mm")
        rd_done = m.sem("rd_done")
        post_done = m.sem("post_done")

        def pass_bank(r):
            return misc[:, :] if r % 3 == 2 else p1b[:, r % 3, :]

        def schedule(unit, epilogue):
            def run(eng, b):
                unit(b, 0, 0, True, False)
                unit(b, 0, 1, False, False)
                with eng.Fori(1, BB - 1) as n:
                    unit(b, n, 0, False, False)
                    unit(b, n, 1, False, False)
                unit(b, BB - 1, 0, False, False)
                unit(b, BB - 1, 1, False, True)
                epilogue(b)
            return run

        with nc.Block() as block:
            @block.vector
            def _(dve):
                nc.vector.memset(ks[QROWS:QROWS + 2, :].bitcast(F32), 1.0).then_inc(zeroed, 1)
                nc.vector.memset(v1[:, :, DK:DK + 1], 1.0).then_inc(zeroed, 1)
                nc.vector.memset(mt[:, :, :], 0.0).then_inc(zeroed, 1)
                nc.vector.memset(ots[:, :], 0.0).then_inc(zeroed, 1)
                dve.wait_ge(zeroed, 4)

                def load(b, i):
                    n = b * BB + i
                    for s in range(BPT):
                        tile = bass.ds(n * BPT + s, 1)
                        nc.vector.tensor_scalar(xn[:, s, :], X[:, tile, :], S.mean[:, tile, 0], S.rr[:, tile],
                                                ALU.subtract, ALU.mult).then_inc(xn_ready, 1)
                    cols = bass.ds(i * BLK, BLK)
                    dve.wait_ge(xh_ready, n + 1)
                    nc.vector.tensor_tensor(xl[:, cols], p1b[:, 0, :], xh[:, cols].bitcast(F32),
                                            ALU.subtract).then_inc(xl_ready, 1)
                    dve.wait_ge(kv_mm, n + 1)
                    nc.vector.tensor_copy(vt[QROWS:P, :], p1b[QROWS:P, 1, :]).then_inc(vt_ready, 1)
                    dve.wait_ge(k_hi, n + 1)
                    nc.vector.tensor_tensor(ks[DK:2 * DK, cols], p1b[DK:2 * DK, 1, :], ks[DK:2 * DK, cols].bitcast(F32),
                                            ALU.subtract).then_inc(k_lo, 1)
                    dve.wait_ge(vt_mm, n + 1)
                    nc.vector.tensor_copy(v1[:, bass.ds(i * BPT, BPT), 0:DK],
                                          misc[:, 0:BPT * DK].rearrange("p (a b) -> p a b", b=DK)).then_inc(v_ready, 1)

                def q_low(V, w):
                    for hh in range(2):
                        src = misc[2 * DK:3 * DK, :] if hh == 0 else p1b[2 * DK:3 * DK, 0, :]
                        dst = qs[w][2 * DK:3 * DK, hh, :]
                        dve.wait_ge(q_hi, V * 2 + hh + 1)
                        nc.vector.tensor_tensor(dst, src, dst.bitcast(F32), ALU.subtract).then_inc(q_lo, 1)

                def maxima(V, w):
                    for r in range(P1):
                        dve.wait_ge(p1_mm, V * P1 + r + 1)
                        nc.vector.tensor_reduce(mxp[:, r // NCH, r % NCH:r % NCH + 1], pass_bank(r), AXX,
                                                ALU.max).then_inc(p1_max, 1)
                    dve.wait_ge(p1_max, V * P1 + P1)
                    nc.vector.tensor_reduce(negm[:, :, :].rearrange("p h t -> p (h t)"), mxp[:, :, :], AXX, ALU.max,
                                            negate=True).then_inc(m_neg, 1)
                    dve.wait_ge(m_neg, V + 1)
                    nt = negm[:, :, :].rearrange("p h t -> p t h")
                    hi, lo = mt[:, :, 0:2 * DK:DK], mt[:, :, 1:2 * DK:DK]
                    nc.vector.tensor_copy(hi.bitcast(F32R), nt).then_inc(m_split, 1)
                    dve.wait_ge(m_split, V * 2 + 1)
                    nc.vector.tensor_tensor(lo.bitcast(F32R), nt, hi, ALU.subtract).then_inc(m_split, 1)
                    dve.wait_ge(mt_mm, V + 1)
                    for hh in range(2):
                        nc.vector.tensor_copy(qs[w][QROWS:QROWS + 2, hh, :], misc[DK * hh:DK * hh + 2, :]).then_inc(m_rows, 1)

                def evacuate(U):
                    dve.wait_ge(pv_mm, (U + 1) * KT)
                    for hh in range(2):
                        nc.vector.tensor_copy(ots[64 * hh:64 * hh + DK + 1, :], pvb[64 * hh:64 * hh + DK + 1, :])\
                            .then_inc(pv_evac, 1)

                def post(U, b, n, w):
                    dve.wait_ge(post_mm, U + 1)
                    o = misc[:, :].rearrange("p (t h c) -> p t h c", t=BPT, h=2)
                    nc.vector.reciprocal(rd[:, :, :], o[:, :, :, DK]).then_inc(rd_done, 1)
                    dve.wait_ge(rd_done, U + 1)
                    for t in range(BPT):
                        dst = ao[:, bass.ds(b * BT + n * BPT + t, 1), w * 64:w * 64 + 64]
                        nc.vector.tensor_tensor(dst.rearrange("p a (h c) -> p (a h) c", h=2), o[:, t, :, 0:DK],
                                                rd[:, t, :, None].to_broadcast([P, 2, DK]),
                                                ALU.mult).then_inc(post_done, 1)

                def unit(b, n, w, first, last):
                    U = b * UNITS + n * 2 + w
                    if not first:
                        post(U - 1, b, n - 1 + w, 1 - w)
                    if not last:
                        q_low(U + 1, 1 - w)
                        maxima(U + 1, 1 - w)
                    evacuate(U)

                def epilogue(b):
                    post(b * UNITS + UNITS - 1, b, BB - 1, 1)

                run = schedule(unit, epilogue)
                with dve.Fori(0, BATCH) as b:
                    with dve.Fori(0, BB) as i:
                        load(b, i)
                    q_low(b * UNITS, 0)
                    maxima(b * UNITS, 0)
                    run(dve, b)

            @block.scalar
            def _(act):
                def load(b, i):
                    n = b * BB + i
                    cols = bass.ds(i * BLK, BLK)
                    act.wait_ge(xt_mm, n + 1)
                    nc.scalar.activation(xh[:, cols], p1b[:, 0, :], ACT.Copy).then_inc(xh_ready, 1)
                    act.wait_ge(kv_mm, n + 1)
                    act.wait_ge(vt_ready, n + 1)
                    nc.scalar.activation(ks[0:QROWS, cols], p1b[0:QROWS, 1, :], ACT.Copy).then_inc(k_hi, 1)

                def q_high(V, w):
                    for hh in range(2):
                        src = misc[0:QROWS, :] if hh == 0 else p1b[0:QROWS, 0, :]
                        act.wait_ge(q_mm, V * 2 + hh + 1)
                        nc.scalar.activation(qs[w][0:QROWS, hh, :], src, ACT.Copy).then_inc(q_hi, 1)

                def unit(b, n, w, first, last):
                    U = b * UNITS + n * 2 + w
                    for i in range(KT):
                        act.wait_ge(st_mm, U * KT + i + 1)
                        if i >= RING:
                            act.wait_ge(pv_mm, U * KT + i - RING + 1)
                        nc.scalar.activation(pt[:, i % RING, :, :], stb[:, 2 * (i % 2):2 * (i % 2) + 2, :], ACT.Exp,
                                             scale=float(SCALE_B)).then_inc(exp_done, 1)
                        if i == 1 and not last:
                            q_high(U + 1, 1 - w)

                run = schedule(unit, lambda b: None)
                with act.Fori(0, BATCH) as b:
                    with act.Fori(0, BB) as i:
                        load(b, i)
                    q_high(b * UNITS, 0)
                    run(act, b)

            @block.tensor
            def _(pe):
                ident = g["ident"]
                pe.wait_ge(zeroed, 4)

                def load(b, i):
                    n = b * BB + i
                    for s in range(BPT):
                        pe.wait_ge(xn_ready, n * BPT + s + 1)
                        last = nc.tensor.transpose(p1b[:, 0, s * P:(s + 1) * P], xn[:, s, :], ident[:, :])
                    last.then_inc(xt_mm, 1)
                    cols = bass.ds(i * BLK, BLK)
                    pe.wait_ge(xh_ready, n + 1)
                    pe.wait_ge(xl_ready, n + 1)
                    matmul_split(nc, p1b[:, 1, :], wkv[0][:, :], wkv[1][:, :], xh[:, cols], xl[:, cols]).then_inc(kv_mm, 1)
                    pe.wait_ge(k_lo, n + 1)
                    wait_alone(pe, vt_ready, n + 1, g["passed_pe"])
                    for s in range(BPT):
                        last = nc.tensor.transpose(misc[:, s * DK:(s + 1) * DK], vt[QROWS:P, s * P:(s + 1) * P],
                                                   ident[QROWS:P, QROWS:P])
                    last.then_inc(vt_mm, 1)
                    pe.wait_ge(v_ready, n + 1)

                def project(V, n, w):
                    cols = bass.ds(n * BLK, BLK)
                    for hh in range(2):
                        h = 2 * w + hh
                        out = misc[0:QROWS, :] if hh == 0 else p1b[0:QROWS, 0, :]
                        matmul_split(nc, out, wq[0][:, h, :], wq[1][:, h, :], xh[:, cols], xl[:, cols]).then_inc(q_mm, 1)

                def first_pass(V, w, r):
                    if r == 0:
                        pe.wait_ge(q_lo, V * 2 + 2)
                    if r >= 3:
                        pe.wait_ge(p1_max, V * P1 + r - 2)
                    hh, t, c = r // (BPT * NCH), (r // NCH) % BPT, r % NCH
                    nc.tensor.matmul(pass_bank(r), qs[w][0:QROWS, hh, t * P:(t + 1) * P],
                                     ks[0:QROWS, c * BLK:(c + 1) * BLK], start=True, stop=True).then_inc(p1_mm, 1)

                def max_rows(V):
                    wait_alone(pe, m_split, V * 2 + 2, g["passed_pe"])
                    for t in range(BPT):
                        last = nc.tensor.transpose(misc[0:2 * DK, t * P:(t + 1) * P], mt[:, t, :], ident[:, :])
                    last.then_inc(mt_mm, 1)

                def scores(U, w, i):
                    if i == 0:
                        pe.wait_ge(m_rows, U * 2 + 2)
                    if i >= 2:
                        pe.wait_ge(exp_done, U * KT + i - 1)
                    for hh in range(2):
                        last = nc.tensor.matmul(stb[:, 2 * (i % 2) + hh, :], ks[:, i * P:(i + 1) * P], qs[w][:, hh, :],
                                                start=True, stop=True)
                    last.then_inc(st_mm, 1)

                def values(U, i):
                    pe.wait_ge(exp_done, U * KT + i + 1)
                    for hh in range(2):
                        last = nc.tensor.matmul(pvb[64 * hh:64 * hh + DK + 1, :], v1[:, i, :], pt[:, i % RING, hh, :],
                                                start=(i == 0), stop=(i == KT - 1), skip_group_check=True)
                    last.then_inc(pv_mm, 1)

                def post(U):
                    pe.wait_ge(pv_evac, U * 2 + 2)
                    for t in range(BPT):
                        last = nc.tensor.transpose(misc[:, t * P:t * P + P], ots[:, t * P:(t + 1) * P], ident[:, :])
                    last.then_inc(post_mm, 1)

                def unit(b, n, w, first, last):
                    U = b * UNITS + n * 2 + w
                    scores(U, w, 0)
                    passes = iter(range(0 if last else P1))

                    def next_pass(i):
                        r = next(passes, None) if i >= 2 else None
                        if r is not None:
                            first_pass(U + 1, 1 - w, r)

                    for i in range(KT):
                        next_pass(i)
                        if i + 1 < KT:
                            scores(U, w, i + 1)
                        next_pass(i)
                        if i == 0 and not first:
                            post(U - 1)
                        if i == 1 and not last:
                            if not first:
                                pe.wait_ge(post_done, U * BPT)
                            project(U + 1, n + w, 1 - w)
                        if i == KT - 1 and not last:
                            max_rows(U + 1)
                        values(U, i)
                        next_pass(i)

                def epilogue(b):
                    post(b * UNITS + UNITS - 1)
                    pe.wait_ge(post_done, (b + 1) * UNITS * BPT)

                run = schedule(unit, epilogue)
                with pe.Fori(0, BATCH) as b:
                    with pe.Fori(0, BB) as i:
                        load(b, i)
                    project(b * UNITS, 0, 0)
                    for r in range(P1):
                        first_pass(b * UNITS, 0, r)
                    max_rows(b * UNITS)
                    run(pe, b)


def ffn_mixture(nc, dr, X, g, S, w, ao):
    m = Mem(nc, "b2_")
    with m:
        w1, w2, wr, wo, ebias = w["w13"], w["w2"], w["wr"], w["wo"], w["ebias"]
        x2 = m.sb("x2", [P, TILES, D])
        nh = m.sb("nh", [P, TILES * P], F32R)
        nl = m.sb("nl", [P, TILES * P], F32R)
        lg = m.sb("lg", [P, TILES, NE])
        gate = m.sb("gate", [P, TILES, NE])
        with Mem(nc, "b2a_") as t:
            aos = t.sb("aos", [P, GRP, BPT, D])
            aot = t.sb("aot", [P, GRP, BLK])
            h = t.sb("h", [P, GRP, BPT, D])
            sq = t.sb("sq", [P, GRP, BPT, D])
            ss = t.sb("ss", [P, GRP, BPT])
            sv = t.sb("sv", [P, GRP, BPT])
            r2 = t.sb("r2", [P, GRP, BPT])
            xn = t.sb("xn", [P, GRP, BPT, D])
            lt = t.sb("lt", [32, GRP, BLK])
            bk = t.ps("bk", 2 * GRP)
            copied = t.sem("copied")
            at_mm = t.sem("at_mm")
            at_ready = t.sem("at_ready")
            o_mm = t.sem("o_mm")
            ln = t.sem("ln")
            x2_done = t.sem("x2_done")
            sq_done = t.sem("sq_done")
            sum_done = t.sem("sum_done")
            var_done = t.sem("var_done")
            powed = t.sem("powed")
            xn_done = t.sem("xn_done")
            xt_mm = t.sem("xt_mm")
            xh_done = t.sem("xh_done")
            xl_done = t.sem("xl_done")
            l_mm = t.sem("l_mm")
            l_copied = t.sem("l_copied")
            lt_mm = t.sem("lt_mm")
            l_done = t.sem("l_done")
            group = range(GRP)
            with nc.Block() as block:
                @block.scalar
                def _(act):
                    with act.Fori(0, NBLK // GRP) as gi:
                        n = gi * GRP
                        for i in group:
                            nc.scalar.activation(aos[:, i, :, :], ao[:, bass.ds((n + i) * BPT, BPT), :],
                                                 ACT.Copy).then_inc(copied, 1)
                        for i in group:
                            act.wait_ge(at_mm, n + i + 1)
                            nc.scalar.activation(aot[:, i, :], bk[:, 2 * i, :], ACT.Copy).then_inc(at_ready, 1)
                        for i in group:
                            act.wait_ge(xt_mm, n + i + 1)
                            nc.scalar.activation(nh[:, bass.ds((n + i) * BLK, BLK)], bk[:, 2 * i, :],
                                                 ACT.Copy).then_inc(xh_done, 1)
                        for i in group:
                            act.wait_ge(l_mm, n + i + 1)
                            nc.scalar.activation(lt[:, i, :], bk[0:32, 2 * i + 1, :], ACT.Copy).then_inc(l_copied, 1)

                @block.gpsimd
                def _(pool):
                    with pool.Fori(0, NBLK // GRP) as gi:
                        pool.wait_ge(var_done, gi * GRP + GRP)
                        nc.gpsimd.tensor_tensor(r2[:, :, :], sv[:, :, :],
                                                S.half[:, 0:GRP * BPT].rearrange("p (a b) -> p a b", b=BPT),
                                                ALU.pow).then_inc(powed, 1)

                @block.vector
                def _(dve):
                    with dve.Fori(0, NBLK // GRP) as gi:
                        n = gi * GRP
                        for i in group:
                            for s in range(BPT):
                                tile = bass.ds((n + i) * BPT + s, 1)
                                nc.vector.tensor_scalar(h[:, i, s, :], X[:, tile, :], S.mean[:, tile, 0], S.r[:, tile],
                                                        ALU.subtract, ALU.mult).then_inc(ln, 1)
                        for i in group:
                            blk = bass.ds((n + i) * BPT, BPT)
                            dve.wait_ge(o_mm, n + i + 1)
                            dve.wait_ge(ln, (n + i + 1) * BPT)
                            nc.vector.tensor_tensor(x2[:, blk, :], bk[:, 2 * i + 1, :].rearrange("p (a b) -> p a b", b=D),
                                                    h[:, i, :, :], ALU.add).then_inc(x2_done, 1)
                        for i in group:
                            blk = bass.ds((n + i) * BPT, BPT)
                            dve.wait_ge(x2_done, n + i + 1)
                            nc.vector.tensor_tensor(sq[:, i, :, :], x2[:, blk, :], x2[:, blk, :], ALU.mult)\
                                .then_inc(sq_done, 1)
                        for i in group:
                            dve.wait_ge(sq_done, n + i + 1)
                            nc.vector.tensor_reduce(ss[:, i, :], sq[:, i, :, :], AXX, ALU.add).then_inc(sum_done, 1)
                        for i in group:
                            dve.wait_ge(sum_done, n + i + 1)
                            nc.vector.tensor_scalar(sv[:, i, :], ss[:, i, :], 1.0 / D, 1e-6, ALU.mult,
                                                    ALU.add).then_inc(var_done, 1)
                        dve.wait_ge(powed, gi + 1)
                        for i in group:
                            nc.vector.tensor_tensor(xn[:, i, :, :], x2[:, bass.ds((n + i) * BPT, BPT), :],
                                                    r2[:, i, :, None].to_broadcast([P, BPT, D]),
                                                    ALU.mult).then_inc(xn_done, 1)
                        for i in group:
                            cols = bass.ds((n + i) * BLK, BLK)
                            dve.wait_ge(xh_done, n + i + 1)
                            nc.vector.tensor_tensor(nl[:, cols], bk[:, 2 * i, :], nh[:, cols].bitcast(F32),
                                                    ALU.subtract).then_inc(xl_done, 1)
                        for i in group:
                            dve.wait_ge(lt_mm, n + i + 1)
                            nc.vector.tensor_tensor(lg[:, bass.ds((n + i) * BPT, BPT), :],
                                                    bk[:, 2 * i, 0:BPT * 32].rearrange("p (a b) -> p a b", b=32)[:, :, 0:NE],
                                                    ebias[:, None, :].to_broadcast([P, BPT, NE]), ALU.add).then_inc(l_done, 1)

                @block.tensor
                def _(pe):
                    ident = g["ident"]
                    with pe.Fori(0, NBLK // GRP) as gi:
                        n = gi * GRP
                        for i in group:
                            pe.wait_ge(copied, n + i + 1)
                            for s in range(BPT):
                                last = nc.tensor.transpose(bk[:, 2 * i, s * P:(s + 1) * P], aos[:, i, s, :], ident[:, :])
                            last.then_inc(at_mm, 1)
                        for i in group:
                            pe.wait_ge(at_ready, n + i + 1)
                            for s in range(BPT):
                                last = nc.tensor.matmul(bk[:, 2 * i + 1, s * P:(s + 1) * P], aot[:, i, s * P:(s + 1) * P],
                                                        wo[:, :], start=True, stop=True)
                            last.then_inc(o_mm, 1)
                        for i in group:
                            pe.wait_ge(xn_done, n + i + 1)
                            for s in range(BPT):
                                last = nc.tensor.transpose(bk[:, 2 * i, s * P:(s + 1) * P], xn[:, i, s, :], ident[:, :])
                            last.then_inc(xt_mm, 1)
                        for i in group:
                            cols = bass.ds((n + i) * BLK, BLK)
                            pe.wait_ge(xh_done, n + i + 1)
                            pe.wait_ge(xl_done, n + i + 1)
                            matmul_split(nc, bk[:, 2 * i + 1, :], wr[0][:, :], wr[1][:, :], nh[:, cols],
                                         nl[:, cols]).then_inc(l_mm, 1)
                        for i in group:
                            wait_alone(pe, l_copied, n + i + 1, g["passed_pe"])
                            for s in range(BPT):
                                last = nc.tensor.transpose(bk[:, 2 * i, s * 32:(s + 1) * 32], lt[:, i, s * P:(s + 1) * P],
                                                           ident[0:32, 0:32])
                            last.then_inc(lt_mm, 1)
                        pe.wait_ge(l_done, n + GRP)

        router(nc, g, lg, gate, softmax_first=True, prefix="b2b_")

        s1 = m.sb("s1", [P, 2, BLK])
        hh = m.sb("hh", [P, 2, BLK])
        acc = m.sb("acc", [P, BPT, D])
        F = FinishNorm(m)
        ub = m.ps("ub", 4)
        db = m.ps("db", 2)
        up_mm = m.sem("up_mm")
        silu = m.sem("silu")
        h_done = m.sem("h_done")
        down_mm = m.sem("down_mm")
        acc_done = m.sem("acc_done")
        NX = NE + 1
        order = [NE] + list(range(NE))
        with nc.Block() as block:
            @block.scalar
            def _(act):
                with act.Fori(0, NBLK) as n:
                    for i in range(NX):
                        act.wait_ge(up_mm, (n * NX + i) * 2 + 1)
                        if i >= 2:
                            act.wait_ge(h_done, n * NX + i - 1)
                        nc.scalar.activation(s1[:, i % 2, :], ub[:, 2 * (i % 2), :], ACT.Silu).then_inc(silu, 1)

            @block.gpsimd
            def _(pool):
                with pool.Fori(0, NBLK) as n:
                    F.pool(nc, pool, n, S)

            @block.vector
            def _(dve):
                with dve.Fori(0, NBLK) as n:
                    def accumulate(i):
                        e = order[i]
                        dve.wait_ge(down_mm, n * NX + i + 1)
                        for s in range(BPT):
                            tile = bass.ds(n * BPT + s, 1)
                            src = db[:, i % 2, s * P:(s + 1) * P]
                            if i == 0:
                                nc.vector.tensor_tensor(acc[:, s, None, :], db[:, 0, None, s * P:(s + 1) * P],
                                                        x2[:, tile, :], ALU.add).then_inc(acc_done, 1)
                            else:
                                dve.wait_ge(acc_done, (n * NX + i) * BPT)
                                nc.vector.scalar_tensor_tensor(acc[:, s, :], src, gate[:, tile, e], acc[:, s, :],
                                                               ALU.mult, ALU.add).then_inc(acc_done, 1)

                    for i in range(NX):
                        dve.wait_ge(up_mm, (n * NX + i) * 2 + 2)
                        dve.wait_ge(silu, n * NX + i + 1)
                        if i >= 2:
                            dve.wait_ge(down_mm, n * NX + i - 1)
                        nc.vector.tensor_tensor(hh[:, i % 2, :], s1[:, i % 2, :], ub[:, 2 * (i % 2) + 1, :],
                                                ALU.mult).then_inc(h_done, 1)
                        if i >= 1:
                            accumulate(i - 1)
                    accumulate(NX - 1)
                    dve.wait_ge(acc_done, (n * NX + NX) * BPT)
                    F.vector(nc, dve, n, acc, X, S)

            @block.tensor
            def _(pe):
                with pe.Fori(0, NBLK) as n:
                    cols = bass.ds(n * BLK, BLK)

                    def up(i):
                        e = order[i]
                        if i >= 2:
                            pe.wait_ge(h_done, n * NX + i - 1)
                        for k in range(2):
                            matmul_split(nc, ub[:, 2 * (i % 2) + k, :], w1[0][:, k, e, :], w1[1][:, k, e, :],
                                         nh[:, cols], nl[:, cols]).then_inc(up_mm, 1)

                    def down(i):
                        pe.wait_ge(h_done, n * NX + i + 1)
                        if i >= 2:
                            pe.wait_ge(acc_done, (n * NX + i - 1) * BPT)
                        for s in range(BPT):
                            last = nc.tensor.matmul(db[:, i % 2, s * P:(s + 1) * P], hh[:, i % 2, s * P:(s + 1) * P],
                                                    w2[:, order[i], :], start=True, stop=True)
                        last.then_inc(down_mm, 1)

                    up(0)
                    for i in range(NX):
                        if i + 1 < NX:
                            up(i + 1)
                        down(i)
                    pe.wait_ge(acc_done, (n * NX + NX) * BPT)


class FinishNorm:

    def __init__(self, m):
        self.st = m.sb("fst", [P, BPT, 6])
        self.mv = m.sb("fmv", [P, BPT, 2])
        self.ve = m.sb("fve", [P, BPT])
        self.rs = m.sb("frs", [P, BPT])
        self.step = m.sem("fstep")
        self.powed = m.sem("fpowed")
        self.N = 2 * BPT + 1 + 2 * BPT

    def vector(self, nc, dve, n, acc, X, S):
        o = n * self.N
        for s in range(BPT):
            nc.vector.bn_stats(self.st[:, s, :], acc[:, s, :]).then_inc(self.step, 1)
        for s in range(BPT):
            wait_alone(dve, self.step, o + s + 1, S.passed)
            nc.vector.bn_aggr(self.mv[:, s, :], self.st[:, s, :]).then_inc(self.step, 1)
        dve.wait_ge(self.step, o + 2 * BPT)
        nc.vector.tensor_scalar(self.ve[:, :], self.mv[:, :, 1], 1e-5, None, ALU.add).then_inc(self.step, 1)
        dve.wait_ge(self.powed, n + 1)
        for s in range(BPT):
            nc.vector.tensor_scalar(acc[:, s, :], acc[:, s, :], self.mv[:, s, 0:1], self.rs[:, s:s + 1],
                                    ALU.subtract, ALU.mult).then_inc(self.step, 1)
        for s in range(BPT):
            dve.wait_ge(self.step, o + 2 * BPT + 2 + s)
            xs = X[:, bass.ds(n * BPT + s, 1), :]
            nc.vector.tensor_tensor(xs, xs, acc[:, s, None, :], ALU.add).then_inc(self.step, 1)
        dve.wait_ge(self.step, o + self.N)

    def pool(self, nc, pool, n, S):
        pool.wait_ge(self.step, n * self.N + 2 * BPT + 1)
        nc.gpsimd.tensor_tensor(self.rs[:, :], self.ve[:, :], S.half[:, 0:BPT], ALU.pow).then_inc(self.powed, 1)


def router(nc, g, lg, gate, softmax_first, prefix):
    T = TILES
    with Mem(nc, prefix) as t:
        pr = t.sb("pr", [P, T, NE])
        mx = t.sb("mx", [P, T])
        top = t.sb("top", [P, T, 8])
        idx = t.sb("idx", [P, T, 8], U32)
        idf = t.sb("idf", [P, T, 2])
        df = t.sb("df", [P, T])
        ex = t.sb("ex", [P, T])
        wt = t.sb("wt", [P, 2, T])
        oh = t.sb("oh", [P, T, NE])
        step = t.sem("step")
        exps = t.sem("exps")
        iota = g["iota"]
        with nc.Block() as block:
            @block.scalar
            def _(act):
                k = 0
                if softmax_first:
                    act.wait_ge(step, 2)
                    nc.scalar.activation(pr[:, :, :], pr[:, :, :], ACT.Exp).then_inc(exps, 1)
                    k = 3
                act.wait_ge(step, 2 + k + 2 * T - (0 if softmax_first else 1))
                nc.scalar.activation(ex[:, :], df[:, :], ACT.Exp).then_inc(exps, 1)

            @block.vector
            def _(dve):
                c = 0

                def bc(x):
                    return x.to_broadcast([P, T, NE])

                if softmax_first:
                    nc.vector.tensor_reduce(mx[:, :], lg[:, :, :], AXX, ALU.max).then_inc(step, 1)
                    dve.wait_ge(step, 1)
                    nc.vector.tensor_tensor(pr[:, :, :], lg[:, :, :], bc(mx[:, :, None]), ALU.subtract).then_inc(step, 1)
                    dve.wait_ge(exps, 1)
                    nc.vector.tensor_reduce(mx[:, :], pr[:, :, :], AXX, ALU.add).then_inc(step, 1)
                    dve.wait_ge(step, 3)
                    nc.vector.reciprocal(df[:, :], mx[:, :]).then_inc(step, 1)
                    dve.wait_ge(step, 4)
                    nc.vector.tensor_tensor(lg[:, :, :], pr[:, :, :], bc(df[:, :, None]), ALU.mult).then_inc(step, 1)
                    c = 5
                    dve.wait_ge(step, c)
                for i in range(T):
                    nc.vector.max(top[:, i, :], lg[:, i, :]).then_inc(step, 1)
                dve.wait_ge(step, c + T)
                nc.vector.tensor_tensor(df[:, :], top[:, :, 1], top[:, :, 0], ALU.subtract).then_inc(step, 1)
                for i in range(T):
                    nc.vector.max_index(idx[:, i, :], top[:, i, :], lg[:, i, :]).then_inc(step, 1)
                dve.wait_ge(step, c + 2 * T + 1)
                nc.vector.tensor_copy(idf[:, :, :], idx[:, :, 0:2]).then_inc(step, 1)
                dve.wait_ge(exps, 2 if softmax_first else 1)
                nc.vector.tensor_scalar(mx[:, :], ex[:, :], 1.0, None, ALU.add).then_inc(step, 1)
                dve.wait_ge(step, c + 2 * T + 3)
                nc.vector.reciprocal(wt[:, 0, :], mx[:, :]).then_inc(step, 1)
                dve.wait_ge(step, c + 2 * T + 4)
                nc.vector.tensor_tensor(wt[:, 1, :], ex[:, :], wt[:, 0, :], ALU.mult).then_inc(step, 1)
                for k, dst in ((0, gate), (1, oh)):
                    nc.vector.tensor_tensor(dst[:, :, :], iota[:, None, :].to_broadcast([P, T, NE]),
                                            bc(idf[:, :, k:k + 1]), ALU.is_equal).then_inc(step, 1)
                    dve.wait_ge(step, c + 2 * T + 6 + 2 * k)
                    nc.vector.tensor_tensor(dst[:, :, :], dst[:, :, :], bc(wt[:, k, :, None]), ALU.mult).then_inc(step, 1)
                dve.wait_ge(step, c + 2 * T + 9)
                nc.vector.tensor_tensor(gate[:, :, :], gate[:, :, :], oh[:, :, :], ALU.add).then_inc(step, 1)


def ffn_layer0(nc, dr, X, g):
    with Mem(nc, "b_") as m:
        ao = m.sb("ao", [P, TILES, D])
        wq = [m.sb(f"wq{k}", [P, HB, QROWS], F32R) for k in range(2)]
        wkv = [m.sb(f"wkv{k}", [P, P], F32R) for k in range(2)]
        w = {"w13": [m.sb(f"w13{k}", [P, 2, NE + 1, D], F32R) for k in range(2)],
             "wr": [m.sb(f"wr{k}", [P, P], F32R) for k in range(2)],
             "w2": m.sb("w2", [P, NE + 1, D]), "wo": m.sb("wo", [P, D]), "ebias": m.sb("ebias", [P, NE])}
        with Mem(nc, "b0_") as t:
            S = Stats(m, t, g)
            rq = t.sb("rq", [P, HB * QROWS])
            rkv = t.sb("rkv", [P, P])
            rr = t.sb("rr", [P, P])
            r13 = t.sb("r13", [P, 2 * (NE + 1) * D])
            g12 = t.sb("g12", [P, 2])
            w_in = t.sem("w_in")
            scaled = t.sem("scaled")
            hi = t.sem("hi")
            lo = t.sem("lo")
            sets = [(rq, wq, "p h q -> p (h q)", 0), (rkv, wkv, None, 0), (rr, w["wr"], None, 1),
                    (r13, w["w13"], "p k e f -> p (k e f)", 1)]

            def flat(x, pat):
                a = x[:, :] if pat is None else x[tuple([slice(None)] * len(x.shape))].rearrange(pat)
                return a

            with nc.Block() as block:
                @block.sync
                def _(sp):
                    for dst, src in ((rq[:, :], "b_wq"), (rkv[:, :], "b_wkv"), (rr[:, :], "b_wr"), (r13[:, :], "b_w13"),
                                     (g12[:, :], "b_g12"), (w["w2"][:, :, :], "b_w2"), (w["wo"][:, :], "b_wo"),
                                     (w["ebias"][:, :], "b_ebias"), (g["iota"][:, :], "iota")):
                        sp.dma_start(dst, dr[src]).then_inc(w_in, 16)
                    sp.wait_ge(w_in, 16 * 9)

                @block.vector
                def _(dve):
                    def weights():
                        dve.wait_ge(w_in, 16 * 9)
                        for raw, _, _, gi in sets:
                            nc.vector.tensor_scalar(raw[:, :], raw[:, :], g12[:, gi:gi + 1], None,
                                                    ALU.mult).then_inc(scaled, 1)
                        for k, (raw, dst, pat, _) in enumerate(sets):
                            dve.wait_ge(hi, k + 1)
                            nc.vector.tensor_tensor(flat(dst[1], pat), raw[:, :], flat(dst[0], pat).bitcast(F32),
                                                    ALU.subtract).then_inc(lo, 1)
                    stats_vector(nc, dve, X, S, 1e-6, weights)

                @block.gpsimd
                def _(pool):
                    stats_pool(nc, pool, S)

                @block.scalar
                def _(act):
                    for k, (raw, dst, pat, _) in enumerate(sets):
                        act.wait_ge(scaled, k + 1)
                        nc.scalar.activation(flat(dst[0], pat), raw[:, :], ACT.Copy).then_inc(hi, 1)
        mqa_attention(nc, dr, X, g, S, wq, wkv, ao)
        ffn_mixture(nc, dr, X, g, S, w, ao)


HC = 2
SCALE_C = float(D) ** -0.5


def causal_attention(nc, dr, X, g):
    with Mem(nc, "c_") as m:
        NW = 2 * (1 + HC)
        wh = m.sb("wh", [P, NW, D], F32R)
        wl = m.sb("wl", [P, NW, D], F32R)
        wv = m.sb("wv", [P, D])
        wo = m.sb("wo", [P, HC, D])
        mask = m.sb("mask", [P, P], BF16)
        cosT = m.sb("cosT", [P, SEQ])
        sinT = m.sb("sinT", [P, SEQ])
        with Mem(nc, "c0_") as t:
            S = Stats(m, t, g)
            raw = t.sb("raw", [P, NW, D])
            w_in = t.sem("w_in")
            c_in = t.sem("c_in")
            rot = t.sem("rot")
            hi = t.sem("hi")
            lo = t.sem("lo")
            with nc.Block() as block:
                @block.sync
                def _(sp):
                    sp.dma_start(raw[:, 0::2, :], dr["c_wkq"]).then_inc(w_in, 16)
                    for dst, src in ((wv[:, :], "c_wv"), (wo[:, :, :], "c_wo"), (mask[:, :], "mask1"),
                                     (cosT[:, :], "cos1"), (sinT[:, :], "sin1")):
                        sp.dma_start(dst, dr[src]).then_inc(c_in, 16)
                    sp.wait_ge(c_in, 16 * 5)

                @block.vector
                def _(dve):
                    def weights():
                        dve.wait_ge(w_in, 16)
                        for k in range(0, NW, 2):
                            src = raw[:, k, :].rearrange("p (n two) -> p n two", two=2)
                            dst = raw[:, k + 1, :].rearrange("p (n two) -> p n two", two=2)
                            nc.vector.tensor_scalar(dst[:, :, 0], src[:, :, 1], -1.0, None, ALU.mult).then_inc(rot, 1)
                            nc.vector.tensor_copy(dst[:, :, 1], src[:, :, 0]).then_inc(rot, 1)
                        dve.wait_ge(hi, 1)
                        nc.vector.tensor_tensor(wl[:, :, :], raw[:, :, :], wh[:, :, :].bitcast(F32),
                                                ALU.subtract).then_inc(lo, 1)
                    stats_vector(nc, dve, X, S, 1e-5, weights)

                @block.gpsimd
                def _(pool):
                    stats_pool(nc, pool, S)

                @block.scalar
                def _(act):
                    act.wait_ge(rot, NW)
                    nc.scalar.activation(wh[:, :, :], raw[:, :, :], ACT.Copy).then_inc(hi, 1)

        xn = m.sb("xn", [P, BPT, D])
        x32 = m.sb("x32", [P, BLK])
        xh = m.sb("xh", [P, BLK], F32R)
        xl = m.sb("xl", [P, BLK], F32R)
        t1 = m.sb("t1", [P, 2, BLK])
        t2 = m.sb("t2", [P, 2, BLK])
        rp = m.sb("rp", [P, 2, BLK])
        kqh = m.sb("kqh", [P, 1 + HC, SEQ], F32R)
        kql = m.sb("kql", [P, 1 + HC, SEQ], F32R)
        v = m.sb("v", [P, KT, D])
        p = m.sb("p", [P, 2, SEQ])
        pt = m.sb("pt", [P, 2, BLK])
        mp = m.sb("mp", [P, 2, NCH])
        mm = m.sb("mm", [P, 2])
        nb = m.sb("nb", [P, 2])
        ps = m.sb("ps", [P, 2, NCH])
        den = m.sb("den", [P, 2])
        rden = m.sb("rden", [P, 2])
        o = m.sb("o", [P, HC, D])
        ot = m.sb("ot", [P, HC * P])
        acc = m.sb("acc", [P, BPT, D])
        F = FinishNorm(m)
        sb4 = m.ps("sb4", 4)
        tb = m.ps("tb", 2)
        pv = m.ps("pv")
        misc = m.ps("misc")

        xn_ready = m.sem("xn_ready")
        xt_mm = m.sem("xt_mm")
        x_copied = m.sem("x_copied")
        xl_ready = m.sem("xl_ready")
        v_mm = m.sem("v_mm")
        v_copied = m.sem("v_copied")
        proj_mm = m.sem("proj_mm")
        rope_mul = m.sem("rope_mul")
        rope_add = m.sem("rope_add")
        rope_hi = m.sem("rope_hi")
        rope_lo = m.sem("rope_lo")
        s_mm = m.sem("s_mm")
        s_max = m.sem("s_max")
        bias_step = m.sem("bias_step")
        exp_done = m.sem("exp_done")
        pt_mm = m.sem("pt_mm")
        pt_copied = m.sem("pt_copied")
        pv_mm = m.sem("pv_mm")
        den_step = m.sem("den_step")
        o_ready = m.sem("o_ready")
        ot_mm = m.sem("ot_mm")
        ot_copied = m.sem("ot_copied")
        out_mm = m.sem("out_mm")
        y_copied = m.sem("y_copied")

        units = [(qt, h) for qt in range(KT) for h in range(HC)]
        NU = len(units)
        chunks = [(qt + BPT) // BPT for qt, _ in units]
        first = [sum(chunks[:u]) for u in range(NU + 1)]
        NC = first[NU]
        R = 1 + HC

        def tiles_of(u, c):
            return min(BPT, units[u][0] + 1 - c * BPT)

        with nc.Block() as block:
            @block.vector
            def _(dve):
                def load(b, i):
                    n = b * BB + i
                    for s in range(BPT):
                        tile = bass.ds(n * BPT + s, 1)
                        nc.vector.tensor_scalar(xn[:, s, :], X[:, tile, :], S.mean[:, tile, 0], S.r[:, tile],
                                                ALU.subtract, ALU.mult).then_inc(xn_ready, 1)
                    dve.wait_ge(x_copied, n * 2 + 2)
                    nc.vector.tensor_tensor(xl[:, :], misc[:, :], xh[:, :].bitcast(F32), ALU.subtract).then_inc(xl_ready, 1)
                    cols = bass.ds(i * BLK, BLK)
                    for k in range(R):
                        dve.wait_ge(proj_mm, n * R + k + 1)
                        if k == 2:
                            dve.wait_ge(rope_add, n * R + 1)
                        nc.vector.tensor_tensor(t1[:, k % 2, :], sb4[:, 2 * (k % 2), :], cosT[:, cols],
                                                ALU.mult).then_inc(rope_mul, 1)
                        nc.vector.tensor_tensor(t2[:, k % 2, :], sb4[:, 2 * (k % 2) + 1, :], sinT[:, cols],
                                                ALU.mult).then_inc(rope_mul, 1)
                    for k in range(R):
                        dve.wait_ge(rope_hi, n * R + k + 1)
                        nc.vector.tensor_tensor(kql[:, k, cols], rp[:, k % 2, :], kqh[:, k, cols].bitcast(F32),
                                                ALU.subtract).then_inc(rope_lo, 1)

                def chunk_max(b, u, c):
                    G = b * NC + first[u] + c
                    dve.wait_ge(s_mm, G + 1)
                    nc.vector.tensor_reduce(mp[:, u % 2, c:c + 1], sb4[:, (first[u] + c) % 4, 0:tiles_of(u, c) * P],
                                            AXX, ALU.max).then_inc(s_max, 1)

                def bias(b, u):
                    U = b * NU + u
                    dve.wait_ge(s_max, b * NC + first[u + 1])
                    nc.vector.tensor_reduce(mm[:, u % 2:u % 2 + 1], mp[:, u % 2, 0:chunks[u]], AXX,
                                            ALU.max).then_inc(bias_step, 1)
                    dve.wait_ge(bias_step, U * 2 + 1)
                    nc.vector.tensor_scalar(nb[:, u % 2:u % 2 + 1], mm[:, u % 2:u % 2 + 1], -SCALE_C, None,
                                            ALU.mult).then_inc(bias_step, 1)

                def output(b, u):
                    U = b * NU + u
                    w = u % 2
                    dve.wait_ge(exp_done, b * NC + first[u + 1])
                    nc.vector.tensor_reduce(den[:, w:w + 1], ps[:, w, 0:chunks[u]], AXX, ALU.add).then_inc(den_step, 1)
                    dve.wait_ge(den_step, U * 2 + 1)
                    nc.vector.reciprocal(rden[:, w:w + 1], den[:, w:w + 1]).then_inc(den_step, 1)
                    dve.wait_ge(den_step, U * 2 + 2)
                    dve.wait_ge(pv_mm, b * NC + first[u + 1])
                    nc.vector.tensor_scalar(o[:, w, :], pv[:, 0:D], rden[:, w:w + 1], None, ALU.mult).then_inc(o_ready, 1)

                def row_done(b, qt):
                    dve.wait_ge(out_mm, b * KT + qt + 1)
                    nc.vector.tensor_copy(acc[:, qt % BPT, :], misc[:, 2 * P:3 * P]).then_inc(y_copied, 1)
                    if qt % BPT == BPT - 1:
                        dve.wait_ge(y_copied, b * KT + qt + 1)
                        F.vector(nc, dve, b * BB + qt // BPT, acc, X, S)

                with dve.Fori(0, BATCH) as b:
                    with dve.Fori(0, BB) as i:
                        load(b, i)
                    for c in range(chunks[0]):
                        chunk_max(b, 0, c)
                    bias(b, 0)
                    for u in range(NU):
                        nxt = chunks[u + 1] if u + 1 < NU else 0
                        for c in range(max(nxt, chunks[u])):
                            if c < nxt:
                                chunk_max(b, u + 1, c)
                            if c < chunks[u]:
                                G = b * NC + first[u] + c
                                dve.wait_ge(pt_mm, G + 1)
                                if first[u] + c >= 2:
                                    dve.wait_ge(pv_mm, G - 1)
                                wd = tiles_of(u, c) * P
                                gi = (first[u] + c) % 2
                                nc.vector.tensor_copy(pt[:, gi, 0:wd], tb[:, gi, 0:wd]).then_inc(pt_copied, 1)
                        if nxt:
                            bias(b, u + 1)
                        output(b, u)
                        if u % 2 == 0 and u > 0:
                            row_done(b, units[u][0] - 1)
                    row_done(b, KT - 1)

            @block.gpsimd
            def _(pool):
                def load(b, i):
                    n = b * BB + i
                    for k in range(R):
                        pool.wait_ge(rope_mul, n * 2 * R + 2 * k + 2)
                        if k == 2:
                            pool.wait_ge(rope_lo, n * R + 1)
                        nc.gpsimd.tensor_tensor(rp[:, k % 2, :], t1[:, k % 2, :], t2[:, k % 2, :], ALU.add)\
                            .then_inc(rope_add, 1)

                with pool.Fori(0, BATCH) as b:
                    with pool.Fori(0, BB) as i:
                        load(b, i)
                    with pool.Fori(0, BB) as i:
                        F.pool(nc, pool, b * BB + i, S)

            @block.scalar
            def _(act):
                def load(b, i):
                    n = b * BB + i
                    act.wait_ge(xt_mm, n + 1)
                    nc.scalar.activation(x32[:, :], misc[:, :], ACT.Copy).then_inc(x_copied, 1)
                    nc.scalar.activation(xh[:, :], misc[:, :], ACT.Copy).then_inc(x_copied, 1)
                    act.wait_ge(v_mm, n + 1)
                    nc.scalar.activation(v[:, bass.ds(i * BPT, BPT), :], pv[:, :].rearrange("p (a b) -> p a b", b=D),
                                         ACT.Copy).then_inc(v_copied, 1)
                    for k in range(R):
                        act.wait_ge(rope_add, n * R + k + 1)
                        nc.scalar.activation(kqh[:, k, bass.ds(i * BLK, BLK)], rp[:, k % 2, :], ACT.Copy).then_inc(rope_hi, 1)

                with act.Fori(0, BATCH) as b:
                    with act.Fori(0, BB) as i:
                        load(b, i)
                    for u in range(NU):
                        w = u % 2
                        act.wait_ge(bias_step, (b * NU + u) * 2 + 2)
                        if u >= 2:
                            act.wait_ge(den_step, (b * NU + u - 1) * 2)
                        for c in range(chunks[u]):
                            wd = tiles_of(u, c) * P
                            nc.scalar.activation(p[:, w, c * BLK:c * BLK + wd], sb4[:, (first[u] + c) % 4, 0:wd], ACT.Exp,
                                                 bias=nb[:, w:w + 1], scale=SCALE_C,
                                                 accum_out=ps[:, w, c:c + 1]).then_inc(exp_done, 1)
                        if w == 0 and u > 0:
                            act.wait_ge(ot_mm, b * KT + units[u][0])
                            nc.scalar.activation(ot[:, :], misc[:, 0:HC * P], ACT.Copy).then_inc(ot_copied, 1)
                    act.wait_ge(ot_mm, b * KT + KT)
                    nc.scalar.activation(ot[:, :], misc[:, 0:HC * P], ACT.Copy).then_inc(ot_copied, 1)

            @block.tensor
            def _(pe):
                ident, identb = g["ident"], g["identb"]

                def load(b, i):
                    n = b * BB + i
                    for s in range(BPT):
                        pe.wait_ge(xn_ready, n * BPT + s + 1)
                        last = nc.tensor.transpose(misc[:, s * P:(s + 1) * P], xn[:, s, :], ident[:, :])
                    last.then_inc(xt_mm, 1)
                    pe.wait_ge(x_copied, n * 2 + 2)
                    for s in range(BPT):
                        last = nc.tensor.matmul(pv[:, s * P:(s + 1) * P], x32[:, s * P:(s + 1) * P], wv[:, :],
                                                start=True, stop=True)
                    last.then_inc(v_mm, 1)
                    pe.wait_ge(xl_ready, n + 1)
                    for k in range(R):
                        if k == 2:
                            pe.wait_ge(rope_mul, n * 2 * R + 2)
                        for r in range(2):
                            last = matmul_split(nc, sb4[:, 2 * (k % 2) + r, :], wh[:, 2 * k + r, :], wl[:, 2 * k + r, :],
                                                xh[:, :], xl[:, :])
                        last.then_inc(proj_mm, 1)
                    pe.wait_ge(rope_mul, n * 2 * R + 2 * R)
                    pe.wait_ge(v_copied, n + 1)

                def scores(b, u, c):
                    qt, h = units[u]
                    k = first[u] + c
                    if k >= 4:
                        pe.wait_ge(exp_done, b * NC + k - 3)
                    qs = slice(qt * P, (qt + 1) * P)
                    wd = max(2, tiles_of(u, c)) * P
                    ks = slice(c * BLK, c * BLK + wd)
                    diag = c == chunks[u] - 1
                    last = matmul_split(nc, sb4[:, k % 4, 0:wd], kqh[:, 1 + h, qs], kql[:, 1 + h, qs],
                                        kqh[:, 0, ks], kql[:, 0, ks])
                    if diag:
                        d0 = (tiles_of(u, c) - 1) * P
                        last = nc.tensor.matmul(sb4[:, k % 4, d0:d0 + P], identb[:, :], mask[:, :], start=False, stop=True,
                                                skip_group_check=True)
                    last.then_inc(s_mm, 1)

                def transposes(b, u, c):
                    k = first[u] + c
                    pe.wait_ge(exp_done, b * NC + k + 1)
                    if k >= 2:
                        pe.wait_ge(pt_copied, b * NC + k - 1)
                    for a in range(tiles_of(u, c)):
                        last = nc.tensor.transpose(tb[:, k % 2, a * P:(a + 1) * P],
                                                   p[:, u % 2, c * BLK + a * P:c * BLK + (a + 1) * P], ident[:, :])
                    last.then_inc(pt_mm, 1)

                def values(b, u, c):
                    k = first[u] + c
                    pe.wait_ge(pt_copied, b * NC + k + 1)
                    if c == 0 and u > 0:
                        pe.wait_ge(o_ready, b * NU + u)
                    nt = tiles_of(u, c)
                    for a in range(nt):
                        last = nc.tensor.matmul(pv[:, 0:D], pt[:, k % 2, a * P:(a + 1) * P], v[:, c * BPT + a, :],
                                                start=(c == 0 and a == 0), stop=(c == chunks[u] - 1 and a == nt - 1))
                    last.then_inc(pv_mm, 1)

                def turn(b, qt):
                    pe.wait_ge(o_ready, b * NU + 2 * qt + 2)
                    if qt > 0:
                        pe.wait_ge(y_copied, b * KT + qt)
                    for h in range(HC):
                        last = nc.tensor.transpose(misc[:, h * P:(h + 1) * P], o[:, h, :], ident[:, :])
                    last.then_inc(ot_mm, 1)

                def out_project(b, qt):
                    pe.wait_ge(ot_copied, b * KT + qt + 1)
                    for h in range(HC):
                        last = nc.tensor.matmul(misc[:, 2 * P:3 * P], ot[:, h * P:(h + 1) * P], wo[:, h, :],
                                                start=(h == 0), stop=(h == HC - 1))
                    last.then_inc(out_mm, 1)

                with pe.Fori(0, BATCH) as b:
                    with pe.Fori(0, BB) as i:
                        load(b, i)
                    pe.wait_ge(rope_lo, (b + 1) * BB * R)
                    for c in range(chunks[0]):
                        scores(b, 0, c)
                    for u in range(NU):
                        nxt = chunks[u + 1] if u + 1 < NU else 0
                        for c in range(max(nxt, chunks[u] + 1)):
                            if c < nxt:
                                scores(b, u + 1, c)
                            if c < chunks[u]:
                                transposes(b, u, c)
                            if c == 0 and u % 2 == 0 and u > 0:
                                turn(b, units[u][0] - 1)
                            if 1 <= c <= chunks[u]:
                                values(b, u, c - 1)
                        if u % 2 == 0 and u > 0:
                            out_project(b, units[u][0] - 1)
                    turn(b, KT - 1)
                    out_project(b, KT - 1)
                    pe.wait_ge(y_copied, (b + 1) * KT)


FF = 4 * D
FC = FF // P


def ffn_layer1(nc, dr, X, g, out):
    with Mem(nc, "d_") as m:
        wh = m.sb("wh", [P, NE, FF], F32R)
        wl = m.sb("wl", [P, NE, FF], F32R)
        w2 = m.sb("w2", [P, NE, FC, D])
        b1 = m.sb("b1", [P, NE, FC])
        b2 = m.sb("b2", [P, NE, D])
        wr = [m.sb(f"wr{k}", [P, P], F32R) for k in range(2)]
        rbias = m.sb("rbias", [P, NE])
        inv = m.sb("inv", [P, TILES])
        with Mem(nc, "d0_") as t:
            S = Stats(m, t, g)
            raw = t.sb("raw", [P, NE, FF])
            b1raw = t.sb("b1raw", [P, NE, FC])
            rr = t.sb("rr", [P, P])
            lng = t.sb("lng", [P, NE])
            lnb = t.sb("lnb", [P, NE])
            bp = t.ps("bp")
            w_in = t.sem("w_in")
            c_in = t.sem("c_in")
            hi = t.sem("hi")
            lo = t.sem("lo")
            b_mm = t.sem("b_mm")
            b_done = t.sem("b_done")
            with nc.Block() as block:
                @block.sync
                def _(sp):
                    for dst, src in ((raw[:, :, :], "d_w1"), (lng[:, :], "d_lng"), (lnb[:, :], "d_lnb"),
                                     (rr[:, :], "d_wr"), (b1raw[:, :, :], "d_b1")):
                        sp.dma_start(dst, dr[src]).then_inc(w_in, 16)
                    for dst, src in ((w2[:, :, :, :], "d_w2"), (b2[:, :, :], "d_b2"), (rbias[:, :], "d_rbias")):
                        sp.dma_start(dst, dr[src]).then_inc(c_in, 16)
                    sp.wait_ge(c_in, 16 * 3)

                @block.scalar
                def _(act):
                    act.wait_ge(w_in, 16 * 5)
                    for e in range(NE):
                        nc.scalar.activation(wh[:, e, :], raw[:, e, :], ACT.Copy, scale=lng[:, e:e + 1]).then_inc(hi, 1)
                    nc.scalar.activation(wr[0][:, :], rr[:, :], ACT.Copy).then_inc(hi, 1)

                @block.vector
                def _(dve):
                    def weights():
                        for e in range(NE):
                            dve.wait_ge(hi, e + 1)
                            nc.vector.scalar_tensor_tensor(wl[:, e, :], raw[:, e, :], lng[:, e:e + 1],
                                                           wh[:, e, :].bitcast(F32), ALU.mult,
                                                           ALU.subtract).then_inc(lo, 1)
                        dve.wait_ge(hi, NE + 1)
                        nc.vector.tensor_tensor(wr[1][:, :], rr[:, :], wr[0][:, :].bitcast(F32),
                                                ALU.subtract).then_inc(lo, 1)
                    stats_vector(nc, dve, X, S, 1e-5, weights)
                    nc.vector.reciprocal(inv[:, :], S.r2[:, :]).then_inc(b_done, 1)
                    dve.wait_ge(b_mm, 1)
                    nc.vector.tensor_tensor(b1[:, :, :], bp[:, 0:NE * FC].rearrange("p (e c) -> p e c", c=FC),
                                            b1raw[:, :, :], ALU.add).then_inc(b_done, 1)

                @block.gpsimd
                def _(pool):
                    stats_pool(nc, pool, S)

                @block.tensor
                def _(pe):
                    pe.wait_ge(w_in, 16 * 5)
                    for e in range(NE):
                        for c in range(FC):
                            last = nc.tensor.matmul(bp[:, e * FC + c:e * FC + c + 1], raw[:, e, c * P:(c + 1) * P],
                                                    lnb[:, e:e + 1], start=True, stop=True)
                    last.then_inc(b_mm, 1)

        nh = m.sb("nh", [P, TILES * P], F32R)
        nl = m.sb("nl", [P, TILES * P], F32R)
        lg = m.sb("lg", [P, TILES, NE])
        gate = m.sb("gate", [P, TILES, NE])
        gsum = m.sb("gsum", [P, TILES])
        with Mem(nc, "d1_") as t:
            xn = t.sb("xn", [P, GRP, BPT, D])
            lt = t.sb("lt", [32, GRP, BLK])
            bk = t.ps("bk", 2 * GRP)
            xn_done = t.sem("xn_done")
            xt_mm = t.sem("xt_mm")
            xh_done = t.sem("xh_done")
            xl_done = t.sem("xl_done")
            l_mm = t.sem("l_mm")
            l_copied = t.sem("l_copied")
            lt_mm = t.sem("lt_mm")
            l_scaled = t.sem("l_scaled")
            l_done = t.sem("l_done")
            group = range(GRP)
            with nc.Block() as block:
                @block.scalar
                def _(act):
                    with act.Fori(0, NBLK // GRP) as gi:
                        n = gi * GRP
                        for i in group:
                            act.wait_ge(xt_mm, n + i + 1)
                            nc.scalar.activation(nh[:, bass.ds((n + i) * BLK, BLK)], bk[:, 2 * i, :],
                                                 ACT.Copy).then_inc(xh_done, 1)
                        for i in group:
                            act.wait_ge(l_mm, n + i + 1)
                            nc.scalar.activation(lt[:, i, :], bk[0:32, 2 * i + 1, :], ACT.Copy).then_inc(l_copied, 1)

                @block.vector
                def _(dve):
                    with dve.Fori(0, NBLK // GRP) as gi:
                        n = gi * GRP
                        for i in group:
                            for s in range(BPT):
                                tile = bass.ds((n + i) * BPT + s, 1)
                                nc.vector.tensor_scalar(xn[:, i, s, :], X[:, tile, :], S.mean[:, tile, 0], S.rr[:, tile],
                                                        ALU.subtract, ALU.mult).then_inc(xn_done, 1)
                        for i in group:
                            cols = bass.ds((n + i) * BLK, BLK)
                            dve.wait_ge(xh_done, n + i + 1)
                            nc.vector.tensor_tensor(nl[:, cols], bk[:, 2 * i, :], nh[:, cols].bitcast(F32),
                                                    ALU.subtract).then_inc(xl_done, 1)
                        for i in group:
                            blk = bass.ds((n + i) * BPT, BPT)
                            dve.wait_ge(lt_mm, n + i + 1)
                            nc.vector.tensor_tensor(lg[:, blk, :],
                                                    bk[:, 2 * i, 0:BPT * 32].rearrange("p (a b) -> p a b", b=32)[:, :, 0:NE],
                                                    inv[:, blk, None].to_broadcast([P, BPT, NE]),
                                                    ALU.mult).then_inc(l_scaled, 1)
                        for i in group:
                            blk = bass.ds((n + i) * BPT, BPT)
                            dve.wait_ge(l_scaled, n + i + 1)
                            nc.vector.tensor_tensor(lg[:, blk, :], lg[:, blk, :], rbias[:, None, :].to_broadcast([P, BPT, NE]),
                                                    ALU.add).then_inc(l_done, 1)

                @block.tensor
                def _(pe):
                    ident = g["ident"]
                    with pe.Fori(0, NBLK // GRP) as gi:
                        n = gi * GRP
                        for i in group:
                            for s in range(BPT):
                                pe.wait_ge(xn_done, (n + i) * BPT + s + 1)
                                last = nc.tensor.transpose(bk[:, 2 * i, s * P:(s + 1) * P], xn[:, i, s, :], ident[:, :])
                            last.then_inc(xt_mm, 1)
                        for i in group:
                            cols = bass.ds((n + i) * BLK, BLK)
                            pe.wait_ge(xh_done, n + i + 1)
                            pe.wait_ge(xl_done, n + i + 1)
                            matmul_split(nc, bk[:, 2 * i + 1, :], wr[0][:, :], wr[1][:, :], nh[:, cols],
                                         nl[:, cols]).then_inc(l_mm, 1)
                        for i in group:
                            wait_alone(pe, l_copied, n + i + 1, g["passed_pe"])
                            for s in range(BPT):
                                last = nc.tensor.transpose(bk[:, 2 * i, s * 32:(s + 1) * 32], lt[:, i, s * P:(s + 1) * P],
                                                           ident[0:32, 0:32])
                            last.then_inc(lt_mm, 1)
                        pe.wait_ge(l_scaled, n + GRP)

        router(nc, g, lg, gate, softmax_first=False, prefix="d2_")

        a = m.sb("a", [P, 2, FC, BLK])
        xi = m.sb("xi", [P, BPT, D])
        acc = m.sb("acc", [P, BPT, D])
        F = FinishNorm(m)
        ub = m.ps("ub", FC)
        db = m.ps("db", 2)
        summed = m.sem("summed")
        ln = m.sem("ln")
        up_mm = m.sem("up_mm")
        gelu = m.sem("gelu")
        down_mm = m.sem("down_mm")
        acc_done = m.sem("acc_done")
        stored = m.sem("stored")
        NA = BPT * (1 + 2 * NE)
        with nc.Block() as block:
            @block.sync
            def _(sp):
                with sp.Fori(0, NBLK) as n:
                    sp.wait_ge(F.step, n * F.N + F.N)
                    sp.dma_start(out.rearrange("(t p) d -> p t d", p=P)[:, bass.ds(n * BPT, BPT), :],
                                 X[:, bass.ds(n * BPT, BPT), :]).then_inc(stored, 16)
                sp.wait_ge(stored, 16 * NBLK)

            @block.scalar
            def _(act):
                with act.Fori(0, NBLK) as n:
                    for e in range(NE):
                        for c in range(FC):
                            act.wait_ge(up_mm, (n * NE + e) * FC + c + 1)
                            if e >= 2 and c == 0:
                                act.wait_ge(down_mm, n * NE + e - 1)
                            nc.scalar.activation(a[:, e % 2, c, :], ub[:, c, :], ACT.Gelu,
                                                 bias=b1[:, e, c:c + 1]).then_inc(gelu, 1)

            @block.gpsimd
            def _(pool):
                with pool.Fori(0, NBLK) as n:
                    F.pool(nc, pool, n, S)

            @block.vector
            def _(dve):
                nc.vector.tensor_reduce(gsum[:, :], gate[:, :, :], AXX, ALU.add).then_inc(summed, 1)
                dve.wait_ge(summed, 1)
                with dve.Fori(0, NBLK) as n:
                    tiles = [bass.ds(n * BPT + s, 1) for s in range(BPT)]
                    for s in range(BPT):
                        nc.vector.tensor_scalar(xi[:, s, :], X[:, tiles[s], :], S.mean[:, tiles[s], 0], S.r[:, tiles[s]],
                                                ALU.subtract, ALU.mult).then_inc(ln, 1)
                    for s in range(BPT):
                        dve.wait_ge(ln, n * BPT + s + 1)
                        nc.vector.tensor_scalar(acc[:, s, :], xi[:, s, :], gsum[:, tiles[s]], None,
                                                ALU.mult).then_inc(acc_done, 1)
                    for e in range(NE):
                        for s in range(BPT):
                            dve.wait_ge(acc_done, n * NA + e * BPT + s + 1)
                            nc.vector.scalar_tensor_tensor(acc[:, s, :], b2[:, e, :], gate[:, tiles[s], e], acc[:, s, :],
                                                           ALU.mult, ALU.add).then_inc(acc_done, 1)
                    for e in range(NE):
                        dve.wait_ge(down_mm, n * NE + e + 1)
                        for s in range(BPT):
                            dve.wait_ge(acc_done, n * NA + (NE + e) * BPT + s + 1)
                            nc.vector.scalar_tensor_tensor(acc[:, s, :], db[:, e % 2, s * P:(s + 1) * P],
                                                           gate[:, tiles[s], e], acc[:, s, :], ALU.mult,
                                                           ALU.add).then_inc(acc_done, 1)
                    dve.wait_ge(acc_done, n * NA + NA)
                    F.vector(nc, dve, n, acc, X, S)

            @block.tensor
            def _(pe):
                with pe.Fori(0, NBLK) as n:
                    cols = bass.ds(n * BLK, BLK)

                    def up(e, c):
                        if e > 0:
                            pe.wait_ge(gelu, (n * NE + e - 1) * FC + c + 1)
                        cs = slice(c * P, (c + 1) * P)
                        matmul_split(nc, ub[:, c, :], wh[:, e, cs], wl[:, e, cs], nh[:, cols], nl[:, cols]).then_inc(up_mm, 1)

                    def down(e, s):
                        if s == 0:
                            pe.wait_ge(gelu, (n * NE + e + 1) * FC)
                            if e >= 2:
                                pe.wait_ge(acc_done, n * NA + (NE + e) * BPT)
                        for c in range(FC):
                            last = nc.tensor.matmul(db[:, e % 2, s * P:(s + 1) * P], a[:, e % 2, c, s * P:(s + 1) * P],
                                                    w2[:, e, c, :], start=(c == 0), stop=(c == FC - 1))
                        if s == BPT - 1:
                            last.then_inc(down_mm, 1)

                    for c in range(FC):
                        up(0, c)
                    for e in range(NE):
                        for s in range(BPT):
                            if e + 1 < NE:
                                up(e + 1, s)
                            down(e, s)
                    pe.wait_ge(gelu, (n + 1) * NE * FC)
                    pe.wait_ge(acc_done, n * NA + NA)


def rope_tables(n, d, scale):
    pos = np.arange(0, d, 2, dtype=np.float32)
    if scale == 1:
        freq = (np.float32(1.0) / np.float32(10000.0) ** (pos / np.float32(d))).astype(np.float32)
    else:
        freq = (np.float32(10000.0) ** (np.float32(-2.0) * pos / np.float32(d))).astype(np.float32)
    ang = np.arange(n, dtype=np.float32)[None, :] * freq[:, None]
    return (np.repeat(np.cos(ang), 2, axis=0).astype(np.float32),
            np.repeat(np.sin(ang), 2, axis=0).astype(np.float32))


def host_layout(a):
    f = np.float32
    z = {}
    z["ident"] = np.eye(P, dtype=f)
    z["identb"] = np.eye(P, dtype=f).astype(mybir.dt.np(BF16))
    cos, sin = rope_tables(SEQ, DH0, 1)
    z["cs0"] = np.tile(np.stack([t.reshape(DH0, SEQ // SUB, SUB) for t in (cos, sin)], axis=2), (2, 1, 1, 1))
    row = np.arange(P)[:, None] % SEG
    col = np.arange(KEYS0)[None, :]
    masked = np.where((col < PM) | (col - PM <= row), 0.0, -1e30)
    z["mask0"] = np.tile(masked, (1, 6)).astype(mybir.dt.np(BF16))
    z["x"] = a["L0_attn_seq"].reshape(-1, D)
    z["norm_w"] = a["L0_attn_norm_w"].reshape(D, 1)
    z["w_qkv"] = a["L0_attn_w_qkv"]
    z["w_out"] = a["L0_attn_w_out"].reshape(PAIRS, P, D).transpose(1, 0, 2)
    z["b_out"] = np.broadcast_to(a["L0_attn_b_out"], (P, D))
    pk, pv = a["L0_attn_pm_k"], a["L0_attn_pm_v"]
    pmk = np.zeros((P, PAIRS, 2 * KEYS0), f)
    pmv = np.zeros((P, PAIRS, P), f)
    for h in range(H0):
        rows = slice((h % 2) * DH0, (h % 2 + 1) * DH0)
        pmk[rows, h // 2, (h % 2) * KEYS0:(h % 2) * KEYS0 + PM] = pk[h].T
        pmv[rows, h // 2, (h % 8) * PM:(h % 8 + 1) * PM] = pv[h].T
    z["pmkT"], z["pmvT"] = pmk, pmv
    wq, wkc, wvc = a["L0_ffn_Wq"].T, a["L0_ffn_Wkc"].T, a["L0_ffn_Wvc"].T
    z["b_wq"] = np.concatenate([wq[:, h * DK:(h + 1) * DK] for h in range(HB) for _ in range(3)], axis=1)
    z["b_wkv"] = np.concatenate([wkc, wkc, wkc, wvc], axis=1)
    z["b_wr"] = np.pad(a["L0_ffn_Wr"].T, ((0, 0), (0, P - NE)))
    z["b_w13"] = np.concatenate([
        np.concatenate([a["L0_ffn_eW" + k].transpose(2, 0, 1), a["L0_ffn_sW" + k].T[:, None, :]], axis=1)
        .reshape(D, -1) for k in "13"], axis=1)
    z["b_g12"] = np.stack([a["L0_ffn_g1"], a["L0_ffn_g2"]], axis=1)
    z["b_w2"] = np.concatenate([a["L0_ffn_eW2"].transpose(2, 0, 1), a["L0_ffn_sW2"].T[:, None, :]], axis=1)
    z["b_wo"] = a["L0_ffn_Wo"].T
    z["b_ebias"] = np.broadcast_to(a["L0_ffn_expert_bias"], (P, NE))
    z["iota"] = np.broadcast_to(np.arange(NE, dtype=f), (P, NE))
    cos, sin = rope_tables(SEQ, D, 2)
    z["cos1"], z["sin1"] = cos, sin
    z["mask1"] = np.where(np.arange(P)[None, :] <= np.arange(P)[:, None], 0.0, -1e30).astype(mybir.dt.np(BF16))
    z["c_wkq"] = np.stack([a["L1_attn_Wk"].T] + [a["L1_attn_Wq"][h].T for h in range(HC)], axis=1)
    z["c_wv"] = a["L1_attn_Wv"].T
    z["c_wo"] = a["L1_attn_Wo"].T.reshape(HC, D, D).transpose(1, 0, 2)
    z["d_w1"] = a["L1_ffn_W1"].transpose(1, 0, 2)
    z["d_lng"], z["d_lnb"] = a["L1_ffn_ln_g"].T, a["L1_ffn_ln_b"].T
    z["d_wr"] = np.pad(a["L1_ffn_router_W"], ((0, 0), (0, P - NE)))
    z["d_b1"] = a["L1_ffn_b1"].reshape(NE, FC, P).transpose(2, 0, 1)
    z["d_w2"] = a["L1_ffn_W2"].reshape(NE, FC, P, D).transpose(2, 0, 1, 3)
    z["d_b2"] = np.broadcast_to(a["L1_ffn_b2"], (P, NE, D))
    z["d_rbias"] = np.broadcast_to(a["L1_ffn_router_b"], (P, NE))
    return {k: np.ascontiguousarray(v) for k, v in z.items()}


def build_program(nc, dr, out):
    with Mem(nc, "g_") as gm:
        X = gm.sb("X", [P, TILES, D])
        g = {"ident": gm.sb("ident", [P, P]), "identb": gm.sb("identb", [P, P], BF16), "iota": gm.sb("iota", [P, NE]),
             "passed_dve": gm.sem("passed_dve"), "passed_pe": gm.sem("passed_pe")}
        local_attention(nc, dr, X, g)
        ffn_layer0(nc, dr, X, g)
        causal_attention(nc, dr, X, g)
        ffn_layer1(nc, dr, X, g, out)


def kernel(**inputs):
    import concourse.bacc as bacc
    from concourse.bass_utils import run_bass_kernel_spmd

    arrays = host_layout({k: np.asarray(v) for k, v in inputs.items()})
    nc = bacc.Bacc("TRN2", target_bir_lowering=False, num_devices=1)
    dr = {k: nc.dram_tensor(k, v.shape, mybir.dt.from_np(v.dtype), kind="ExternalInput").ap()
          for k, v in arrays.items()}
    out = nc.dram_tensor("out", (BATCH * SEQ, D), F32, kind="ExternalOutput").ap()
    build_program(nc, dr, out)
    r = run_bass_kernel_spmd(nc, [arrays], core_ids=[0])
    return r.results[0]["out"].reshape(BATCH, SEQ, D)
```

```python
import numpy as np
import concourse.bass as bass
import concourse.mybir as mybir
from contextlib import ExitStack

F32 = mybir.dt.float32
F32R = mybir.dt.float32r
BF16 = mybir.dt.bfloat16
U32 = mybir.dt.uint32
ALU = mybir.AluOpType
ACT = mybir.ActivationFunctionType
AXX = mybir.AxisListType.X

P = 128
D = 128
BATCH = 2
SEQ = 2048
TILES = BATCH * SEQ // P
BT = SEQ // P
BLK = 512
BPT = BLK // P
NBLK = BATCH * SEQ // BLK
BB = SEQ // BLK


class Mem:

    def __init__(self, nc, prefix):
        self.nc, self.prefix, self.ctx, self.sems = nc, "m" + prefix, ExitStack(), []

    def __enter__(self):
        self.ctx.__enter__()
        return self

    def __exit__(self, *a):
        if self.sems:
            self.nc.clear_and_free_semaphores(self.sems)
            self.nc.all_engine_barrier()
        return self.ctx.__exit__(*a)

    def sb(self, name, shape, dt=F32):
        return self.ctx.enter_context(self.nc.sbuf_tensor(self.prefix + name, shape, dt))

    def ps(self, name, banks=1, dt=F32, cols=512):
        shape = [P, cols] if banks == 1 else [P, banks, cols]
        return self.ctx.enter_context(self.nc.psum_tensor(self.prefix + name, shape, dt))

    def sem(self, name):
        s = self.nc.alloc_semaphore(self.prefix + name)
        self.sems.append(s)
        return s


def wait_alone(eng, sem, value, passed):
    eng.wait_ge(sem, value)
    eng.sem_inc(passed, 1)


def matmul_split(nc, out, lhs_hi, lhs_lo, rhs_hi, rhs_lo, start=True, stop=True):
    nc.tensor.matmul(out, lhs_hi, rhs_hi, start=start, stop=False)
    nc.tensor.matmul(out, lhs_lo, rhs_hi, start=False, stop=False)
    return nc.tensor.matmul(out, lhs_hi, rhs_lo, start=False, stop=stop)


H0 = 16
DH0 = 64
SEG = 64
PM = 16
PAIRS = H0 // 2
KEYS0 = PM + SEG
SCALE0 = DH0 ** -0.5
SBANKS = 3
PAIRS_OF_BANK = [(0, 1, 2), (3, 4, 5), (6, 7)]
SUB = 256
ST = SUB // P
SSEG = SUB // SEG
NSUB = BATCH * SEQ // SUB
FILL = [("pt", 0), ("pt", 1), ("ot", 0), ("pt", 2), ("pt", 3), ("ot", 1), ("pt", 4)]
FILLS = len(FILL)


def local_attention(nc, dr, X, g):
    m = Mem(nc, "a_")
    with m:
        NQK = 4 * 1024
        wh = m.sb("wh", [P, 5 * 1024], F32R)
        wl = m.sb("wl", [P, 5 * 1024], F32R)
        cs = m.sb("cs", [P, SEQ // SUB, 2, SUB])
        kt = m.sb("kt", [P, 2, PAIRS, SSEG, 2 * KEYS0])
        wout = m.sb("wout", [P, PAIRS, D])
        pmvw = m.sb("pmvw", [P, 2, D])
        bout = m.sb("bout", [P, D])
        mask = m.sb("mask", [P, 3 * 2 * KEYS0], BF16)
        mean = m.sb("mean", [P, TILES, 2])
        xsc = m.sb("xsc", [P, TILES])
        eps = m.sb("eps", [P, TILES])

        with Mem(nc, "a0_") as t:
            raw = t.sb("raw", [P, 3 * 1024])
            rot = t.sb("rot", [P, 2 * 1024])
            nw = t.sb("nw", [P, 1])
            pmvT = t.sb("pmvT", [P, PAIRS, P])
            bst = t.sb("bst", [P, TILES, 6])
            ve = t.sb("ve", [P, TILES])
            vt = t.sb("vt", [P, TILES])
            pp = t.ps("pp", 2, cols=512)
            CH = 4
            CT = TILES // CH
            CS = 2 * CT + 2
            x_in = [t.sem(f"x_in{c}") for c in range(CH)]
            w_in = t.sem("w_in")
            pm_in = t.sem("pm_in")
            c_in = t.sem("c_in")
            scaled = t.sem("scaled")
            rotated = t.sem("rotated")
            hi_done = t.sem("hi_done")
            lo_done = t.sem("lo_done")
            stat = t.sem("stat")
            powed = t.sem("powed")
            pm_spread = t.sem("pm_spread")
            pm_mm = t.sem("pm_mm")
            pm_cp = t.sem("pm_cp")
            srcs = [(raw, 0, 0), (rot, 0, 2), (raw, 1024, 0), (rot, 1024, 0), (raw, 2048, 0)]
            with nc.Block() as block:
                @block.sync
                def _(sp):
                    for c in range(CH):
                        sp.dma_start(X[:, c * CT:(c + 1) * CT, :],
                                     dr["x"].rearrange("(t p) d -> p t d", p=P)[:, c * CT:(c + 1) * CT, :])\
                            .then_inc(x_in[c], 16)
                        if c == 0:
                            sp.dma_start(nw[:, :], dr["norm_w"]).then_inc(w_in, 16)
                            sp.dma_start(raw[:, :], dr["w_qkv"]).then_inc(w_in, 16)
                    sp.dma_start(kt[:, 0, :, 0, :], dr["pmkT"]).then_inc(pm_in, 16)
                    for dst, src in ((pmvT[:, :, :], "pmvT"), (wout[:, :, :], "w_out"), (cs[:, :, :, :], "cs0"),
                                     (g["ident"][:, :], "ident"), (g["identb"][:, :], "identb"), (mask[:, :], "mask0"),
                                     (bout[:, :], "b_out")):
                        sp.dma_start(dst, dr[src]).then_inc(c_in, 16)
                    sp.wait_ge(c_in, 16 * 7)

                @block.vector
                def _(dve):
                    nc.vector.memset(eps[:, :], -0.5).then_inc(stat, 1)

                    def chunk(c):
                        at = 1 + c * CS
                        tiles = slice(c * CT, (c + 1) * CT)
                        dve.wait_ge(x_in[c], 16)
                        for i in range(tiles.start, tiles.stop):
                            nc.vector.bn_stats(bst[:, i, :], X[:, i, :]).then_inc(stat, 1)
                        for i in range(tiles.start, tiles.stop):
                            dve.wait_ge(stat, at + i - tiles.start + 1)
                            nc.vector.bn_aggr(mean[:, i, :], bst[:, i, :]).then_inc(stat, 1)
                        dve.wait_ge(stat, at + 2 * CT)
                        nc.vector.tensor_scalar(vt[:, tiles], mean[:, tiles, 1], 1e-5, 1e-6, ALU.add,
                                                ALU.mult).then_inc(stat, 1)
                        dve.wait_ge(stat, at + 2 * CT + 1)
                        nc.vector.tensor_tensor(ve[:, tiles], vt[:, tiles], mean[:, tiles, 1], ALU.add).then_inc(stat, 1)

                    chunk(0)
                    dve.wait_ge(w_in, 32)
                    for k in range(3):
                        cols = slice(k * 1024, (k + 1) * 1024)
                        nc.vector.tensor_scalar(raw[:, cols], raw[:, cols], nw[:, 0:1], None, ALU.mult).then_inc(scaled, 1)
                    dve.wait_ge(scaled, 2)
                    pair = raw[:, 0:2048].rearrange("p (n two) -> p n two", two=2)
                    rpair = rot[:, :].rearrange("p (n two) -> p n two", two=2)
                    nc.vector.tensor_scalar(rpair[:, :, 0], pair[:, :, 1], -1.0, None, ALU.mult).then_inc(rotated, 1)
                    nc.vector.tensor_copy(rpair[:, :, 1], pair[:, :, 0]).then_inc(rotated, 1)
                    chunk(1)
                    chunk(2)
                    chunk(3)
                    for k in range(3):
                        src, o, _ = srcs[k]
                        dve.wait_ge(hi_done, k + 1)
                        nc.vector.tensor_tensor(wl[:, k * 1024:(k + 1) * 1024], src[:, o:o + 1024],
                                                wh[:, k * 1024:(k + 1) * 1024].bitcast(F32),
                                                ALU.subtract).then_inc(lo_done, 1)
                    dve.wait_ge(pm_mm, 1)
                    nc.vector.tensor_copy(pmvw[:, :, :], pp[:, :, 0:D]).then_inc(pm_cp, 1)

                @block.gpsimd
                def _(pool):
                    def power(c):
                        tiles = slice(c * CT, (c + 1) * CT)
                        pool.wait_ge(stat, 1 + (c + 1) * CS)
                        nc.gpsimd.tensor_tensor(xsc[:, tiles], ve[:, tiles], eps[:, tiles], ALU.pow).then_inc(powed, 1)

                    power(0)
                    power(1)
                    power(2)
                    for k in (3, 4):
                        src, o, _ = srcs[k]
                        pool.wait_ge(hi_done, k + 1)
                        nc.gpsimd.tensor_tensor(wl[:, k * 1024:(k + 1) * 1024], src[:, o:o + 1024],
                                                wh[:, k * 1024:(k + 1) * 1024].bitcast(F32),
                                                ALU.subtract).then_inc(lo_done, 1)
                    power(3)

                @block.scalar
                def _(act):
                    for k, (src, o, need) in enumerate(srcs):
                        if k == 0:
                            act.wait_ge(scaled, 3)
                        if need:
                            act.wait_ge(rotated, need)
                        nc.scalar.activation(wh[:, k * 1024:(k + 1) * 1024], src[:, o:o + 1024],
                                             ACT.Copy).then_inc(hi_done, 1)
                    act.wait_ge(pm_in, 16)
                    for s in range(1, 2 * SSEG):
                        nc.scalar.activation(kt[:, s // SSEG, :, s % SSEG, :], kt[:, 0, :, 0, :],
                                             ACT.Copy).then_inc(pm_spread, 1)

                @block.tensor
                def _(pe):
                    pe.wait_ge(c_in, 16 * 7)
                    for half in range(2):
                        for k in range(4):
                            last = nc.tensor.matmul(pp[:, half, 0:D], pmvT[:, 4 * half + k, :],
                                                    wout[:, 4 * half + k, :], start=(k == 0), stop=(k == 3))
                    last.then_inc(pm_mm, 1)

        xn = m.sb("xn", [P, ST, D])
        xth = m.sb("xth", [P, SUB], F32R)
        xtl = m.sb("xtl", [P, SUB], F32R)
        tr = m.sb("tr", [P, 4, 2, SUB])
        qt = m.sb("qt", [P, 2, PAIRS, SUB])
        v = m.sb("v", [P, 2, ST, H0 * DH0])
        e = m.sb("e", [P, ST, H0, KEYS0])
        mx = m.sb("mx", [P, ST, H0])
        den = m.sb("den", [P, ST, H0])
        rden = m.sb("rden", [P, ST, H0])
        pb = m.sb("pb", [P, ST, H0, P])
        ppm = m.sb("ppm", [P, ST, H0 * PM])
        pt = m.sb("pt", [P, H0 + 2, P])
        ot = m.sb("ot", [P, PAIRS, P])
        y = m.sb("y", [P, ST, D])
        yst = m.sb("yst", [P, ST, 6])
        ymv = m.sb("ymv", [P, ST, 2])
        yve = m.sb("yve", [P, ST])
        yr = m.sb("yr", [P, ST])
        pbank = m.ps("pbank", 2)
        sbank = m.ps("sbank", SBANKS)
        fbank = m.ps("fbank", 2)
        misc = m.ps("misc")

        zeroed = m.sem("zeroed")
        xn_ready = m.sem("xn_ready")
        xt_mm = m.sem("xt_mm")
        xth_ready = m.sem("xth_ready")
        xtl_ready = m.sem("xtl_ready")
        proj_mm = m.sem("proj_mm")
        rope_mul = m.sem("rope_mul")
        rope_add = m.sem("rope_add")
        k_high = m.sem("k_high")
        v_mm = m.sem("v_mm")
        v_copied = m.sem("v_copied")
        s_mm = m.sem("s_mm")
        s_max = m.sem("s_max")
        s_sub = m.sem("s_sub")
        exp_done = m.sem("exp_done")
        den_done = m.sem("den_done")
        rden_done = m.sem("rden_done")
        p_norm = m.sem("p_norm")
        p_norm_high = m.sem("p_norm_high")
        fill_mm = m.sem("fill_mm")
        fill_copied = m.sem("fill_copied")
        out_mm = m.sem("out_mm")
        y_read = m.sem("y_read")
        y_chain = m.sem("y_chain")
        y_pow = m.sem("y_pow")
        y_fin = m.sem("y_fin")
        NCT = 2 * PAIRS

        class Sub:

            def __init__(self, j, par):
                self.n, self.par, self.j = j * 2 + par, par, j
                self.tile0 = par * BT + j * ST

        def steps(eng, step):
            step(Sub(0, 0), None, Sub(0, 1))
            step(Sub(0, 1), Sub(0, 0), Sub(1, 0))
            with eng.Fori(1, NSUB // 2 - 1) as j:
                step(Sub(j, 0), Sub(j - 1, 1), Sub(j, 1))
                step(Sub(j, 1), Sub(j, 0), Sub(j + 1, 0))
            last = NSUB // 2 - 1
            step(Sub(last, 0), Sub(last - 1, 1), Sub(last, 1))
            step(Sub(last, 1), Sub(last, 0), None)
            step(None, Sub(last, 1), None)

        with nc.Block() as block:
            @block.vector
            def _(dve):
                def norm(b):
                    if not (isinstance(b.n, int) and b.n == 0):
                        dve.wait_ge(xt_mm, b.n)
                    for s in range(ST):
                        tile = bass.ds(b.tile0 + s, 1)
                        nc.vector.tensor_scalar(xn[:, s, :], X[:, tile, :], mean[:, tile, 0], xsc[:, tile],
                                                ALU.subtract, ALU.mult).then_inc(xn_ready, 1)

                def low(b):
                    dve.wait_ge(xth_ready, b.n + 1)
                    nc.vector.tensor_tensor(xtl[:, :], misc[:, 0:SUB], xth[:, :].bitcast(F32),
                                            ALU.subtract).then_inc(xtl_ready, 1)

                def high_half(b, ct):
                    if ct < PAIRS:
                        return
                    dve.wait_ge(rope_mul, b.n * NCT + ct + 1)
                    nc.vector.tensor_tensor(
                        kt[64:128, b.par, ct - PAIRS, :, KEYS0 + PM:2 * KEYS0],
                        tr[64:128, ct % 4, 0, :].rearrange("p (a b) -> p a b", b=SEG),
                        tr[64:128, ct % 4, 1, :].rearrange("p (a b) -> p a b", b=SEG), ALU.add).then_inc(k_high, 1)

                def rope(b, ct):
                    dve.wait_ge(proj_mm, b.n * NCT + ct + 1)
                    if ct >= 4 or not isinstance(b.n, int) or b.n > 0:
                        dve.wait_ge(rope_add, b.n * NCT + ct - 3)
                    nc.vector.tensor_tensor(tr[:, ct % 4, :, :], pbank[:, ct % 2, :].rearrange("p (r c) -> p r c", r=2),
                                            cs[:, bass.ds(b.j, 1), :, :].rearrange("p o r c -> p (o r) c"),
                                            ALU.mult).then_inc(rope_mul, 1)
                    high_half(b, ct)

                def tile_max(a, s, b3):
                    h0, nh = 2 * PAIRS_OF_BANK[b3][0], 2 * len(PAIRS_OF_BANK[b3])
                    c = (a.n * ST + s) * 3 + b3 + 1
                    dve.wait_ge(s_mm, c)
                    nc.vector.tensor_reduce(mx[:, s, h0:h0 + nh],
                                            sbank[:, b3, 0:nh * KEYS0].rearrange("p (h k) -> p h k", k=KEYS0),
                                            AXX, ALU.max).then_inc(s_max, 1)

                def tile_sub(a, s, b3):
                    h0, nh = 2 * PAIRS_OF_BANK[b3][0], 2 * len(PAIRS_OF_BANK[b3])
                    dve.wait_ge(s_max, (a.n * ST + s) * 3 + b3 + 1)
                    nc.vector.tensor_tensor(e[:, s, h0:h0 + nh, :],
                                            sbank[:, b3, 0:nh * KEYS0].rearrange("p (h k) -> p h k", k=KEYS0),
                                            mx[:, s, h0:h0 + nh, None].to_broadcast([P, nh, KEYS0]),
                                            ALU.subtract).then_inc(s_sub, 1)

                def softmax_back(a, s):
                    T = a.n * ST + s
                    dve.wait_ge(exp_done, T + 1)
                    nc.vector.tensor_reduce(den[:, s, :], e[:, s, :, :], AXX, ALU.add).then_inc(den_done, 1)
                    dve.wait_ge(den_done, T + 1)
                    nc.vector.reciprocal(rden[:, s, :], den[:, s, :]).then_inc(rden_done, 1)
                    dve.wait_ge(rden_done, T + 1)
                    if isinstance(a.n, int) and a.n == 0:
                        dve.wait_ge(zeroed, 1)
                    nc.vector.tensor_tensor(pb[64:128, s, :, SEG:2 * SEG], e[64:128, s, :, PM:KEYS0],
                                            rden[64:128, s, :, None].to_broadcast([64, H0, SEG]),
                                            ALU.mult).then_inc(p_norm_high, 1)

                def out_read(a, s):
                    T = a.n * ST + s
                    dve.wait_ge(out_mm, T + 1)
                    nc.vector.tensor_tensor(y[:, s, :], misc[:, SUB:SUB + D], bout[:, :], ALU.add).then_inc(y_read, 1)
                    dve.wait_ge(y_read, T + 1)
                    nc.vector.bn_stats(yst[:, s, :], y[:, s, :]).then_inc(y_chain, 1)
                    wait_alone(dve, y_chain, T * 3 + 1, g["passed_dve"])
                    nc.vector.bn_aggr(ymv[:, s, :], yst[:, s, :]).then_inc(y_chain, 1)
                    dve.wait_ge(y_chain, T * 3 + 2)
                    nc.vector.tensor_scalar(yve[:, s:s + 1], ymv[:, s, 1:2], 1e-5, None, ALU.add).then_inc(y_chain, 1)

                def finish(a, s):
                    T = a.n * ST + s
                    dve.wait_ge(y_pow, T + 1)
                    nc.vector.tensor_scalar(y[:, s, :], y[:, s, :], ymv[:, s, 0:1], yr[:, s:s + 1],
                                            ALU.subtract, ALU.mult).then_inc(y_fin, 1)
                    dve.wait_ge(y_fin, T * 2 + 1)
                    xs = X[:, bass.ds(a.tile0 + s, 1), :]
                    nc.vector.tensor_tensor(xs, xs, y[:, s, None, :], ALU.add).then_inc(y_fin, 1)

                def step(b, a, nxt):
                    def ropes(*cts):
                        if b:
                            for ct in cts:
                                rope(b, ct)

                    def attend(f, *args):
                        if a:
                            f(a, *args)

                    if b:
                        low(b)
                    for k in range(3):
                        attend(tile_max, 0, k)
                    for k in range(3):
                        attend(tile_sub, 0, k)
                    ropes(0)
                    attend(softmax_back, 0)
                    ropes(1, 2, 3, 4)
                    for k in range(3):
                        attend(tile_max, 1, k)
                    for k in range(3):
                        attend(tile_sub, 1, k)
                    ropes(5, 6)
                    attend(softmax_back, 1)
                    ropes(7, 8, 9, 10)
                    attend(out_read, 0)
                    ropes(11, 12)
                    if nxt:
                        norm(nxt)
                    ropes(13)
                    attend(finish, 0)
                    ropes(14, 15)
                    attend(out_read, 1)
                    attend(finish, 1)

                norm(Sub(0, 0))
                steps(dve, step)

            @block.gpsimd
            def _(pool):
                def step(b, a, nxt):
                    def adds(*cts):
                        for ct in cts if b else ():
                            pool.wait_ge(rope_mul, b.n * NCT + ct + 1)
                            if ct < PAIRS:
                                nc.gpsimd.tensor_tensor(qt[:, b.par, ct, :], tr[:, ct % 4, 0, :], tr[:, ct % 4, 1, :],
                                                        ALU.add).then_inc(rope_add, 1)
                            else:
                                nc.gpsimd.tensor_tensor(
                                    kt[0:64, b.par, ct - PAIRS, :, PM:KEYS0],
                                    tr[0:64, ct % 4, 0, :].rearrange("p (a b) -> p a b", b=SEG),
                                    tr[0:64, ct % 4, 1, :].rearrange("p (a b) -> p a b", b=SEG),
                                    ALU.add).then_inc(rope_add, 1)

                    def normalise(s):
                        if a:
                            pool.wait_ge(rden_done, a.n * ST + s + 1)
                            nc.gpsimd.tensor_tensor(pb[0:64, s, :, 0:SEG], e[0:64, s, :, PM:KEYS0],
                                                    rden[0:64, s, :, None].to_broadcast([64, H0, SEG]),
                                                    ALU.mult).then_inc(p_norm, 1)
                            nc.gpsimd.tensor_tensor(ppm[:, s, :].rearrange("p (h k) -> p h k", k=PM), e[:, s, :, 0:PM],
                                                    rden[:, s, :, None].to_broadcast([P, H0, PM]),
                                                    ALU.mult).then_inc(p_norm, 1)

                    def power(s):
                        if a:
                            pool.wait_ge(y_chain, (a.n * ST + s + 1) * 3)
                            nc.gpsimd.tensor_tensor(yr[:, s:s + 1], yve[:, s:s + 1], eps[:, 0:1], ALU.pow).then_inc(y_pow, 1)

                    adds(0)
                    if not a:
                        adds(*range(1, NCT))
                        nc.gpsimd.memset(pb[:, :, :, :], 0.0).then_inc(zeroed, 1)
                        pool.wait_ge(zeroed, 1)
                        return
                    normalise(0)
                    adds(*range(1, 7))
                    normalise(1)
                    adds(7, 8, 9, 10)
                    power(0)
                    adds(*range(11, 16))
                    power(1)

                steps(pool, step)

            @block.scalar
            def _(act):
                def high(b):
                    act.wait_ge(xt_mm, b.n + 1)
                    nc.scalar.activation(xth[:, :], misc[:, 0:SUB], ACT.Copy).then_inc(xth_ready, 1)

                def step(b, a, nxt):
                    def exps(s):
                        if a:
                            act.wait_ge(s_sub, (a.n * ST + s + 1) * 3)
                            nc.scalar.activation(e[:, s, :, :], e[:, s, :, :], ACT.Exp, scale=SCALE0).then_inc(exp_done, 1)

                    def evacuate(s, *fills):
                        for i in fills if a else ():
                            F = (a.n * ST + s) * FILLS + i
                            kind, q = FILL[i]
                            act.wait_ge(fill_mm, F + 1)
                            nh = 2 if (kind, q) == ("pt", 4) else 4
                            dst = pt if kind == "pt" else ot
                            nc.scalar.activation(dst[:, 4 * q:4 * q + nh, :],
                                                 fbank[:, (s * FILLS + i) % 2, 0:nh * P].rearrange("p (a b) -> p a b", b=P),
                                                 ACT.Copy).then_inc(fill_copied, 1)

                    def values(*cs):
                        for c in cs if b else ():
                            act.wait_ge(v_mm, b.n * 2 * ST + c + 1)
                            nc.scalar.activation(v[:, b.par, c // 2, (c % 2) * 512:(c % 2) * 512 + 512], pbank[:, c % 2, :],
                                                 ACT.Copy).then_inc(v_copied, 1)

                    values(0, 1, 2, 3)
                    exps(0)
                    evacuate(0, 0, 1)
                    exps(1)
                    evacuate(0, 2, 3, 4, 5, 6)
                    evacuate(1, *range(FILLS))
                    if nxt:
                        high(nxt)

                high(Sub(0, 0))
                steps(act, step)

            @block.tensor
            def _(pe):
                ident, identb = g["ident"], g["identb"]

                def turn(b):
                    for s in range(ST):
                        pe.wait_ge(xn_ready, b.n * ST + s + 1)
                        last = nc.tensor.transpose(misc[:, s * P:(s + 1) * P], xn[:, s, :], ident[:, :])
                    last.then_inc(xt_mm, 1)

                def scores(b, s, b3):
                    T = b.n * ST + s
                    if s > 0 or not isinstance(b.n, int) or b.n > 0:
                        pe.wait_ge(s_sub, (T - 1) * 3 + b3 + 1)
                    if (s, b3) == (0, 0):
                        pe.wait_ge(rope_add, (b.n + 1) * NCT)
                        pe.wait_ge(k_high, (b.n + 1) * PAIRS)
                    prs = PAIRS_OF_BANK[b3]
                    wd = 2 * KEYS0 * len(prs)
                    for hf in range(2):
                        nc.tensor.matmul(sbank[64 * hf:64 * hf + 64, b3, 0:wd], identb[:, 64 * hf:64 * hf + 64],
                                         mask[:, 0:wd], start=True, stop=False, skip_group_check=True)
                    for i, pr in enumerate(prs):
                        for hf in range(2):
                            q0 = s * P + 64 * hf
                            last = nc.tensor.matmul(
                                sbank[64 * hf:64 * hf + 64, b3, i * 160:(i + 1) * 160],
                                qt[:, b.par, pr, q0:q0 + 64], kt[:, b.par, pr, 2 * s + hf, :],
                                start=False, stop=True, skip_group_check=True)
                    last.then_inc(s_mm, 1)

                def step(b, a, nxt):
                    def project(*cts):
                        for ct in cts if b else ():
                            if ct >= 2:
                                pe.wait_ge(rope_mul, b.n * NCT + ct - 1)
                            else:
                                pe.wait_ge(v_copied, b.n * 2 * ST + 3 + ct)
                            for r in range(2):
                                c = (ct // PAIRS) * 2048 + r * 1024 + (ct % PAIRS) * P
                                last = matmul_split(nc, pbank[:, ct % 2, r * SUB:(r + 1) * SUB], wh[:, c:c + P],
                                                    wl[:, c:c + P], xth[:, :], xtl[:, :])
                            last.then_inc(proj_mm, 1)

                    def values_of(*cs):
                        for c in cs if b else ():
                            if c == 0:
                                pe.wait_ge(xth_ready, b.n + 1)
                                pe.wait_ge(xtl_ready, b.n + 1)
                            if c < 2 and a:
                                pe.wait_ge(rope_mul, b.n * NCT - 1 + c)
                            if c >= 2:
                                pe.wait_ge(v_copied, b.n * 2 * ST + c - 1)
                            ts = slice((c // 2) * P, (c // 2 + 1) * P)
                            vc = slice(4096 + (c % 2) * 512, 4096 + (c % 2) * 512 + 512)
                            matmul_split(nc, pbank[:, c % 2, :], xth[:, ts], xtl[:, ts], wh[:, vc],
                                         wl[:, vc]).then_inc(v_mm, 1)

                    def fill(s, i):
                        if not a:
                            return
                        T = a.n * ST + s
                        F = T * FILLS + i
                        kind, q = FILL[i]
                        bank = fbank[:, (s * FILLS + i) % 2, :]
                        if i == 0:
                            pe.wait_ge(p_norm, T * 2 + 2)
                            pe.wait_ge(p_norm_high, T + 1)
                        if s > 0 or i >= 2 or not isinstance(a.n, int) or a.n > 0:
                            pe.wait_ge(fill_copied, F - 1)
                        if kind == "pt":
                            for k in range(4 if q < 4 else 2):
                                src = pb[:, s, 4 * q + k, :] if q < 4 else ppm[:, s, k * P:(k + 1) * P]
                                last = nc.tensor.transpose(bank[:, k * P:(k + 1) * P], src, ident[:, :])
                        else:
                            pe.wait_ge(fill_copied, T * FILLS + FILL.index(("pt", 2 * q + 1)) + 1)
                            if (s, q) == (0, 0):
                                pe.wait_ge(v_copied, (a.n + 1) * 2 * ST)
                            for pr in range(4 * q, 4 * q + 4):
                                for hh in range(2):
                                    h = 2 * pr + hh
                                    last = nc.tensor.matmul(
                                        bank[64 * hh:64 * hh + 64, (pr % 4) * P:(pr % 4 + 1) * P],
                                        v[:, a.par, s, h * DH0:(h + 1) * DH0], pt[:, h, :], start=True, stop=True)
                        last.then_inc(fill_mm, 1)

                    def out_project(s):
                        if not a:
                            return
                        T = a.n * ST + s
                        if s > 0 or not isinstance(a.n, int) or a.n > 0:
                            pe.wait_ge(y_read, T)
                        pe.wait_ge(fill_copied, (T + 1) * FILLS - 1)
                        for pr in range(PAIRS):
                            nc.tensor.matmul(misc[:, SUB:SUB + D], ot[:, pr, :], wout[:, pr, :], start=(pr == 0), stop=False)
                        pe.wait_ge(fill_copied, (T + 1) * FILLS)
                        for i in range(2):
                            last = nc.tensor.matmul(misc[:, SUB:SUB + D], pt[:, H0 + i, :], pmvw[:, i, :], start=False,
                                                    stop=(i == 1))
                        last.then_inc(out_mm, 1)

                    values_of(0, 1, 2, 3)
                    for b3 in range(SBANKS):
                        project(b3)
                        if a:
                            scores(a, 1, b3)
                    project(3, 4, 5)
                    fill(0, 0)
                    fill(0, 1)
                    project(6)
                    fill(0, 2)
                    fill(0, 3)
                    project(7)
                    fill(0, 4)
                    fill(0, 5)
                    project(8)
                    fill(0, 6)
                    project(9)
                    out_project(0)
                    project(10, 11)
                    fill(1, 0)
                    fill(1, 1)
                    project(12)
                    fill(1, 2)
                    fill(1, 3)
                    project(13)
                    fill(1, 4)
                    project(14)
                    fill(1, 5)
                    project(15)
                    fill(1, 6)
                    out_project(1)
                    if b:
                        scores(b, 0, 0)
                    if nxt:
                        if a:
                            pe.wait_ge(y_read, (a.n + 1) * ST)
                        turn(nxt)
                    if b:
                        scores(b, 0, 1)
                        scores(b, 0, 2)

                turn(Sub(0, 0))
                steps(pe, step)


class Stats:

    CHUNKS = 4
    CT = TILES // CHUNKS

    def __init__(self, m, t, g):
        self.passed = g["passed_dve"]
        self.mean = m.sb("mean", [P, TILES, 2])
        self.rs = m.sb("rs", [P, 2, TILES])
        self.r, self.rr = self.rs[:, 0, :], self.rs[:, 1, :]
        self.half = m.sb("half", [P, TILES])
        self.ve = m.sb("ve", [P, 2, TILES])
        self.bst = t.sb("bst", [P, TILES, 6])
        self.vt = t.sb("vt", [P, TILES])
        self.step = t.sem("stat_step")
        self.powed = t.sem("stat_pow")
        self.chunk_steps = 2 * self.CT + 3


def stats_vector(nc, dve, X, S, eps2, mid=None):
    nc.vector.memset(S.half[:, :], -0.5).then_inc(S.step, 1)
    for c in range(S.CHUNKS):
        at = 1 + c * S.chunk_steps
        tiles = slice(c * S.CT, (c + 1) * S.CT)
        for i in range(tiles.start, tiles.stop):
            nc.vector.bn_stats(S.bst[:, i, :], X[:, i, :]).then_inc(S.step, 1)
        for i in range(tiles.start, tiles.stop):
            dve.wait_ge(S.step, at + i - tiles.start + 1)
            nc.vector.bn_aggr(S.mean[:, i, :], S.bst[:, i, :]).then_inc(S.step, 1)
        dve.wait_ge(S.step, at + 2 * S.CT)
        nc.vector.tensor_scalar(S.vt[:, tiles], S.mean[:, tiles, 1], 1e-5, eps2, ALU.add, ALU.mult).then_inc(S.step, 1)
        nc.vector.tensor_scalar(S.ve[:, 0, tiles], S.mean[:, tiles, 1], 1e-5, None, ALU.add).then_inc(S.step, 1)
        dve.wait_ge(S.step, at + 2 * S.CT + 2)
        nc.vector.tensor_tensor(S.ve[:, 1, tiles], S.vt[:, tiles], S.mean[:, tiles, 1], ALU.add).then_inc(S.step, 1)
    if mid:
        mid()


def stats_pool(nc, pool, S, rows=slice(0, 2)):
    n = rows.stop - rows.start
    for c in range(S.CHUNKS):
        tiles = slice(c * S.CT, (c + 1) * S.CT)
        pool.wait_ge(S.step, 1 + (c + 1) * S.chunk_steps)
        nc.gpsimd.tensor_tensor(S.rs[:, rows, tiles], S.ve[:, rows, tiles],
                                S.half[:, 0:n * S.CT].rearrange("p (a b) -> p a b", b=S.CT),
                                ALU.pow).then_inc(S.powed, 1)


HB = 4
DK = D // HB
QROWS = 3 * DK
SCALE_B = 1.0 / np.sqrt(np.float32(DK))
KT = SEQ // P
NCH = SEQ // BLK
NE = 8
UNITS = 2 * BB
P1 = 2 * BPT * NCH
RING = 3
GRP = 4


def mqa_attention(nc, dr, X, g, S, wq, wkv, ao):
    m = Mem(nc, "b1_")
    with m:
        xn = m.sb("xn", [P, 2, BPT, D])
        xh = m.sb("xh", [P, SEQ], F32R)
        xl = m.sb("xl", [P, SEQ], F32R)
        ks = m.sb("ks", [QROWS + 2, SEQ], F32R)
        qs = [m.sb(f"qs{w}", [QROWS + 2, 2, BLK], F32R) for w in range(2)]
        vt = m.sb("vt", [P, 2, BLK])
        v1 = m.sb("v1", [P, KT, DK + 1])
        pt = m.sb("pt", [P, RING, 2, BLK])
        mxp = m.sb("mxp", [P, 2 * BPT, NCH])
        negm = m.sb("negm", [P, 2, BPT])
        mt = m.sb("mt", [P, BPT, 2 * DK])
        ots = m.sb("ots", [P, BLK])
        rd = m.sb("rd", [P, BPT, 2])
        p1b = m.ps("p1b", 2)
        stb = m.ps("stb", 4)
        pvb = m.ps("pvb")
        misc = m.ps("misc")

        r_done = m.sem("r_done")
        zeroed = m.sem("zeroed")
        xn_ready = m.sem("xn_ready")
        xt_mm = m.sem("xt_mm")
        xh_ready = m.sem("xh_ready")
        xl_ready = m.sem("xl_ready")
        kv_mm = m.sem("kv_mm")
        k_hi = m.sem("k_hi")
        k_lo = m.sem("k_lo")
        vt_ready = m.sem("vt_ready")
        vt_mm = m.sem("vt_mm")
        v_ready = m.sem("v_ready")
        q_mm = m.sem("q_mm")
        q_hi = m.sem("q_hi")
        q_lo = m.sem("q_lo")
        p1_mm = m.sem("p1_mm")
        p1_max = m.sem("p1_max")
        m_neg = m.sem("m_neg")
        m_split = m.sem("m_split")
        mt_mm = m.sem("mt_mm")
        m_rows = m.sem("m_rows")
        st_mm = m.sem("st_mm")
        exp_done = m.sem("exp_done")
        pv_mm = m.sem("pv_mm")
        pv_evac = m.sem("pv_evac")
        post_mm = m.sem("post_mm")
        rd_done = m.sem("rd_done")
        post_done = m.sem("post_done")

        def pass_bank(r):
            return misc[:, :] if r % 3 == 2 else p1b[:, r % 3, :]

        def schedule(unit, epilogue):
            def run(eng, b):
                unit(b, 0, 0, True, False)
                unit(b, 0, 1, False, False)
                with eng.Fori(1, BB - 1) as n:
                    unit(b, n, 0, False, False)
                    unit(b, n, 1, False, False)
                unit(b, BB - 1, 0, False, False)
                unit(b, BB - 1, 1, False, True)
                epilogue(b)
            return run

        def vbank(i):
            return misc if i % 2 == 0 else pvb

        with nc.Block() as block:
            @block.vector
            def _(dve):
                nc.vector.memset(ks[QROWS:QROWS + 2, :].bitcast(F32), 1.0).then_inc(zeroed, 1)
                nc.vector.memset(v1[:, :, DK:DK + 1], 1.0).then_inc(zeroed, 1)
                nc.vector.memset(mt[:, :, :], 0.0).then_inc(zeroed, 1)
                nc.vector.memset(ots[:, :], 0.0).then_inc(zeroed, 1)
                dve.wait_ge(zeroed, 4)

                def norm(b, i):
                    n = b * BB + i
                    if i >= 2:
                        dve.wait_ge(xt_mm, n - 1)
                    for s in range(BPT):
                        tile = bass.ds(n * BPT + s, 1)
                        nc.vector.tensor_scalar(xn[:, i % 2, s, :], X[:, tile, :], S.mean[:, tile, 0], S.rr[:, tile],
                                                ALU.subtract, ALU.mult).then_inc(xn_ready, 1)

                def x_low(b, i):
                    dve.wait_ge(xh_ready, b * BB + i + 1)
                    cols = slice(i * BLK, (i + 1) * BLK)
                    nc.vector.tensor_tensor(xl[:, cols], stb[:, i, :], xh[:, cols].bitcast(F32),
                                            ALU.subtract).then_inc(xl_ready, 1)

                def kv_read(b, i):
                    n = b * BB + i
                    cols = slice(i * BLK, (i + 1) * BLK)
                    dve.wait_ge(kv_mm, n + 1)
                    if i >= 2:
                        dve.wait_ge(vt_mm, n - 1)
                    nc.vector.tensor_copy(vt[QROWS:P, i % 2, :], p1b[QROWS:P, i % 2, :]).then_inc(vt_ready, 1)
                    dve.wait_ge(k_hi, n + 1)
                    nc.vector.tensor_tensor(ks[DK:2 * DK, cols], p1b[DK:2 * DK, i % 2, :],
                                            ks[DK:2 * DK, cols].bitcast(F32), ALU.subtract).then_inc(k_lo, 1)

                def v_read(b, i):
                    dve.wait_ge(vt_mm, b * BB + i + 1)
                    nc.vector.tensor_copy(v1[:, i * BPT:(i + 1) * BPT, 0:DK],
                                          vbank(i)[:, 0:BPT * DK].rearrange("p (a b) -> p a b", b=DK)).then_inc(v_ready, 1)

                def load(b):
                    norm(b, 0)
                    norm(b, 1)
                    x_low(b, 0)
                    for i in range(BB):
                        if i + 2 < BB:
                            norm(b, i + 2)
                        if i + 1 < BB:
                            x_low(b, i + 1)
                        kv_read(b, i)
                        if i > 0:
                            v_read(b, i - 1)
                    v_read(b, BB - 1)

                def q_low(V, w):
                    for hh in range(2):
                        src = misc[2 * DK:3 * DK, :] if hh == 0 else p1b[2 * DK:3 * DK, 0, :]
                        dst = qs[w][2 * DK:3 * DK, hh, :]
                        dve.wait_ge(q_hi, V * 2 + hh + 1)
                        nc.vector.tensor_tensor(dst, src, dst.bitcast(F32), ALU.subtract).then_inc(q_lo, 1)

                def maxima(V, w):
                    for r in range(P1):
                        dve.wait_ge(p1_mm, V * P1 + r + 1)
                        nc.vector.tensor_reduce(mxp[:, r // NCH, r % NCH:r % NCH + 1], pass_bank(r), AXX,
                                                ALU.max).then_inc(p1_max, 1)
                    dve.wait_ge(p1_max, V * P1 + P1)
                    nc.vector.tensor_reduce(negm[:, :, :].rearrange("p h t -> p (h t)"), mxp[:, :, :], AXX, ALU.max,
                                            negate=True).then_inc(m_neg, 1)
                    dve.wait_ge(m_neg, V + 1)
                    nt = negm[:, :, :].rearrange("p h t -> p t h")
                    hi, lo = mt[:, :, 0:2 * DK:DK], mt[:, :, 1:2 * DK:DK]
                    nc.vector.tensor_copy(hi.bitcast(F32R), nt).then_inc(m_split, 1)
                    dve.wait_ge(m_split, V * 2 + 1)
                    nc.vector.tensor_tensor(lo.bitcast(F32R), nt, hi, ALU.subtract).then_inc(m_split, 1)
                    dve.wait_ge(mt_mm, V + 1)
                    for hh in range(2):
                        nc.vector.tensor_copy(qs[w][QROWS:QROWS + 2, hh, :], misc[DK * hh:DK * hh + 2, :]).then_inc(m_rows, 1)

                def evacuate(U):
                    dve.wait_ge(pv_mm, (U + 1) * KT)
                    for hh in range(2):
                        nc.vector.tensor_copy(ots[64 * hh:64 * hh + DK + 1, :], pvb[64 * hh:64 * hh + DK + 1, :])\
                            .then_inc(pv_evac, 1)

                def post(U, b, n, w):
                    dve.wait_ge(post_mm, U + 1)
                    o = misc[:, :].rearrange("p (t h c) -> p t h c", t=BPT, h=2)
                    nc.vector.reciprocal(rd[:, :, :], o[:, :, :, DK]).then_inc(rd_done, 1)
                    dve.wait_ge(rd_done, U + 1)
                    for t in range(BPT):
                        dst = ao[:, bass.ds(b * BT + n * BPT + t, 1), w * 64:w * 64 + 64]
                        nc.vector.tensor_tensor(dst.rearrange("p a (h c) -> p (a h) c", h=2), o[:, t, :, 0:DK],
                                                rd[:, t, :, None].to_broadcast([P, 2, DK]),
                                                ALU.mult).then_inc(post_done, 1)

                def unit(b, n, w, first, last):
                    U = b * UNITS + n * 2 + w
                    if not first:
                        post(U - 1, b, n - 1 + w, 1 - w)
                    if not last:
                        q_low(U + 1, 1 - w)
                        maxima(U + 1, 1 - w)
                    evacuate(U)

                def epilogue(b):
                    post(b * UNITS + UNITS - 1, b, BB - 1, 1)

                run = schedule(unit, epilogue)
                with dve.Fori(0, BATCH) as b:
                    load(b)
                    q_low(b * UNITS, 0)
                    maxima(b * UNITS, 0)
                    run(dve, b)

            @block.scalar
            def _(act):
                def x_high(b, i):
                    act.wait_ge(xt_mm, b * BB + i + 1)
                    nc.scalar.activation(xh[:, i * BLK:(i + 1) * BLK], stb[:, i, :], ACT.Copy).then_inc(xh_ready, 1)

                def load(b):
                    x_high(b, 0)
                    x_high(b, 1)
                    for i in range(BB):
                        if i + 2 < BB:
                            x_high(b, i + 2)
                        n = b * BB + i
                        act.wait_ge(kv_mm, n + 1)
                        act.wait_ge(vt_ready, n + 1)
                        nc.scalar.activation(ks[0:QROWS, i * BLK:(i + 1) * BLK], p1b[0:QROWS, i % 2, :],
                                             ACT.Copy).then_inc(k_hi, 1)

                def q_high(V, w):
                    for hh in range(2):
                        src = misc[0:QROWS, :] if hh == 0 else p1b[0:QROWS, 0, :]
                        act.wait_ge(q_mm, V * 2 + hh + 1)
                        nc.scalar.activation(qs[w][0:QROWS, hh, :], src, ACT.Copy).then_inc(q_hi, 1)

                def unit(b, n, w, first, last):
                    U = b * UNITS + n * 2 + w
                    for i in range(KT):
                        act.wait_ge(st_mm, U * KT + i + 1)
                        if i >= RING:
                            act.wait_ge(pv_mm, U * KT + i - RING + 1)
                        nc.scalar.activation(pt[:, i % RING, :, :], stb[:, 2 * (i % 2):2 * (i % 2) + 2, :], ACT.Exp,
                                             scale=float(SCALE_B)).then_inc(exp_done, 1)
                        if i == 1 and not last:
                            q_high(U + 1, 1 - w)

                run = schedule(unit, lambda b: None)
                with act.Fori(0, BATCH) as b:
                    load(b)
                    q_high(b * UNITS, 0)
                    run(act, b)

            @block.gpsimd
            def _(pool):
                nc.gpsimd.tensor_tensor(S.r, S.ve[:, 0, :], S.half[:, :], ALU.pow).then_inc(r_done, 1)
                pool.wait_ge(r_done, 1)

            @block.tensor
            def _(pe):
                ident = g["ident"]
                pe.wait_ge(zeroed, 4)

                def turn_in(b, i):
                    for s in range(BPT):
                        pe.wait_ge(xn_ready, (b * BB + i) * BPT + s + 1)
                        last = nc.tensor.transpose(stb[:, i, s * P:(s + 1) * P], xn[:, i % 2, s, :], ident[:, :])
                    last.then_inc(xt_mm, 1)

                def turn_values(b, i):
                    n = b * BB + i
                    if i >= 2:
                        pe.wait_ge(v_ready, n - 1)
                    wait_alone(pe, vt_ready, n + 1, g["passed_pe"])
                    for s in range(BPT):
                        last = nc.tensor.transpose(vbank(i)[:, s * DK:(s + 1) * DK], vt[QROWS:P, i % 2, s * P:(s + 1) * P],
                                                   ident[QROWS:P, QROWS:P])
                    last.then_inc(vt_mm, 1)

                def load(b):
                    turn_in(b, 0)
                    turn_in(b, 1)
                    for i in range(BB):
                        n = b * BB + i
                        cols = slice(i * BLK, (i + 1) * BLK)
                        if i + 2 < BB:
                            turn_in(b, i + 2)
                        pe.wait_ge(xh_ready, n + 1)
                        pe.wait_ge(xl_ready, n + 1)
                        if i >= 2:
                            pe.wait_ge(k_lo, n - 1)
                        matmul_split(nc, p1b[:, i % 2, :], wkv[0][:, :], wkv[1][:, :], xh[:, cols],
                                     xl[:, cols]).then_inc(kv_mm, 1)
                        if i > 0:
                            turn_values(b, i - 1)
                    turn_values(b, BB - 1)
                    pe.wait_ge(k_lo, (b + 1) * BB)
                    pe.wait_ge(v_ready, (b + 1) * BB)

                def project(V, n, w):
                    cols = bass.ds(n * BLK, BLK)
                    for hh in range(2):
                        h = 2 * w + hh
                        out = misc[0:QROWS, :] if hh == 0 else p1b[0:QROWS, 0, :]
                        matmul_split(nc, out, wq[0][:, h, :], wq[1][:, h, :], xh[:, cols], xl[:, cols]).then_inc(q_mm, 1)

                def first_pass(V, w, r):
                    if r == 0:
                        pe.wait_ge(q_lo, V * 2 + 2)
                    if r >= 3:
                        pe.wait_ge(p1_max, V * P1 + r - 2)
                    hh, t, c = r // (BPT * NCH), (r // NCH) % BPT, r % NCH
                    nc.tensor.matmul(pass_bank(r), qs[w][0:QROWS, hh, t * P:(t + 1) * P],
                                     ks[0:QROWS, c * BLK:(c + 1) * BLK], start=True, stop=True).then_inc(p1_mm, 1)

                def max_rows(V):
                    wait_alone(pe, m_split, V * 2 + 2, g["passed_pe"])
                    for t in range(BPT):
                        last = nc.tensor.transpose(misc[0:2 * DK, t * P:(t + 1) * P], mt[:, t, :], ident[:, :])
                    last.then_inc(mt_mm, 1)

                def scores(U, w, i):
                    if i == 0:
                        pe.wait_ge(m_rows, U * 2 + 2)
                    if i >= 2:
                        pe.wait_ge(exp_done, U * KT + i - 1)
                    for hh in range(2):
                        last = nc.tensor.matmul(stb[:, 2 * (i % 2) + hh, :], ks[:, i * P:(i + 1) * P], qs[w][:, hh, :],
                                                start=True, stop=True)
                    last.then_inc(st_mm, 1)

                def values(U, i):
                    pe.wait_ge(exp_done, U * KT + i + 1)
                    for hh in range(2):
                        last = nc.tensor.matmul(pvb[64 * hh:64 * hh + DK + 1, :], v1[:, i, :], pt[:, i % RING, hh, :],
                                                start=(i == 0), stop=(i == KT - 1), skip_group_check=True)
                    last.then_inc(pv_mm, 1)

                def post(U):
                    pe.wait_ge(pv_evac, U * 2 + 2)
                    for t in range(BPT):
                        last = nc.tensor.transpose(misc[:, t * P:t * P + P], ots[:, t * P:(t + 1) * P], ident[:, :])
                    last.then_inc(post_mm, 1)

                def unit(b, n, w, first, last):
                    U = b * UNITS + n * 2 + w
                    scores(U, w, 0)
                    passes = iter(range(0 if last else P1))

                    def next_pass(i):
                        r = next(passes, None) if i >= 2 else None
                        if r is not None:
                            first_pass(U + 1, 1 - w, r)

                    for i in range(KT):
                        next_pass(i)
                        if i + 1 < KT:
                            scores(U, w, i + 1)
                        next_pass(i)
                        if i == 0 and not first:
                            post(U - 1)
                        if i == 1 and not last:
                            if not first:
                                pe.wait_ge(post_done, U * BPT)
                            project(U + 1, n + w, 1 - w)
                        if i == KT - 1 and not last:
                            max_rows(U + 1)
                        values(U, i)
                        next_pass(i)

                def epilogue(b):
                    post(b * UNITS + UNITS - 1)
                    pe.wait_ge(post_done, (b + 1) * UNITS * BPT)

                run = schedule(unit, epilogue)
                with pe.Fori(0, BATCH) as b:
                    load(b)
                    project(b * UNITS, 0, 0)
                    for r in range(P1):
                        first_pass(b * UNITS, 0, r)
                    max_rows(b * UNITS)
                    run(pe, b)


def ffn_mixture(nc, dr, X, g, S, w, ao):
    m = Mem(nc, "b2_")
    with m:
        w1, w2, wr, wo, ebias = w["w13"], w["w2"], w["wr"], w["wo"], w["ebias"]
        x2 = m.sb("x2", [P, TILES, D])
        nh = m.sb("nh", [P, TILES * P], F32R)
        nl = m.sb("nl", [P, TILES * P], F32R)
        lg = m.sb("lg", [P, TILES, NE])
        gate = m.sb("gate", [P, TILES, NE])
        with Mem(nc, "b2a_") as t:
            aos = t.sb("aos", [P, GRP, BPT, D])
            aot = t.sb("aot", [P, GRP, BLK])
            h = t.sb("h", [P, GRP, BPT, D])
            sq = t.sb("sq", [P, GRP, BPT, D])
            ss = t.sb("ss", [P, GRP, BPT])
            sv = t.sb("sv", [P, GRP, BPT])
            r2 = t.sb("r2", [P, GRP, BPT])
            xn = t.sb("xn", [P, GRP, BPT, D])
            lt = t.sb("lt", [32, GRP, BLK])
            bk = t.ps("bk", 2 * GRP)
            copied = t.sem("copied")
            at_mm = t.sem("at_mm")
            at_ready = t.sem("at_ready")
            o_mm = t.sem("o_mm")
            ln = t.sem("ln")
            x2_done = t.sem("x2_done")
            sq_done = t.sem("sq_done")
            sum_done = t.sem("sum_done")
            var_done = t.sem("var_done")
            powed = t.sem("powed")
            xn_done = t.sem("xn_done")
            xt_mm = t.sem("xt_mm")
            xh_done = t.sem("xh_done")
            xl_done = t.sem("xl_done")
            l_mm = t.sem("l_mm")
            l_copied = t.sem("l_copied")
            lt_mm = t.sem("lt_mm")
            l_done = t.sem("l_done")
            group = range(GRP)
            with nc.Block() as block:
                @block.scalar
                def _(act):
                    with act.Fori(0, NBLK // GRP) as gi:
                        n = gi * GRP
                        for i in group:
                            nc.scalar.activation(aos[:, i, :, :], ao[:, bass.ds((n + i) * BPT, BPT), :],
                                                 ACT.Copy).then_inc(copied, 1)
                        for i in group:
                            act.wait_ge(at_mm, n + i + 1)
                            nc.scalar.activation(aot[:, i, :], bk[:, 2 * i, :], ACT.Copy).then_inc(at_ready, 1)
                        for i in group:
                            act.wait_ge(xt_mm, n + i + 1)
                            nc.scalar.activation(nh[:, bass.ds((n + i) * BLK, BLK)], bk[:, 2 * i, :],
                                                 ACT.Copy).then_inc(xh_done, 1)
                        for i in group:
                            act.wait_ge(l_mm, n + i + 1)
                            nc.scalar.activation(lt[:, i, :], bk[0:32, 2 * i + 1, :], ACT.Copy).then_inc(l_copied, 1)

                @block.gpsimd
                def _(pool):
                    with pool.Fori(0, NBLK // GRP) as gi:
                        pool.wait_ge(var_done, gi * GRP + GRP)
                        nc.gpsimd.tensor_tensor(r2[:, :, :], sv[:, :, :],
                                                S.half[:, 0:GRP * BPT].rearrange("p (a b) -> p a b", b=BPT),
                                                ALU.pow).then_inc(powed, 1)

                @block.vector
                def _(dve):
                    with dve.Fori(0, NBLK // GRP) as gi:
                        n = gi * GRP
                        for i in group:
                            for s in range(BPT):
                                tile = bass.ds((n + i) * BPT + s, 1)
                                nc.vector.tensor_scalar(h[:, i, s, :], X[:, tile, :], S.mean[:, tile, 0], S.r[:, tile],
                                                        ALU.subtract, ALU.mult).then_inc(ln, 1)
                        for i in group:
                            blk = bass.ds((n + i) * BPT, BPT)
                            dve.wait_ge(o_mm, n + i + 1)
                            dve.wait_ge(ln, (n + i + 1) * BPT)
                            nc.vector.tensor_tensor(x2[:, blk, :], bk[:, 2 * i + 1, :].rearrange("p (a b) -> p a b", b=D),
                                                    h[:, i, :, :], ALU.add).then_inc(x2_done, 1)
                        for i in group:
                            blk = bass.ds((n + i) * BPT, BPT)
                            dve.wait_ge(x2_done, n + i + 1)
                            nc.vector.tensor_tensor(sq[:, i, :, :], x2[:, blk, :], x2[:, blk, :], ALU.mult)\
                                .then_inc(sq_done, 1)
                        for i in group:
                            dve.wait_ge(sq_done, n + i + 1)
                            nc.vector.tensor_reduce(ss[:, i, :], sq[:, i, :, :], AXX, ALU.add).then_inc(sum_done, 1)
                        for i in group:
                            dve.wait_ge(sum_done, n + i + 1)
                            nc.vector.tensor_scalar(sv[:, i, :], ss[:, i, :], 1.0 / D, 1e-6, ALU.mult,
                                                    ALU.add).then_inc(var_done, 1)
                        dve.wait_ge(powed, gi + 1)
                        for i in group:
                            nc.vector.tensor_tensor(xn[:, i, :, :], x2[:, bass.ds((n + i) * BPT, BPT), :],
                                                    r2[:, i, :, None].to_broadcast([P, BPT, D]),
                                                    ALU.mult).then_inc(xn_done, 1)
                        for i in group:
                            cols = bass.ds((n + i) * BLK, BLK)
                            dve.wait_ge(xh_done, n + i + 1)
                            nc.vector.tensor_tensor(nl[:, cols], bk[:, 2 * i, :], nh[:, cols].bitcast(F32),
                                                    ALU.subtract).then_inc(xl_done, 1)
                        for i in group:
                            dve.wait_ge(lt_mm, n + i + 1)
                            nc.vector.tensor_tensor(lg[:, bass.ds((n + i) * BPT, BPT), :],
                                                    bk[:, 2 * i, 0:BPT * 32].rearrange("p (a b) -> p a b", b=32)[:, :, 0:NE],
                                                    ebias[:, None, :].to_broadcast([P, BPT, NE]), ALU.add).then_inc(l_done, 1)

                @block.tensor
                def _(pe):
                    ident = g["ident"]
                    with pe.Fori(0, NBLK // GRP) as gi:
                        n = gi * GRP
                        for i in group:
                            pe.wait_ge(copied, n + i + 1)
                            for s in range(BPT):
                                last = nc.tensor.transpose(bk[:, 2 * i, s * P:(s + 1) * P], aos[:, i, s, :], ident[:, :])
                            last.then_inc(at_mm, 1)
                        for i in group:
                            pe.wait_ge(at_ready, n + i + 1)
                            for s in range(BPT):
                                last = nc.tensor.matmul(bk[:, 2 * i + 1, s * P:(s + 1) * P], aot[:, i, s * P:(s + 1) * P],
                                                        wo[:, :], start=True, stop=True)
                            last.then_inc(o_mm, 1)
                        for i in group:
                            pe.wait_ge(xn_done, n + i + 1)
                            for s in range(BPT):
                                last = nc.tensor.transpose(bk[:, 2 * i, s * P:(s + 1) * P], xn[:, i, s, :], ident[:, :])
                            last.then_inc(xt_mm, 1)
                        for i in group:
                            cols = bass.ds((n + i) * BLK, BLK)
                            pe.wait_ge(xh_done, n + i + 1)
                            pe.wait_ge(xl_done, n + i + 1)
                            matmul_split(nc, bk[:, 2 * i + 1, :], wr[0][:, :], wr[1][:, :], nh[:, cols],
                                         nl[:, cols]).then_inc(l_mm, 1)
                        for i in group:
                            wait_alone(pe, l_copied, n + i + 1, g["passed_pe"])
                            for s in range(BPT):
                                last = nc.tensor.transpose(bk[:, 2 * i, s * 32:(s + 1) * 32], lt[:, i, s * P:(s + 1) * P],
                                                           ident[0:32, 0:32])
                            last.then_inc(lt_mm, 1)
                        pe.wait_ge(l_done, n + GRP)

        router = Router(m, g, lg, gate, softmax_first=True)
        s1 = m.sb("s1", [P, 2, BLK])
        hh = m.sb("hh", [P, 2, BLK])
        acc = m.sb("acc", [P, BPT, D])
        F = FinishNorm(m)
        ub = m.ps("ub", 4)
        db = m.ps("db", 2)
        up_mm = m.sem("up_mm")
        silu = m.sem("silu")
        h_done = m.sem("h_done")
        down_mm = m.sem("down_mm")
        acc_done = m.sem("acc_done")
        NX = NE + 1
        order = [NE] + list(range(NE))
        with nc.Block() as block:
            @block.scalar
            def _(act):
                router.scalar(nc, act)
                with act.Fori(0, NBLK) as n:
                    for i in range(NX):
                        act.wait_ge(up_mm, (n * NX + i) * 2 + 1)
                        if i >= 2:
                            act.wait_ge(h_done, n * NX + i - 1)
                        nc.scalar.activation(s1[:, i % 2, :], ub[:, 2 * (i % 2), :], ACT.Silu).then_inc(silu, 1)

            @block.gpsimd
            def _(pool):
                with pool.Fori(0, NBLK) as n:
                    F.pool(nc, pool, n, S)

            @block.vector
            def _(dve):
                router.vector(nc, dve)
                with dve.Fori(0, NBLK) as n:
                    def accumulate(i):
                        e = order[i]
                        dve.wait_ge(down_mm, n * NX + i + 1)
                        for s in range(BPT):
                            tile = bass.ds(n * BPT + s, 1)
                            src = db[:, i % 2, s * P:(s + 1) * P]
                            if i == 0:
                                nc.vector.tensor_tensor(acc[:, s, None, :], db[:, 0, None, s * P:(s + 1) * P],
                                                        x2[:, tile, :], ALU.add).then_inc(acc_done, 1)
                            else:
                                dve.wait_ge(acc_done, (n * NX + i) * BPT)
                                nc.vector.scalar_tensor_tensor(acc[:, s, :], src, gate[:, tile, e], acc[:, s, :],
                                                               ALU.mult, ALU.add).then_inc(acc_done, 1)

                    for i in range(NX):
                        dve.wait_ge(up_mm, (n * NX + i) * 2 + 2)
                        dve.wait_ge(silu, n * NX + i + 1)
                        if i >= 2:
                            dve.wait_ge(down_mm, n * NX + i - 1)
                        nc.vector.tensor_tensor(hh[:, i % 2, :], s1[:, i % 2, :], ub[:, 2 * (i % 2) + 1, :],
                                                ALU.mult).then_inc(h_done, 1)
                        if i >= 1:
                            accumulate(i - 1)
                    accumulate(NX - 1)
                    dve.wait_ge(acc_done, (n * NX + NX) * BPT)
                    F.vector(nc, dve, n, acc, X, S)

            @block.tensor
            def _(pe):
                with pe.Fori(0, NBLK) as n:
                    cols = bass.ds(n * BLK, BLK)

                    def up(i):
                        e = order[i]
                        if i >= 2:
                            pe.wait_ge(h_done, n * NX + i - 1)
                        for k in range(2):
                            matmul_split(nc, ub[:, 2 * (i % 2) + k, :], w1[0][:, k, e, :], w1[1][:, k, e, :],
                                         nh[:, cols], nl[:, cols]).then_inc(up_mm, 1)

                    def down(i):
                        pe.wait_ge(h_done, n * NX + i + 1)
                        if i >= 2:
                            pe.wait_ge(acc_done, (n * NX + i - 1) * BPT)
                        for s in range(BPT):
                            last = nc.tensor.matmul(db[:, i % 2, s * P:(s + 1) * P], hh[:, i % 2, s * P:(s + 1) * P],
                                                    w2[:, order[i], :], start=True, stop=True)
                        last.then_inc(down_mm, 1)

                    up(0)
                    for i in range(NX):
                        if i + 1 < NX:
                            up(i + 1)
                        down(i)
                    pe.wait_ge(acc_done, (n * NX + NX) * BPT)


class FinishNorm:

    def __init__(self, m, by_rows=False):
        self.st = m.sb("fst", [P, BPT, 6])
        self.mv = m.sb("fmv", [P, BPT, 2])
        self.ve = m.sb("fve", [P, BPT])
        self.rs = m.sb("frs", [P, BPT])
        self.step = m.sem("fstep")
        self.powed = m.sem("fpowed")
        self.N = 2 * BPT + 1 + (0 if by_rows else 2 * BPT)
        if by_rows:
            self.added = m.sem("fadded")
            self.passed = m.sem("fpassed")

    def vector(self, nc, dve, n, acc, X, S):
        o = n * self.N
        for s in range(BPT):
            nc.vector.bn_stats(self.st[:, s, :], acc[:, s, :]).then_inc(self.step, 1)
        for s in range(BPT):
            wait_alone(dve, self.step, o + s + 1, S.passed)
            nc.vector.bn_aggr(self.mv[:, s, :], self.st[:, s, :]).then_inc(self.step, 1)
        dve.wait_ge(self.step, o + 2 * BPT)
        nc.vector.tensor_scalar(self.ve[:, :], self.mv[:, :, 1], 1e-5, None, ALU.add).then_inc(self.step, 1)
        dve.wait_ge(self.powed, n + 1)
        for s in range(BPT):
            nc.vector.tensor_scalar(acc[:, s, :], acc[:, s, :], self.mv[:, s, 0:1], self.rs[:, s:s + 1],
                                    ALU.subtract, ALU.mult).then_inc(self.step, 1)
        for s in range(BPT):
            dve.wait_ge(self.step, o + 2 * BPT + 2 + s)
            xs = X[:, bass.ds(n * BPT + s, 1), :]
            nc.vector.tensor_tensor(xs, xs, acc[:, s, None, :], ALU.add).then_inc(self.step, 1)
        dve.wait_ge(self.step, o + self.N)

    def row_stats(self, nc, dve, n, s, acc):
        o = n * self.N
        nc.vector.bn_stats(self.st[:, s, :], acc[:, s, :]).then_inc(self.step, 1)
        wait_alone(dve, self.step, o + 2 * s + 1, self.passed)
        nc.vector.bn_aggr(self.mv[:, s, :], self.st[:, s, :]).then_inc(self.step, 1)
        if s == BPT - 1:
            dve.wait_ge(self.step, o + 2 * BPT)
            nc.vector.tensor_scalar(self.ve[:, :], self.mv[:, :, 1], 1e-5, None, ALU.add).then_inc(self.step, 1)

    def applied(self, n, s):
        return (n * BPT + s + 1) * 2

    def apply(self, nc, dve, n, s, acc, X, tile):
        dve.wait_ge(self.powed, n + 1)
        nc.vector.tensor_scalar(acc[:, s, :], acc[:, s, :], self.mv[:, s, 0:1], self.rs[:, s:s + 1],
                                ALU.subtract, ALU.mult).then_inc(self.added, 1)
        dve.wait_ge(self.added, self.applied(n, s) - 1)
        xs = X[:, bass.ds(tile, 1), :]
        nc.vector.tensor_tensor(xs, xs, acc[:, s, None, :], ALU.add).then_inc(self.added, 1)

    def pool(self, nc, pool, n, S):
        pool.wait_ge(self.step, n * self.N + 2 * BPT + 1)
        nc.gpsimd.tensor_tensor(self.rs[:, :], self.ve[:, :], S.half[:, 0:BPT], ALU.pow).then_inc(self.powed, 1)


class Router:

    def __init__(self, m, g, lg, gate, softmax_first):
        T = TILES
        self.g, self.lg, self.gate, self.first = g, lg, gate, softmax_first
        self.pr = m.sb("r_pr", [P, T, NE])
        self.mx = m.sb("r_mx", [P, T])
        self.top = m.sb("r_top", [P, T, 8])
        self.idx = m.sb("r_idx", [P, T, 8], U32)
        self.idf = m.sb("r_idf", [P, T, 2])
        self.df = m.sb("r_df", [P, T])
        self.ex = m.sb("r_ex", [P, T])
        self.wt = m.sb("r_wt", [P, 2, T])
        self.oh = m.sb("r_oh", [P, T, NE])
        self.step = m.sem("r_step")
        self.exps = m.sem("r_exps")

    def scalar(self, nc, act):
        k = 0
        if self.first:
            act.wait_ge(self.step, 2)
            nc.scalar.activation(self.pr[:, :, :], self.pr[:, :, :], ACT.Exp).then_inc(self.exps, 1)
            k = 5
        act.wait_ge(self.step, k + TILES + 1)
        nc.scalar.activation(self.ex[:, :], self.df[:, :], ACT.Exp).then_inc(self.exps, 1)

    def vector(self, nc, dve):
        T, step, exps, iota = TILES, self.step, self.exps, self.g["iota"]
        lg, gate, pr, mx, top, idx, idf, df, ex, wt, oh = (
            self.lg, self.gate, self.pr, self.mx, self.top, self.idx, self.idf, self.df, self.ex, self.wt, self.oh)
        c = 0

        def bc(x):
            return x.to_broadcast([P, T, NE])

        if self.first:
            nc.vector.tensor_reduce(mx[:, :], lg[:, :, :], AXX, ALU.max).then_inc(step, 1)
            dve.wait_ge(step, 1)
            nc.vector.tensor_tensor(pr[:, :, :], lg[:, :, :], bc(mx[:, :, None]), ALU.subtract).then_inc(step, 1)
            dve.wait_ge(exps, 1)
            nc.vector.tensor_reduce(mx[:, :], pr[:, :, :], AXX, ALU.add).then_inc(step, 1)
            dve.wait_ge(step, 3)
            nc.vector.reciprocal(df[:, :], mx[:, :]).then_inc(step, 1)
            dve.wait_ge(step, 4)
            nc.vector.tensor_tensor(lg[:, :, :], pr[:, :, :], bc(df[:, :, None]), ALU.mult).then_inc(step, 1)
            c = 5
            dve.wait_ge(step, c)
        for i in range(T):
            nc.vector.max(top[:, i, :], lg[:, i, :]).then_inc(step, 1)
        dve.wait_ge(step, c + T)
        nc.vector.tensor_tensor(df[:, :], top[:, :, 1], top[:, :, 0], ALU.subtract).then_inc(step, 1)
        for i in range(T):
            nc.vector.max_index(idx[:, i, :], top[:, i, :], lg[:, i, :]).then_inc(step, 1)
        dve.wait_ge(step, c + 2 * T + 1)
        nc.vector.tensor_copy(idf[:, :, :], idx[:, :, 0:2]).then_inc(step, 1)
        dve.wait_ge(exps, 2 if self.first else 1)
        nc.vector.tensor_scalar(mx[:, :], ex[:, :], 1.0, None, ALU.add).then_inc(step, 1)
        dve.wait_ge(step, c + 2 * T + 3)
        nc.vector.reciprocal(wt[:, 0, :], mx[:, :]).then_inc(step, 1)
        dve.wait_ge(step, c + 2 * T + 4)
        nc.vector.tensor_tensor(wt[:, 1, :], ex[:, :], wt[:, 0, :], ALU.mult).then_inc(step, 1)
        for k, dst in ((0, gate), (1, oh)):
            nc.vector.tensor_tensor(dst[:, :, :], iota[:, None, :].to_broadcast([P, T, NE]),
                                    bc(idf[:, :, k:k + 1]), ALU.is_equal).then_inc(step, 1)
            dve.wait_ge(step, c + 2 * T + 6 + 2 * k)
            nc.vector.tensor_tensor(dst[:, :, :], dst[:, :, :], bc(wt[:, k, :, None]), ALU.mult).then_inc(step, 1)
        dve.wait_ge(step, c + 2 * T + 9)
        nc.vector.tensor_tensor(gate[:, :, :], gate[:, :, :], oh[:, :, :], ALU.add).then_inc(step, 1)
        dve.wait_ge(step, c + 2 * T + 10)


def ffn_layer0(nc, dr, X, g):
    with Mem(nc, "b_") as m:
        ao = m.sb("ao", [P, TILES, D])
        wq = [m.sb(f"wq{k}", [P, HB, QROWS], F32R) for k in range(2)]
        wkv = [m.sb(f"wkv{k}", [P, P], F32R) for k in range(2)]
        w = {"w13": [m.sb(f"w13{k}", [P, 2, NE + 1, D], F32R) for k in range(2)],
             "wr": [m.sb(f"wr{k}", [P, P], F32R) for k in range(2)],
             "w2": m.sb("w2", [P, NE + 1, D]), "wo": m.sb("wo", [P, D]), "ebias": m.sb("ebias", [P, NE])}
        with Mem(nc, "b0_") as t:
            S = Stats(m, t, g)
            rq = t.sb("rq", [P, HB * QROWS])
            rkv = t.sb("rkv", [P, P])
            rr = t.sb("rr", [P, P])
            r13 = t.sb("r13", [P, 2 * (NE + 1) * D])
            g12 = t.sb("g12", [P, 2])
            w_in = t.sem("w_in")
            scaled = t.sem("scaled")
            hi = t.sem("hi")
            lo = t.sem("lo")
            sets = [(rq, wq, "p h q -> p (h q)", 0), (rkv, wkv, None, 0), (rr, w["wr"], None, 1),
                    (r13, w["w13"], "p k e f -> p (k e f)", 1)]

            def flat(x, pat):
                a = x[:, :] if pat is None else x[tuple([slice(None)] * len(x.shape))].rearrange(pat)
                return a

            with nc.Block() as block:
                @block.sync
                def _(sp):
                    for dst, src in ((rq[:, :], "b_wq"), (rkv[:, :], "b_wkv"), (rr[:, :], "b_wr"), (r13[:, :], "b_w13"),
                                     (g12[:, :], "b_g12"), (w["w2"][:, :, :], "b_w2"), (w["wo"][:, :], "b_wo"),
                                     (w["ebias"][:, :], "b_ebias"), (g["iota"][:, :], "iota")):
                        sp.dma_start(dst, dr[src]).then_inc(w_in, 16)
                    sp.wait_ge(w_in, 16 * 9)

                @block.vector
                def _(dve):
                    def weights():
                        dve.wait_ge(w_in, 16 * 9)
                        for raw, _, _, gi in sets:
                            nc.vector.tensor_scalar(raw[:, :], raw[:, :], g12[:, gi:gi + 1], None,
                                                    ALU.mult).then_inc(scaled, 1)
                        for k, (raw, dst, pat, _) in enumerate(sets):
                            dve.wait_ge(hi, k + 1)
                            nc.vector.tensor_tensor(flat(dst[1], pat), raw[:, :], flat(dst[0], pat).bitcast(F32),
                                                    ALU.subtract).then_inc(lo, 1)
                    stats_vector(nc, dve, X, S, 1e-6, weights)

                @block.gpsimd
                def _(pool):
                    stats_pool(nc, pool, S, rows=slice(1, 2))

                @block.scalar
                def _(act):
                    for k, (raw, dst, pat, _) in enumerate(sets):
                        act.wait_ge(scaled, k + 1)
                        nc.scalar.activation(flat(dst[0], pat), raw[:, :], ACT.Copy).then_inc(hi, 1)
        mqa_attention(nc, dr, X, g, S, wq, wkv, ao)
        ffn_mixture(nc, dr, X, g, S, w, ao)


HC = 2
SCALE_C = float(D) ** -0.5


def causal_attention(nc, dr, X, g):
    with Mem(nc, "c_") as m:
        NW = 2 * (1 + HC)
        wh = m.sb("wh", [P, NW, D], F32R)
        wl = m.sb("wl", [P, NW, D], F32R)
        wv = m.sb("wv", [P, D])
        wo = m.sb("wo", [P, HC, D])
        mask = m.sb("mask", [P, P], BF16)
        cs = m.sb("cs", [P, BB, 2, BLK])
        with Mem(nc, "c0_") as t:
            S = Stats(m, t, g)
            raw = t.sb("raw", [P, NW, D])
            w_in = t.sem("w_in")
            c_in = t.sem("c_in")
            rot = t.sem("rot")
            hi = t.sem("hi")
            lo = t.sem("lo")
            with nc.Block() as block:
                @block.sync
                def _(sp):
                    sp.dma_start(raw[:, 0::2, :], dr["c_wkq"]).then_inc(w_in, 16)
                    for dst, src in ((wv[:, :], "c_wv"), (wo[:, :, :], "c_wo"), (mask[:, :], "mask1"),
                                     (cs[:, :, :, :], "cs1")):
                        sp.dma_start(dst, dr[src]).then_inc(c_in, 16)
                    sp.wait_ge(c_in, 16 * 4)

                @block.vector
                def _(dve):
                    def weights():
                        dve.wait_ge(w_in, 16)
                        for k in range(0, NW, 2):
                            src = raw[:, k, :].rearrange("p (n two) -> p n two", two=2)
                            dst = raw[:, k + 1, :].rearrange("p (n two) -> p n two", two=2)
                            nc.vector.tensor_scalar(dst[:, :, 0], src[:, :, 1], -1.0, None, ALU.mult).then_inc(rot, 1)
                            nc.vector.tensor_copy(dst[:, :, 1], src[:, :, 0]).then_inc(rot, 1)
                        dve.wait_ge(hi, 1)
                        nc.vector.tensor_tensor(wl[:, :, :], raw[:, :, :], wh[:, :, :].bitcast(F32),
                                                ALU.subtract).then_inc(lo, 1)
                    stats_vector(nc, dve, X, S, 1e-5, weights)

                @block.gpsimd
                def _(pool):
                    stats_pool(nc, pool, S, rows=slice(0, 1))

                @block.scalar
                def _(act):
                    act.wait_ge(rot, NW)
                    nc.scalar.activation(wh[:, :, :], raw[:, :, :], ACT.Copy).then_inc(hi, 1)

        xn = m.sb("xn", [P, 2, BPT, D])
        x32 = m.sb("x32", [P, 2, BLK])
        xh = m.sb("xh", [P, 2, BLK], F32R)
        xl = m.sb("xl", [P, 2, BLK], F32R)
        tr = m.sb("tr", [P, 2, 2, BLK])
        rp = m.sb("rp", [P, 2, BLK])
        kqh = m.sb("kqh", [P, 1 + HC, SEQ], F32R)
        kql = m.sb("kql", [P, 1 + HC, SEQ], F32R)
        v = m.sb("v", [P, KT, D])
        p = m.sb("p", [P, 2, SEQ])
        pt = m.sb("pt", [P, 2, BLK])
        mp = m.sb("mp", [P, 2, NCH])
        mm = m.sb("mm", [P, 2])
        nb = m.sb("nb", [P, 2])
        ps = m.sb("ps", [P, 2, NCH])
        den = m.sb("den", [P, 2])
        rden = m.sb("rden", [P, 2])
        o = m.sb("o", [P, HC, D])
        ot = m.sb("ot", [P, HC * P])
        acc = m.sb("acc", [P, BPT, D])
        F = FinishNorm(m, by_rows=True)
        sb4 = m.ps("sb4", 4)
        tb = m.ps("tb", 2)
        pv = m.ps("pv")
        misc = m.ps("misc")

        xn_ready = m.sem("xn_ready")
        xt_mm = m.sem("xt_mm")
        x_copied = m.sem("x_copied")
        xl_ready = m.sem("xl_ready")
        v_mm = m.sem("v_mm")
        v_copied = m.sem("v_copied")
        proj_mm = m.sem("proj_mm")
        rope_mul = m.sem("rope_mul")
        rope_add = m.sem("rope_add")
        rope_hi = m.sem("rope_hi")
        rope_lo = m.sem("rope_lo")
        s_mm = m.sem("s_mm")
        s_max = m.sem("s_max")
        bias_step = m.sem("bias_step")
        exp_done = m.sem("exp_done")
        pt_mm = m.sem("pt_mm")
        pt_copied = m.sem("pt_copied")
        pv_mm = m.sem("pv_mm")
        den_step = m.sem("den_step")
        o_ready = m.sem("o_ready")
        ot_mm = m.sem("ot_mm")
        ot_copied = m.sem("ot_copied")
        out_mm = m.sem("out_mm")
        y_copied = m.sem("y_copied")

        rows = [qt for k in range(KT // 2) for qt in (k, KT - 1 - k)]
        units = [(qt, h) for qt in rows for h in range(HC)]
        NU = len(units)
        chunks = [(qt + BPT) // BPT for qt, _ in units]
        first = [sum(chunks[:u]) for u in range(NU + 1)]
        NC = first[NU]
        R = 1 + HC
        NR = BB * R

        def steps_of(u):
            nxt = chunks[u + 1] if u + 1 < NU else 0
            for j in range(max((nxt + 1) // 2, chunks[u] + 1)):
                yield j, [c for c in (2 * j, 2 * j + 1) if c < nxt], 2 * j < nxt <= 2 * j + 2

        def tiles_of(u, c):
            return min(BPT, units[u][0] + 1 - c * BPT)

        def vbank(i):
            return pv[:, :] if i % 2 == 0 else misc[:, :]

        with nc.Block() as block:
            @block.vector
            def _(dve):
                def norm(b, i):
                    n = b * BB + i
                    if i >= 2:
                        dve.wait_ge(xt_mm, n - 1)
                    for s in range(BPT):
                        tile = bass.ds(n * BPT + s, 1)
                        nc.vector.tensor_scalar(xn[:, i % 2, s, :], X[:, tile, :], S.mean[:, tile, 0], S.r[:, tile],
                                                ALU.subtract, ALU.mult).then_inc(xn_ready, 1)

                def low(b, i):
                    dve.wait_ge(x_copied, (b * BB + i) * 2 + 2)
                    nc.vector.tensor_tensor(xl[:, i % 2, :], tb[:, i % 2, :], xh[:, i % 2, :].bitcast(F32),
                                            ALU.subtract).then_inc(xl_ready, 1)

                def rope(b, q):
                    dve.wait_ge(proj_mm, b * NR + q + 1)
                    if q >= 2:
                        dve.wait_ge(rope_add, b * NR + q - 1)
                    nc.vector.tensor_tensor(tr[:, q % 2, :, :], sb4[:, 2 * (q % 2):2 * (q % 2) + 2, :], cs[:, q // R, :, :],
                                            ALU.mult).then_inc(rope_mul, 1)

                def rope_low(b, q):
                    dve.wait_ge(rope_hi, b * NR + q + 1)
                    cols = slice(q // R * BLK, (q // R + 1) * BLK)
                    nc.vector.tensor_tensor(kql[:, q % R, cols], rp[:, q % 2, :], kqh[:, q % R, cols].bitcast(F32),
                                            ALU.subtract).then_inc(rope_lo, 1)

                def load(b):
                    norm(b, 0)
                    norm(b, 1)
                    low(b, 0)
                    for i in range(BB):
                        rope(b, R * i)
                        if i > 0:
                            rope_low(b, R * i - 1)
                        if i + 2 < BB:
                            norm(b, i + 2)
                        rope(b, R * i + 1)
                        rope_low(b, R * i)
                        if i + 1 < BB:
                            low(b, i + 1)
                        rope(b, R * i + 2)
                        rope_low(b, R * i + 1)
                    rope_low(b, NR - 1)

                def chunk_max(b, u, c):
                    G = b * NC + first[u] + c
                    dve.wait_ge(s_mm, G + 1)
                    nc.vector.tensor_reduce(mp[:, u % 2, c:c + 1], sb4[:, (first[u] + c) % 4, 0:tiles_of(u, c) * P],
                                            AXX, ALU.max).then_inc(s_max, 1)

                def bias(b, u):
                    U = b * NU + u
                    dve.wait_ge(s_max, b * NC + first[u + 1])
                    nc.vector.tensor_reduce(mm[:, u % 2:u % 2 + 1], mp[:, u % 2, 0:chunks[u]], AXX,
                                            ALU.max).then_inc(bias_step, 1)
                    dve.wait_ge(bias_step, U * 2 + 1)
                    nc.vector.tensor_scalar(nb[:, u % 2:u % 2 + 1], mm[:, u % 2:u % 2 + 1], -SCALE_C, None,
                                            ALU.mult).then_inc(bias_step, 1)

                def output(b, u):
                    U = b * NU + u
                    w = u % 2
                    dve.wait_ge(exp_done, b * NC + first[u + 1])
                    nc.vector.tensor_reduce(den[:, w:w + 1], ps[:, w, 0:chunks[u]], AXX, ALU.add).then_inc(den_step, 1)
                    dve.wait_ge(den_step, U * 2 + 1)
                    nc.vector.reciprocal(rden[:, w:w + 1], den[:, w:w + 1]).then_inc(den_step, 1)
                    dve.wait_ge(den_step, U * 2 + 2)
                    dve.wait_ge(pv_mm, b * NC + first[u + 1])
                    nc.vector.tensor_scalar(o[:, w, :], pv[:, 0:D], rden[:, w:w + 1], None, ALU.mult).then_inc(o_ready, 1)

                def row_done(b, r):
                    n, s = b * BB + r // BPT, r % BPT
                    if r >= BPT:
                        dve.wait_ge(F.added, F.applied(n - 1, s))
                    dve.wait_ge(out_mm, b * KT + r + 1)
                    nc.vector.tensor_copy(acc[:, s, :], misc[:, 2 * P:3 * P]).then_inc(y_copied, 1)
                    dve.wait_ge(y_copied, b * KT + r + 1)
                    F.row_stats(nc, dve, n, s, acc)

                def apply(b, r):
                    F.apply(nc, dve, b * BB + r // BPT, r % BPT, acc, X, b * BT + rows[r])

                def unit_out(b, u):
                    k = u - 1 - 2 * BPT
                    if k >= 0 and k % (2 * BPT) < BPT:
                        apply(b, k // (2 * BPT) * BPT + k % (2 * BPT))
                    if u % 2 == 0 and u > 0:
                        row_done(b, u // 2 - 1)

                with dve.Fori(0, BATCH) as b:
                    load(b)
                    for c in range(chunks[0]):
                        chunk_max(b, 0, c)
                    bias(b, 0)
                    for u in range(NU):
                        for c, ahead, complete in steps_of(u):
                            if c < chunks[u]:
                                G = b * NC + first[u] + c
                                dve.wait_ge(pt_mm, G + 1)
                                if first[u] + c >= 2:
                                    dve.wait_ge(pv_mm, G - 1)
                                wd = tiles_of(u, c) * P
                                gi = (first[u] + c) % 2
                                nc.vector.tensor_copy(pt[:, gi, 0:wd], tb[:, gi, 0:wd]).then_inc(pt_copied, 1)
                            for a in ahead:
                                chunk_max(b, u + 1, a)
                            if complete:
                                bias(b, u + 1)
                            if c == 1 and u > 0:
                                unit_out(b, u - 1)
                        output(b, u)
                    unit_out(b, NU - 1)
                    row_done(b, KT - 1)
                    for s in range(BPT):
                        apply(b, KT - BPT + s)
                    dve.wait_ge(F.added, F.applied(b * BB + BB - 1, BPT - 1))

            @block.gpsimd
            def _(pool):
                def load(b):
                    for q in range(NR):
                        pool.wait_ge(rope_mul, b * NR + q + 1)
                        if q >= 2:
                            pool.wait_ge(rope_lo, b * NR + q - 1)
                        nc.gpsimd.tensor_tensor(rp[:, q % 2, :], tr[:, q % 2, 0, :], tr[:, q % 2, 1, :], ALU.add)\
                            .then_inc(rope_add, 1)

                with pool.Fori(0, BATCH) as b:
                    load(b)
                    with pool.Fori(0, BB) as i:
                        F.pool(nc, pool, b * BB + i, S)

            @block.scalar
            def _(act):
                def copies(b, i):
                    act.wait_ge(xt_mm, b * BB + i + 1)
                    nc.scalar.activation(xh[:, i % 2, :], tb[:, i % 2, :], ACT.Copy).then_inc(x_copied, 1)
                    nc.scalar.activation(x32[:, i % 2, :], tb[:, i % 2, :], ACT.Copy).then_inc(x_copied, 1)

                def rope_high(b, q):
                    act.wait_ge(rope_add, b * NR + q + 1)
                    nc.scalar.activation(kqh[:, q % R, q // R * BLK:(q // R + 1) * BLK], rp[:, q % 2, :],
                                         ACT.Copy).then_inc(rope_hi, 1)

                def load(b):
                    copies(b, 0)
                    copies(b, 1)
                    for i in range(BB):
                        act.wait_ge(v_mm, b * BB + i + 1)
                        nc.scalar.activation(v[:, i * BPT:(i + 1) * BPT, :], vbank(i).rearrange("p (a b) -> p a b", b=D),
                                             ACT.Copy).then_inc(v_copied, 1)
                        rope_high(b, R * i)
                        rope_high(b, R * i + 1)
                        if i + 2 < BB:
                            copies(b, i + 2)
                        rope_high(b, R * i + 2)

                with act.Fori(0, BATCH) as b:
                    load(b)
                    for u in range(NU):
                        w = u % 2
                        act.wait_ge(bias_step, (b * NU + u) * 2 + 2)
                        if u >= 2:
                            act.wait_ge(den_step, (b * NU + u - 1) * 2)
                        for c in range(chunks[u]):
                            wd = tiles_of(u, c) * P
                            nc.scalar.activation(p[:, w, c * BLK:c * BLK + wd], sb4[:, (first[u] + c) % 4, 0:wd], ACT.Exp,
                                                 bias=nb[:, w:w + 1], scale=SCALE_C,
                                                 accum_out=ps[:, w, c:c + 1]).then_inc(exp_done, 1)
                        if w == 0 and u > 0:
                            act.wait_ge(ot_mm, b * KT + u // 2)
                            nc.scalar.activation(ot[:, :], misc[:, 0:HC * P], ACT.Copy).then_inc(ot_copied, 1)
                    act.wait_ge(ot_mm, b * KT + KT)
                    nc.scalar.activation(ot[:, :], misc[:, 0:HC * P], ACT.Copy).then_inc(ot_copied, 1)

            @block.tensor
            def _(pe):
                ident, identb = g["ident"], g["identb"]

                def turn_in(b, i):
                    for s in range(BPT):
                        pe.wait_ge(xn_ready, (b * BB + i) * BPT + s + 1)
                        last = nc.tensor.transpose(tb[:, i % 2, s * P:(s + 1) * P], xn[:, i % 2, s, :], ident[:, :])
                    last.then_inc(xt_mm, 1)

                def load(b):
                    turn_in(b, 0)
                    turn_in(b, 1)
                    for i in range(BB):
                        pe.wait_ge(x_copied, (b * BB + i) * 2 + 2)
                        if i >= 2:
                            pe.wait_ge(v_copied, b * BB + i - 1)
                        for s in range(BPT):
                            last = nc.tensor.matmul(vbank(i)[:, s * P:(s + 1) * P], x32[:, i % 2, s * P:(s + 1) * P],
                                                    wv[:, :], start=True, stop=True)
                        last.then_inc(v_mm, 1)
                        pe.wait_ge(xl_ready, b * BB + i + 1)
                        for k in range(R):
                            q = R * i + k
                            if q >= 2:
                                pe.wait_ge(rope_mul, b * NR + q - 1)
                            for r in range(2):
                                last = matmul_split(nc, sb4[:, 2 * (q % 2) + r, :], wh[:, 2 * k + r, :],
                                                    wl[:, 2 * k + r, :], xh[:, i % 2, :], xl[:, i % 2, :])
                            last.then_inc(proj_mm, 1)
                        if i + 2 < BB:
                            turn_in(b, i + 2)
                    pe.wait_ge(rope_mul, (b + 1) * NR)
                    pe.wait_ge(v_copied, (b + 1) * BB)

                def scores(b, u, c):
                    qt, h = units[u]
                    k = first[u] + c
                    if k >= 4:
                        pe.wait_ge(exp_done, b * NC + k - 3)
                    qs = slice(qt * P, (qt + 1) * P)
                    wd = max(2, tiles_of(u, c)) * P
                    ks = slice(c * BLK, c * BLK + wd)
                    diag = c == chunks[u] - 1
                    last = matmul_split(nc, sb4[:, k % 4, 0:wd], kqh[:, 1 + h, qs], kql[:, 1 + h, qs],
                                        kqh[:, 0, ks], kql[:, 0, ks])
                    if diag:
                        d0 = (tiles_of(u, c) - 1) * P
                        last = nc.tensor.matmul(sb4[:, k % 4, d0:d0 + P], identb[:, :], mask[:, :], start=False, stop=True,
                                                skip_group_check=True)
                    last.then_inc(s_mm, 1)

                def transposes(b, u, c):
                    k = first[u] + c
                    pe.wait_ge(exp_done, b * NC + k + 1)
                    if k >= 2:
                        pe.wait_ge(pt_copied, b * NC + k - 1)
                    for a in range(tiles_of(u, c)):
                        last = nc.tensor.transpose(tb[:, k % 2, a * P:(a + 1) * P],
                                                   p[:, u % 2, c * BLK + a * P:c * BLK + (a + 1) * P], ident[:, :])
                    last.then_inc(pt_mm, 1)

                def values(b, u, c):
                    k = first[u] + c
                    pe.wait_ge(pt_copied, b * NC + k + 1)
                    if c == 0 and u > 0:
                        pe.wait_ge(o_ready, b * NU + u)
                    nt = tiles_of(u, c)
                    for a in range(nt):
                        last = nc.tensor.matmul(pv[:, 0:D], pt[:, k % 2, a * P:(a + 1) * P], v[:, c * BPT + a, :],
                                                start=(c == 0 and a == 0), stop=(c == chunks[u] - 1 and a == nt - 1))
                    last.then_inc(pv_mm, 1)

                def turn(b, r):
                    pe.wait_ge(o_ready, b * NU + 2 * r + 2)
                    if r > 0:
                        pe.wait_ge(y_copied, b * KT + r)
                    for h in range(HC):
                        last = nc.tensor.transpose(misc[:, h * P:(h + 1) * P], o[:, h, :], ident[:, :])
                    last.then_inc(ot_mm, 1)

                def out_project(b, r):
                    pe.wait_ge(ot_copied, b * KT + r + 1)
                    for h in range(HC):
                        last = nc.tensor.matmul(misc[:, 2 * P:3 * P], ot[:, h * P:(h + 1) * P], wo[:, h, :],
                                                start=(h == 0), stop=(h == HC - 1))
                    last.then_inc(out_mm, 1)

                with pe.Fori(0, BATCH) as b:
                    load(b)
                    pe.wait_ge(rope_lo, (b + 1) * NR)
                    for c in range(chunks[0]):
                        scores(b, 0, c)
                    for u in range(NU):
                        for c, ahead, _ in steps_of(u):
                            if c < chunks[u]:
                                transposes(b, u, c)
                            if ahead:
                                scores(b, u + 1, ahead[0])
                            if c == 0 and u % 2 == 0 and u > 0:
                                turn(b, u // 2 - 1)
                            if 1 <= c <= chunks[u]:
                                values(b, u, c - 1)
                            if len(ahead) > 1:
                                scores(b, u + 1, ahead[1])
                        if u % 2 == 0 and u > 0:
                            out_project(b, u // 2 - 1)
                    turn(b, KT - 1)
                    out_project(b, KT - 1)
                    pe.wait_ge(y_copied, (b + 1) * KT)


FF = 4 * D
FC = FF // P


def ffn_layer1(nc, dr, X, g, out):
    with Mem(nc, "d_") as m:
        wh = m.sb("wh", [P, NE, FF], F32R)
        wl = m.sb("wl", [P, NE, FF], F32R)
        w2 = m.sb("w2", [P, NE, FC, D])
        b1 = m.sb("b1", [P, NE, FC])
        b2 = m.sb("b2", [P, NE, D])
        wr = [m.sb(f"wr{k}", [P, P], F32R) for k in range(2)]
        rbias = m.sb("rbias", [P, NE])
        inv = m.sb("inv", [P, TILES])
        S = Stats(m, m, g)
        raw = m.sb("raw", [P, NE, FF])
        b1raw = m.sb("b1raw", [P, NE, FC])
        rr = m.sb("rr", [P, P])
        lng = m.sb("lng", [P, NE])
        lnb = m.sb("lnb", [P, NE])
        nh = m.sb("nh", [P, TILES * P], F32R)
        nl = m.sb("nl", [P, TILES * P], F32R)
        lg = m.sb("lg", [P, TILES, NE])
        gate = m.sb("gate", [P, TILES, NE])
        gsum = m.sb("gsum", [P, TILES])
        xn = m.sb("xn", [P, GRP, BPT, D])
        lt = m.sb("lt", [32, GRP, BLK])
        router = Router(m, g, lg, gate, softmax_first=False)
        a = m.sb("a", [P, 2, FC, BLK])
        xi = m.sb("xi", [P, BPT, D])
        acc = m.sb("acc", [P, BPT, D])
        F = FinishNorm(m)
        bk = m.ps("bk", 2 * GRP)
        ub, db = bk[:, 0:FC, :], bk[:, FC:FC + 2, :]
        bp = bk[:, 2 * GRP - 1, :]

        w_in = m.sem("w_in")
        c_in = m.sem("c_in")
        hi = m.sem("hi")
        lo = m.sem("lo")
        b_mm = m.sem("b_mm")
        b_done = m.sem("b_done")
        inv_step = m.sem("inv_step")
        xn_done = m.sem("xn_done")
        xt_mm = m.sem("xt_mm")
        xh_done = m.sem("xh_done")
        xl_done = m.sem("xl_done")
        l_mm = m.sem("l_mm")
        l_copied = m.sem("l_copied")
        lt_mm = m.sem("lt_mm")
        l_scaled = m.sem("l_scaled")
        l_done = m.sem("l_done")
        summed = m.sem("summed")
        ln = m.sem("ln")
        up_mm = m.sem("up_mm")
        gelu = m.sem("gelu")
        down_mm = m.sem("down_mm")
        acc_done = m.sem("acc_done")
        stored = m.sem("stored")
        NA = BPT * (1 + 2 * NE)
        group = range(GRP)
        firsts = range(0, NBLK, GRP)
        with nc.Block() as block:
            @block.sync
            def _(sp):
                for dst, src in ((raw[:, :, :], "d_w1"), (lng[:, :], "d_lng"), (lnb[:, :], "d_lnb"),
                                 (rr[:, :], "d_wr"), (b1raw[:, :, :], "d_b1")):
                    sp.dma_start(dst, dr[src]).then_inc(w_in, 16)
                for dst, src in ((w2[:, :, :, :], "d_w2"), (b2[:, :, :], "d_b2"), (rbias[:, :], "d_rbias")):
                    sp.dma_start(dst, dr[src]).then_inc(c_in, 16)
                with sp.Fori(0, NBLK) as n:
                    sp.wait_ge(F.step, n * F.N + F.N)
                    sp.dma_start(out.rearrange("(t p) d -> p t d", p=P)[:, bass.ds(n * BPT, BPT), :],
                                 X[:, bass.ds(n * BPT, BPT), :]).then_inc(stored, 16)
                sp.wait_ge(stored, 16 * NBLK)

            @block.scalar
            def _(act):
                act.wait_ge(w_in, 16 * 5)
                nc.scalar.activation(wr[0][:, :], rr[:, :], ACT.Copy).then_inc(hi, 1)
                for e in range(NE):
                    nc.scalar.activation(wh[:, e, :], raw[:, e, :], ACT.Copy, scale=lng[:, e:e + 1]).then_inc(hi, 1)
                for n in firsts:
                    for i in group:
                        act.wait_ge(xt_mm, n + i + 1)
                        nc.scalar.activation(nh[:, (n + i) * BLK:(n + i + 1) * BLK], bk[:, 2 * i, :],
                                             ACT.Copy).then_inc(xh_done, 1)
                    for i in group:
                        act.wait_ge(l_mm, n + i + 1)
                        nc.scalar.activation(lt[:, i, :], bk[0:32, 2 * i + 1, :], ACT.Copy).then_inc(l_copied, 1)
                router.scalar(nc, act)
                with act.Fori(0, NBLK) as n:
                    for e in range(NE):
                        for c in range(FC):
                            act.wait_ge(up_mm, (n * NE + e) * FC + c + 1)
                            if e >= 2 and c == 0:
                                act.wait_ge(down_mm, n * NE + e - 1)
                            nc.scalar.activation(a[:, e % 2, c, :], ub[:, c, :], ACT.Gelu,
                                                 bias=b1[:, e, c:c + 1]).then_inc(gelu, 1)

            @block.gpsimd
            def _(pool):
                stats_pool(nc, pool, S)
                with pool.Fori(0, NBLK) as n:
                    F.pool(nc, pool, n, S)

            @block.vector
            def _(dve):
                def norm(n):
                    for i in group:
                        dve.wait_ge(S.powed, (n + i) * BPT // S.CT + 1)
                        if n > 0:
                            dve.wait_ge(xt_mm, n - GRP + i + 1)
                        for s in range(BPT):
                            tile = (n + i) * BPT + s
                            nc.vector.tensor_scalar(xn[:, i, s, :], X[:, tile, :], S.mean[:, tile, 0:1],
                                                    S.rr[:, tile:tile + 1], ALU.subtract, ALU.mult).then_inc(xn_done, 1)

                def low(n):
                    for i in group:
                        cols = slice((n + i) * BLK, (n + i + 1) * BLK)
                        dve.wait_ge(xh_done, n + i + 1)
                        nc.vector.tensor_tensor(nl[:, cols], bk[:, 2 * i, :], nh[:, cols].bitcast(F32),
                                                ALU.subtract).then_inc(xl_done, 1)

                def logits(n):
                    for i in group:
                        blk = slice((n + i) * BPT, (n + i + 1) * BPT)
                        dve.wait_ge(lt_mm, n + i + 1)
                        nc.vector.tensor_tensor(lg[:, blk, :],
                                                bk[:, 2 * i, 0:BPT * 32].rearrange("p (a b) -> p a b", b=32)[:, :, 0:NE],
                                                inv[:, blk, None].to_broadcast([P, BPT, NE]),
                                                ALU.mult).then_inc(l_scaled, 1)
                    for i in group:
                        blk = slice((n + i) * BPT, (n + i + 1) * BPT)
                        dve.wait_ge(l_scaled, n + i + 1)
                        nc.vector.tensor_tensor(lg[:, blk, :], lg[:, blk, :], rbias[:, None, :].to_broadcast([P, BPT, NE]),
                                                ALU.add).then_inc(l_done, 1)

                def weights(experts):
                    for e in experts:
                        dve.wait_ge(hi, e + 2)
                        nc.vector.scalar_tensor_tensor(wl[:, e, :], raw[:, e, :], lng[:, e:e + 1],
                                                       wh[:, e, :].bitcast(F32), ALU.mult, ALU.subtract).then_inc(lo, 1)

                def router_weights():
                    dve.wait_ge(hi, 1)
                    nc.vector.tensor_tensor(wr[1][:, :], rr[:, :], wr[0][:, :].bitcast(F32), ALU.subtract).then_inc(lo, 1)

                def hidden_bias():
                    dve.wait_ge(b_mm, 1)
                    nc.vector.tensor_tensor(b1[:, :, :], bp[:, 0:NE * FC].rearrange("p (e c) -> p e c", c=FC),
                                            b1raw[:, :, :], ALU.add).then_inc(b_done, 1)

                stats_vector(nc, dve, X, S, 1e-5, router_weights)
                norm(0)
                dve.wait_ge(S.powed, S.CHUNKS)
                nc.vector.reciprocal(inv[:, :], S.rr).then_inc(inv_step, 1)
                dve.wait_ge(inv_step, 1)
                nc.vector.tensor_tensor(inv[:, :], inv[:, :], S.r, ALU.mult).then_inc(inv_step, 1)
                low(0)
                norm(GRP)
                hidden_bias()
                weights(range(NE // 2))
                dve.wait_ge(inv_step, 2)
                dve.wait_ge(c_in, 16 * 3)
                logits(0)
                low(GRP)
                weights(range(NE // 2, NE))
                logits(GRP)
                dve.wait_ge(l_done, NBLK)
                router.vector(nc, dve)
                nc.vector.tensor_reduce(gsum[:, :], gate[:, :, :], AXX, ALU.add).then_inc(summed, 1)
                dve.wait_ge(summed, 1)
                with dve.Fori(0, NBLK) as n:
                    tiles = [bass.ds(n * BPT + s, 1) for s in range(BPT)]
                    for s in range(BPT):
                        nc.vector.tensor_scalar(xi[:, s, :], X[:, tiles[s], :], S.mean[:, tiles[s], 0], S.r[:, tiles[s]],
                                                ALU.subtract, ALU.mult).then_inc(ln, 1)
                    for s in range(BPT):
                        dve.wait_ge(ln, n * BPT + s + 1)
                        nc.vector.tensor_scalar(acc[:, s, :], xi[:, s, :], gsum[:, tiles[s]], None,
                                                ALU.mult).then_inc(acc_done, 1)
                    for e in range(NE):
                        for s in range(BPT):
                            dve.wait_ge(acc_done, n * NA + e * BPT + s + 1)
                            nc.vector.scalar_tensor_tensor(acc[:, s, :], b2[:, e, :], gate[:, tiles[s], e], acc[:, s, :],
                                                           ALU.mult, ALU.add).then_inc(acc_done, 1)
                    for e in range(NE):
                        dve.wait_ge(down_mm, n * NE + e + 1)
                        for s in range(BPT):
                            dve.wait_ge(acc_done, n * NA + (NE + e) * BPT + s + 1)
                            nc.vector.scalar_tensor_tensor(acc[:, s, :], db[:, e % 2, s * P:(s + 1) * P],
                                                           gate[:, tiles[s], e], acc[:, s, :], ALU.mult,
                                                           ALU.add).then_inc(acc_done, 1)
                    dve.wait_ge(acc_done, n * NA + NA)
                    F.vector(nc, dve, n, acc, X, S)

            @block.tensor
            def _(pe):
                ident = g["ident"]
                for n in firsts:
                    for i in group:
                        if n > 0:
                            pe.wait_ge(l_scaled, n - GRP + i + 1)
                        for s in range(BPT):
                            pe.wait_ge(xn_done, (n + i) * BPT + s + 1)
                            last = nc.tensor.transpose(bk[:, 2 * i, s * P:(s + 1) * P], xn[:, i, s, :], ident[:, :])
                        last.then_inc(xt_mm, 1)
                    if n == 0:
                        pe.wait_ge(w_in, 16 * 5)
                        for e in range(NE):
                            for c in range(FC):
                                last = nc.tensor.matmul(bp[:, e * FC + c:e * FC + c + 1], raw[:, e, c * P:(c + 1) * P],
                                                        lnb[:, e:e + 1], start=True, stop=True)
                        last.then_inc(b_mm, 1)
                        pe.wait_ge(lo, 1)
                        pe.wait_ge(b_done, 1)
                    for i in group:
                        cols = slice((n + i) * BLK, (n + i + 1) * BLK)
                        pe.wait_ge(xh_done, n + i + 1)
                        pe.wait_ge(xl_done, n + i + 1)
                        matmul_split(nc, bk[:, 2 * i + 1, :], wr[0][:, :], wr[1][:, :], nh[:, cols],
                                     nl[:, cols]).then_inc(l_mm, 1)
                    for i in group:
                        wait_alone(pe, l_copied, n + i + 1, g["passed_pe"])
                        for s in range(BPT):
                            last = nc.tensor.transpose(bk[:, 2 * i, s * 32:(s + 1) * 32], lt[:, i, s * P:(s + 1) * P],
                                                       ident[0:32, 0:32])
                        last.then_inc(lt_mm, 1)
                pe.wait_ge(l_scaled, NBLK)
                pe.wait_ge(lo, 1 + NE)
                pe.wait_ge(c_in, 16 * 3)
                with pe.Fori(0, NBLK) as n:
                    cols = bass.ds(n * BLK, BLK)

                    def up(e, c):
                        if e > 0:
                            pe.wait_ge(gelu, (n * NE + e - 1) * FC + c + 1)
                        cs = slice(c * P, (c + 1) * P)
                        matmul_split(nc, ub[:, c, :], wh[:, e, cs], wl[:, e, cs], nh[:, cols], nl[:, cols]).then_inc(up_mm, 1)

                    def down(e, s):
                        if s == 0:
                            pe.wait_ge(gelu, (n * NE + e + 1) * FC)
                            if e >= 2:
                                pe.wait_ge(acc_done, n * NA + (NE + e) * BPT)
                        for c in range(FC):
                            last = nc.tensor.matmul(db[:, e % 2, s * P:(s + 1) * P], a[:, e % 2, c, s * P:(s + 1) * P],
                                                    w2[:, e, c, :], start=(c == 0), stop=(c == FC - 1))
                        if s == BPT - 1:
                            last.then_inc(down_mm, 1)

                    for c in range(FC):
                        up(0, c)
                    for e in range(NE):
                        for s in range(BPT):
                            if e + 1 < NE:
                                up(e + 1, s)
                            down(e, s)
                    pe.wait_ge(gelu, (n + 1) * NE * FC)
                    pe.wait_ge(acc_done, n * NA + NA)


def rope_tables(n, d, scale):
    pos = np.arange(0, d, 2, dtype=np.float32)
    if scale == 1:
        freq = (np.float32(1.0) / np.float32(10000.0) ** (pos / np.float32(d))).astype(np.float32)
    else:
        freq = (np.float32(10000.0) ** (np.float32(-2.0) * pos / np.float32(d))).astype(np.float32)
    ang = np.arange(n, dtype=np.float32)[None, :] * freq[:, None]
    return (np.repeat(np.cos(ang), 2, axis=0).astype(np.float32),
            np.repeat(np.sin(ang), 2, axis=0).astype(np.float32))


def host_layout(a):
    f = np.float32
    z = {}
    z["ident"] = np.eye(P, dtype=f)
    z["identb"] = np.eye(P, dtype=f).astype(mybir.dt.np(BF16))
    cos, sin = rope_tables(SEQ, DH0, 1)
    z["cs0"] = np.tile(np.stack([t.reshape(DH0, SEQ // SUB, SUB) for t in (cos, sin)], axis=2), (2, 1, 1, 1))
    row = np.arange(P)[:, None] % SEG
    col = np.arange(KEYS0)[None, :]
    masked = np.where((col < PM) | (col - PM <= row), 0.0, -1e30)
    z["mask0"] = np.tile(masked, (1, 6)).astype(mybir.dt.np(BF16))
    z["x"] = a["L0_attn_seq"].reshape(-1, D)
    z["norm_w"] = a["L0_attn_norm_w"].reshape(D, 1)
    z["w_qkv"] = a["L0_attn_w_qkv"]
    z["w_out"] = a["L0_attn_w_out"].reshape(PAIRS, P, D).transpose(1, 0, 2)
    z["b_out"] = np.broadcast_to(a["L0_attn_b_out"], (P, D))
    pk, pv = a["L0_attn_pm_k"], a["L0_attn_pm_v"]
    pmk = np.zeros((P, PAIRS, 2 * KEYS0), f)
    pmv = np.zeros((P, PAIRS, P), f)
    for h in range(H0):
        rows = slice((h % 2) * DH0, (h % 2 + 1) * DH0)
        pmk[rows, h // 2, (h % 2) * KEYS0:(h % 2) * KEYS0 + PM] = pk[h].T
        pmv[rows, h // 2, (h % 8) * PM:(h % 8 + 1) * PM] = pv[h].T
    z["pmkT"], z["pmvT"] = pmk, pmv
    wq, wkc, wvc = a["L0_ffn_Wq"].T, a["L0_ffn_Wkc"].T, a["L0_ffn_Wvc"].T
    z["b_wq"] = np.concatenate([wq[:, h * DK:(h + 1) * DK] for h in range(HB) for _ in range(3)], axis=1)
    z["b_wkv"] = np.concatenate([wkc, wkc, wkc, wvc], axis=1)
    z["b_wr"] = np.pad(a["L0_ffn_Wr"].T, ((0, 0), (0, P - NE)))
    z["b_w13"] = np.concatenate([
        np.concatenate([a["L0_ffn_eW" + k].transpose(2, 0, 1), a["L0_ffn_sW" + k].T[:, None, :]], axis=1)
        .reshape(D, -1) for k in "13"], axis=1)
    z["b_g12"] = np.stack([a["L0_ffn_g1"], a["L0_ffn_g2"]], axis=1)
    z["b_w2"] = np.concatenate([a["L0_ffn_eW2"].transpose(2, 0, 1), a["L0_ffn_sW2"].T[:, None, :]], axis=1)
    z["b_wo"] = a["L0_ffn_Wo"].T
    z["b_ebias"] = np.broadcast_to(a["L0_ffn_expert_bias"], (P, NE))
    z["iota"] = np.broadcast_to(np.arange(NE, dtype=f), (P, NE))
    cos, sin = rope_tables(SEQ, D, 2)
    z["cs1"] = np.stack([t.reshape(D, BB, BLK) for t in (cos, sin)], axis=2)
    z["mask1"] = np.where(np.arange(P)[None, :] <= np.arange(P)[:, None], 0.0, -1e30).astype(mybir.dt.np(BF16))
    z["c_wkq"] = np.stack([a["L1_attn_Wk"].T] + [a["L1_attn_Wq"][h].T for h in range(HC)], axis=1)
    z["c_wv"] = a["L1_attn_Wv"].T
    z["c_wo"] = a["L1_attn_Wo"].T.reshape(HC, D, D).transpose(1, 0, 2)
    z["d_w1"] = a["L1_ffn_W1"].transpose(1, 0, 2)
    z["d_lng"], z["d_lnb"] = a["L1_ffn_ln_g"].T, a["L1_ffn_ln_b"].T
    z["d_wr"] = np.pad(a["L1_ffn_router_W"], ((0, 0), (0, P - NE)))
    z["d_b1"] = a["L1_ffn_b1"].reshape(NE, FC, P).transpose(2, 0, 1)
    z["d_w2"] = a["L1_ffn_W2"].reshape(NE, FC, P, D).transpose(2, 0, 1, 3)
    z["d_b2"] = np.broadcast_to(a["L1_ffn_b2"], (P, NE, D))
    z["d_rbias"] = np.broadcast_to(a["L1_ffn_router_b"], (P, NE))
    return {k: np.ascontiguousarray(v) for k, v in z.items()}


def build_program(nc, dr, out):
    with Mem(nc, "g_") as gm:
        X = gm.sb("X", [P, TILES, D])
        g = {"ident": gm.sb("ident", [P, P]), "identb": gm.sb("identb", [P, P], BF16), "iota": gm.sb("iota", [P, NE]),
             "passed_dve": gm.sem("passed_dve"), "passed_pe": gm.sem("passed_pe")}
        local_attention(nc, dr, X, g)
        ffn_layer0(nc, dr, X, g)
        causal_attention(nc, dr, X, g)
        ffn_layer1(nc, dr, X, g, out)


def kernel(**inputs):
    import concourse.bacc as bacc
    from concourse.bass_utils import run_bass_kernel_spmd

    arrays = host_layout({k: np.asarray(v) for k, v in inputs.items()})
    nc = bacc.Bacc("TRN2", target_bir_lowering=False, num_devices=1)
    dr = {k: nc.dram_tensor(k, v.shape, mybir.dt.from_np(v.dtype), kind="ExternalInput").ap()
          for k, v in arrays.items()}
    out = nc.dram_tensor("out", (BATCH * SEQ, D), F32, kind="ExternalOutput").ap()
    build_program(nc, dr, out)
    r = run_bass_kernel_spmd(nc, [arrays], core_ids=[0])
    return r.results[0]["out"].reshape(BATCH, SEQ, D)
```
